# Optimizing a Trainium2 kernel written in Bass

```python
import numpy as np
import jax
import jax.numpy as jnp

def _softmax(x, axis=-1):
    return jax.nn.softmax(x, axis=axis)

def _gelu(x):
    return jax.nn.gelu(x, approximate=True)

def _silu(x):
    return jax.nn.silu(x)

def _sigmoid(x):
    return jax.nn.sigmoid(x)

def _layernorm(x, axis=-1, eps=1e-05):
    m = jnp.mean(x, axis=axis, keepdims=True)
    v = jnp.var(x, axis=axis, keepdims=True)
    return (x - m) / jnp.sqrt(v + eps)

def _scatter_add(tgt, idx, src, axis=0):
    return tgt.at[idx].add(src)

def _segment_sum(src, seg, n):
    return jax.ops.segment_sum(src, seg, n)
kernel_name = 'mk_sandwich_d2_jaxref_r8_96af5b'

def setup_inputs(seed: int=0):
    np.random.seed(seed)
    _w = jnp.asarray

    def _L0_attn_setup():
        import jax, jax.numpy as jnp
        import numpy as np
        from jax import lax
        H = 64
        P = 64
        N = 128
        G = 8
        K = 4
        D_MODEL = 512
        I = H * P
        GN = G * N
        CONV_DIM = I + 2 * GN
        PROJ = I + CONV_DIM + H
        EPS = 1e-05
        GROUP_SIZE = I // G

        def _reference_tuple_inner(hidden_states, in_proj_w, conv_weight, conv_bias, dt_bias, A_log, D, norm_weight, out_proj_w):
            B, L, _ = hidden_states.shape
            proj = jnp.einsum('bld,pd->blp', hidden_states, in_proj_w)
            gate = proj[..., :I]
            hbc = proj[..., I:I + CONV_DIM]
            dt = proj[..., -H:]
            pad = jnp.pad(hbc, ((0, 0), (K - 1, 0), (0, 0)))
            conv = conv_bias
            for k in range(K):
                conv = conv + pad[:, k:k + L, :] * conv_weight[:, k]
            xBC = jax.nn.silu(conv)
            x = xBC[..., :I].reshape(B, L, H, P)
            Bm = xBC[..., I:I + GN].reshape(B, L, G, N)
            Cm = xBC[..., I + GN:].reshape(B, L, G, N)
            hpg = H // G
            B_h = jnp.repeat(Bm, hpg, axis=2)
            C_h = jnp.repeat(Cm, hpg, axis=2)
            dt_p = jax.nn.softplus(dt + dt_bias)
            A = -jnp.exp(A_log)
            dA = jnp.exp(dt_p * A)
            dtx = dt_p[..., None] * x

            def step(state, inp):
                dA_t, dtx_t, B_t, C_t = inp
                state = state * dA_t[..., None, None] + dtx_t[..., None] * B_t[:, :, None, :]
                y_t = jnp.einsum('bhpn,bhn->bhp', state, C_t)
                return (state, y_t)
            xs = (jnp.moveaxis(dA, 1, 0), jnp.moveaxis(dtx, 1, 0), jnp.moveaxis(B_h, 1, 0), jnp.moveaxis(C_h, 1, 0))
            state0 = jnp.zeros((B, H, P, N), jnp.float32)
            final_state, ys = lax.scan(step, state0, xs)
            y = jnp.moveaxis(ys, 0, 1) + x * D[None, None, :, None]
            y = y.reshape(B, L, I)
            yg = y.reshape(B, L, G, GROUP_SIZE)
            var = jnp.mean(yg * yg, axis=-1, keepdims=True)
            yn = (yg * lax.rsqrt(var + EPS)).reshape(B, L, I) * norm_weight
            yn = yn * jax.nn.silu(gate)
            out = jnp.einsum('bli,di->bld', yn, out_proj_w)
            conv_state_new = jnp.moveaxis(hbc[:, L - (K - 1):, :], 1, 2)
            return (out, conv_state_new, final_state)
        key = jax.random.key(seed)
        ks = jax.random.split(key, 6)
        B, L = (2, 256)
        s = 0.02
        return {'hidden_states': jax.random.normal(ks[0], (B, L, D_MODEL), jnp.float32), 'in_proj_w': jax.random.normal(ks[1], (PROJ, D_MODEL), jnp.float32) * s, 'conv_weight': jax.random.normal(ks[2], (CONV_DIM, K), jnp.float32) * s, 'conv_bias': jnp.zeros((CONV_DIM,), jnp.float32), 'dt_bias': jnp.ones((H,), jnp.float32), 'A_log': jnp.log(jnp.arange(1, H + 1, dtype=jnp.float32)), 'D': jnp.ones((H,), jnp.float32), 'norm_weight': jnp.ones((I,), jnp.float32), 'out_proj_w': jax.random.normal(ks[3], (D_MODEL, I), jnp.float32) * s}
    _L0_attn_in = _L0_attn_setup()

    def _L0_ffn_setup():
        import jax, jax.numpy as jnp
        import numpy as np
        H, FF = (512, 1792)
        B, S = (4, 256)
        key = jax.random.key(seed)
        ks = jax.random.split(key, 7)
        x = jax.random.normal(ks[0], (B, S, H), dtype=jnp.float32)
        gate_t = jax.random.randint(ks[1], (FF, H), -1, 2, dtype=jnp.int32)
        up_t = jax.random.randint(ks[2], (FF, H), -1, 2, dtype=jnp.int32)
        down_t = jax.random.randint(ks[3], (H, FF), -1, 2, dtype=jnp.int32)
        gate_s = jax.random.uniform(ks[4], (FF,), jnp.float32, 0.01, 0.1)
        up_s = jax.random.uniform(ks[5], (FF,), jnp.float32, 0.01, 0.1)
        down_s = jax.random.uniform(ks[6], (H,), jnp.float32, 0.01, 0.1)
        return {'x': x, 'gate_t': gate_t, 'up_t': up_t, 'down_t': down_t, 'gate_s': gate_s, 'up_s': up_s, 'down_s': down_s}
    _L0_ffn_in = _L0_ffn_setup()

    def _L1_attn_setup():
        import jax, jax.numpy as jnp
        import numpy as np
        import math
        B, L, D, H = (32, 64, 512, 32)
        HD = D // H
        key = jax.random.key(seed)
        ks = jax.random.split(key, 9)
        s = 1.0 / math.sqrt(D)
        return {'x': jax.random.normal(ks[0], (B, L, D), jnp.float32), 'Wq': jax.random.normal(ks[1], (D, D), jnp.float32) * s, 'bq': jax.random.normal(ks[2], (D,), jnp.float32) * s, 'Wk': jax.random.normal(ks[3], (D, D), jnp.float32) * s, 'bk': jax.random.normal(ks[4], (D,), jnp.float32) * s, 'Wv': jax.random.normal(ks[5], (D, D), jnp.float32) * s, 'bv': jax.random.normal(ks[6], (D,), jnp.float32) * s, 'Wo': jax.random.normal(ks[7], (D, D), jnp.float32) * s, 'bo': jax.random.normal(ks[8], (D,), jnp.float32) * s}
    _L1_attn_in = _L1_attn_setup()

    def _L1_ffn_setup():
        import jax, jax.numpy as jnp
        import numpy as np
        TOP_K = 2
        key = jax.random.key(seed)
        k1, k2, k3 = jax.random.split(key, 3)
        B, S, H, O, E = (1024, 1, 512, 512, 8)
        x = jax.random.normal(k1, (B, S, H), dtype=jnp.float32)
        gate_w = jax.random.normal(k2, (H, E), dtype=jnp.float32) * 0.02
        expert_w = jax.random.normal(k3, (E, H, O), dtype=jnp.float32) * 0.02
        return {'x': x, 'gate_w': gate_w, 'expert_w': expert_w}
    _L1_ffn_in = _L1_ffn_setup()
    _d = {'L0_attn_hidden_states': _L0_attn_in['hidden_states'], 'L0_attn_in_proj_w': _L0_attn_in['in_proj_w'], 'L0_attn_conv_weight': _L0_attn_in['conv_weight'], 'L0_attn_conv_bias': _L0_attn_in['conv_bias'], 'L0_attn_dt_bias': _L0_attn_in['dt_bias'], 'L0_attn_A_log': _L0_attn_in['A_log'], 'L0_attn_D': _L0_attn_in['D'], 'L0_attn_norm_weight': _L0_attn_in['norm_weight'], 'L0_attn_out_proj_w': _L0_attn_in['out_proj_w'], 'L0_ffn_gate_t': _L0_ffn_in['gate_t'], 'L0_ffn_up_t': _L0_ffn_in['up_t'], 'L0_ffn_down_t': _L0_ffn_in['down_t'], 'L0_ffn_gate_s': _L0_ffn_in['gate_s'], 'L0_ffn_up_s': _L0_ffn_in['up_s'], 'L0_ffn_down_s': _L0_ffn_in['down_s'], 'L1_attn_Wq': _L1_attn_in['Wq'], 'L1_attn_bq': _L1_attn_in['bq'], 'L1_attn_Wk': _L1_attn_in['Wk'], 'L1_attn_bk': _L1_attn_in['bk'], 'L1_attn_Wv': _L1_attn_in['Wv'], 'L1_attn_bv': _L1_attn_in['bv'], 'L1_attn_Wo': _L1_attn_in['Wo'], 'L1_attn_bo': _L1_attn_in['bo'], 'L1_ffn_gate_w': _L1_ffn_in['gate_w'], 'L1_ffn_expert_w': _L1_ffn_in['expert_w']}
    _x0 = _d['L0_attn_hidden_states']
    _d['L0_attn_hidden_states'] = jax.random.normal(jax.random.fold_in(jax.random.key(seed), 1), (2, 512, 512), dtype=_x0.dtype)
    del _x0
    return _d

def reference(L0_attn_hidden_states, L0_attn_in_proj_w, L0_attn_conv_weight, L0_attn_conv_bias, L0_attn_dt_bias, L0_attn_A_log, L0_attn_D, L0_attn_norm_weight, L0_attn_out_proj_w, L0_ffn_gate_t, L0_ffn_up_t, L0_ffn_down_t, L0_ffn_gate_s, L0_ffn_up_s, L0_ffn_down_s, L1_attn_Wq, L1_attn_bq, L1_attn_Wk, L1_attn_bk, L1_attn_Wv, L1_attn_bv, L1_attn_Wo, L1_attn_bo, L1_ffn_gate_w, L1_ffn_expert_w):

    def _L0_attn_ref(hidden_states, in_proj_w, conv_weight, conv_bias, dt_bias, A_log, D, norm_weight, out_proj_w):
        import jax, jax.numpy as jnp
        import numpy as np
        from jax import lax
        H = 64
        P = 64
        N = 128
        G = 8
        K = 4
        D_MODEL = 512
        I = H * P
        GN = G * N
        CONV_DIM = I + 2 * GN
        PROJ = I + CONV_DIM + H
        EPS = 1e-05
        GROUP_SIZE = I // G

        def _reference_tuple_inner(hidden_states, in_proj_w, conv_weight, conv_bias, dt_bias, A_log, D, norm_weight, out_proj_w):
            B, L, _ = hidden_states.shape
            proj = jnp.einsum('bld,pd->blp', hidden_states, in_proj_w)
            gate = proj[..., :I]
            hbc = proj[..., I:I + CONV_DIM]
            dt = proj[..., -H:]
            pad = jnp.pad(hbc, ((0, 0), (K - 1, 0), (0, 0)))
            conv = conv_bias
            for k in range(K):
                conv = conv + pad[:, k:k + L, :] * conv_weight[:, k]
            xBC = jax.nn.silu(conv)
            x = xBC[..., :I].reshape(B, L, H, P)
            Bm = xBC[..., I:I + GN].reshape(B, L, G, N)
            Cm = xBC[..., I + GN:].reshape(B, L, G, N)
            hpg = H // G
            B_h = jnp.repeat(Bm, hpg, axis=2)
            C_h = jnp.repeat(Cm, hpg, axis=2)
            dt_p = jax.nn.softplus(dt + dt_bias)
            A = -jnp.exp(A_log)
            dA = jnp.exp(dt_p * A)
            dtx = dt_p[..., None] * x

            def step(state, inp):
                dA_t, dtx_t, B_t, C_t = inp
                state = state * dA_t[..., None, None] + dtx_t[..., None] * B_t[:, :, None, :]
                y_t = jnp.einsum('bhpn,bhn->bhp', state, C_t)
                return (state, y_t)
            xs = (jnp.moveaxis(dA, 1, 0), jnp.moveaxis(dtx, 1, 0), jnp.moveaxis(B_h, 1, 0), jnp.moveaxis(C_h, 1, 0))
            state0 = jnp.zeros((B, H, P, N), jnp.float32)
            final_state, ys = lax.scan(step, state0, xs)
            y = jnp.moveaxis(ys, 0, 1) + x * D[None, None, :, None]
            y = y.reshape(B, L, I)
            yg = y.reshape(B, L, G, GROUP_SIZE)
            var = jnp.mean(yg * yg, axis=-1, keepdims=True)
            yn = (yg * lax.rsqrt(var + EPS)).reshape(B, L, I) * norm_weight
            yn = yn * jax.nn.silu(gate)
            out = jnp.einsum('bli,di->bld', yn, out_proj_w)
            conv_state_new = jnp.moveaxis(hbc[:, L - (K - 1):, :], 1, 2)
            return (out, conv_state_new, final_state)
        return _reference_tuple_inner(hidden_states, in_proj_w, conv_weight, conv_bias, dt_bias, A_log, D, norm_weight, out_proj_w)[0]

    def _L0_ffn_ref(x, gate_t, up_t, down_t, gate_s, up_s, down_s):
        import jax, jax.numpy as jnp
        import numpy as np
        H, FF = (512, 1792)
        B, S = (4, 256)
        Bb, Ss, Hh = x.shape
        x_flat = x.reshape(Bb * Ss, Hh)
        gate_w = gate_t.astype(jnp.float32) * gate_s[:, None]
        up_w = up_t.astype(jnp.float32) * up_s[:, None]
        down_w = down_t.astype(jnp.float32) * down_s[:, None]
        gate_out = x_flat @ gate_w.T
        up_out = x_flat @ up_w.T
        hidden = jax.nn.silu(gate_out) * up_out
        out_flat = hidden @ down_w.T
        return out_flat.reshape(Bb, Ss, -1)

    def _L1_attn_ref(x, Wq, bq, Wk, bk, Wv, bv, Wo, bo):
        import jax, jax.numpy as jnp
        import numpy as np
        import math
        B, L, D, H = (32, 64, 512, 32)
        HD = D // H
        b, l, d = x.shape
        h, hd = (H, HD)
        q = (x @ Wq.T + bq).reshape(b, l, h, hd).transpose(0, 2, 1, 3)
        k = (x @ Wk.T + bk).reshape(b, l, h, hd).transpose(0, 2, 1, 3)
        v = (x @ Wv.T + bv).reshape(b, l, h, hd).transpose(0, 2, 1, 3)
        scores = jnp.einsum('bhqd,bhkd->bhqk', q, k) / math.sqrt(hd)
        causal = jnp.tril(jnp.ones((l, l), bool))
        scores = jnp.where(causal, scores, -jnp.inf)
        att = jax.nn.softmax(scores, axis=-1)
        out = jnp.einsum('bhqk,bhkd->bhqd', att, v)
        out = out.transpose(0, 2, 1, 3).reshape(b, l, d)
        return out @ Wo.T + bo

    def _L1_ffn_ref(x, gate_w, expert_w):
        import jax, jax.numpy as jnp
        import numpy as np
        TOP_K = 2
        E = gate_w.shape[-1]
        logits = jnp.einsum('bsh,he->bse', x, gate_w)
        topv, topi = jax.lax.top_k(logits, TOP_K)
        w = jax.nn.softmax(topv, axis=-1)
        onehot = jax.nn.one_hot(topi, E, dtype=x.dtype)
        w_e = jnp.einsum('bske,bsk->bse', onehot, w)
        out = jnp.einsum('bsh,eho,bse->bso', x, expert_w, w_e)
        return out
    x = L0_attn_hidden_states
    x = x + _layernorm(_L0_attn_ref(_layernorm(x, axis=-1), L0_attn_in_proj_w, L0_attn_conv_weight, L0_attn_conv_bias, L0_attn_dt_bias, L0_attn_A_log, L0_attn_D, L0_attn_norm_weight, L0_attn_out_proj_w), axis=-1)
    x = x + _layernorm(_L0_ffn_ref(_layernorm(x, axis=-1), L0_ffn_gate_t, L0_ffn_up_t, L0_ffn_down_t, L0_ffn_gate_s, L0_ffn_up_s, L0_ffn_down_s), axis=-1)
    x = x + _layernorm(_L1_attn_ref(_layernorm(x, axis=-1), L1_attn_Wq, L1_attn_bq, L1_attn_Wk, L1_attn_bk, L1_attn_Wv, L1_attn_bv, L1_attn_Wo, L1_attn_bo), axis=-1)
    x = x + _layernorm(_L1_ffn_ref(_layernorm(x, axis=-1), L1_ffn_gate_w, L1_ffn_expert_w), axis=-1)
    return x

_drawn_inputs = setup_inputs


def setup_inputs(seed=0):
    import zlib

    import numpy as np

    out = dict(_drawn_inputs(seed))
    spreads = {'L0_attn_conv_bias': (0.0, 0.1),
     'L0_attn_dt_bias': (1.0, 0.6),
     'L0_attn_D': (1.0, 0.2),
     'L0_attn_norm_weight': (1.0, 0.2)}
    factors = {'L0_attn_A_log': 2.729, 'L1_attn_bk': 8.0}
    for name, (base, spread) in spreads.items():
        noise = np.random.default_rng([zlib.crc32(name.encode()), seed]).standard_normal(out[name].shape)
        drawn = base * np.exp(spread * noise) if base else spread * noise
        out[name] = jnp.asarray(drawn.astype(out[name].dtype))
    for name, factor in factors.items():
        out[name] = (out[name] * factor).astype(out[name].dtype)
    return out
```

```python
import numpy as np
import concourse.bass as bass
from concourse import mybir
from concourse.alu_op_type import AluOpType as ALU
from contextlib import ExitStack

F32 = mybir.dt.float32
F32R = mybir.dt.float32r
I32 = mybir.dt.int32
U32 = mybir.dt.uint32
ACT = mybir.ActivationFunctionType
AX = mybir.AxisListType.X

P = 128
DM = 512
KT = DM // P
NB, L = 2, 512
NT = NB * L // P
CH = L // P
EPS = 1e-5
H, HP, NS, G, KC = 64, 64, 128, 8, 4
HG = H // G
GI = HG * HP
CT = GI // P + 2
JB, JC = CT - 2, CT - 1
FF = 1792
FT = FF // P
FP = FT // 2
AH, HD = 32, 16
AT = DM // P
HT = P // HD
NE = 8
STAGES = 4


class Count:

    def __init__(self, sem):
        self.sem, self.n = sem, 0

    def inc(self, instruction):
        self.n += 1
        instruction.then_inc(self.sem, 1)
        return self.n


def program(nc, hidden, w_conv, w_gate, w_dt, conv_w, conv_b, dt_bias, A_log, Dskip, norm_w, w_out,
            ff_gu, ff_dn, gate_s, up_s, down_s, wq, wk, bqk, wv, bv, wo, bo, gate_w, expert_w, out):
    ctx = ExitStack()
    with ctx:

        def sb(name, shape, dt=F32, stack=ctx):
            return stack.enter_context(nc.sbuf_tensor(name, shape, dt))

        def sem(name):
            return ctx.enter_context(nc.semaphore(name))

        banks = ctx.enter_context(nc.psum_tensor("banks", [P, 8, 512], F32))

        def bk(i):
            return banks[:, i, :]

        x = sb("x", [P, NT, DM])
        acc = sb("acc", [P, NT, DM])
        xT = sb("xT", [P, KT, NB * L])
        ident = sb("ident", [P, P])
        ones = sb("ones", [P, P])
        upto = sb("upto", [P, P])
        after = sb("after", [P, P])
        mhalf = sb("mhalf", [P, NT])
        epsc = sb("epsc", [P, 1])
        stats = sb("stats", [P, NT, 6])
        mv = sb("mv", [P, NT, 2])
        ve = sb("ve", [P, NT])
        rs = sb("rs", [P, NT])
        xn = sb("xn", [P, 2, DM])

        A = ExitStack()

        def sa(name, shape, dt=F32):
            return sb(name, shape, dt, A)

        wc = sa("wc", [P, KT, CT * P])
        wg = sa("wg", [P, KT, GI])
        wor = sa("wor", [P, KT, DM])
        wos = sa("wos", [P, KT, DM])
        wdt = sa("wdt", [P, KT, H])
        par = sa("par", [P, G, CT * KC + CT + KT])
        parg = sa("parg", [P, CT * KC + CT + KT])
        bcast = sa("bcast", [P, 2, H])
        per = sa("per", [P, 5 * NT + 1, H])
        cur = sa("cur", [P, 5 * NT + 1, HG])
        z = sa("z", [P, 4, NT * H])
        tap = sa("tap", [P, 2, L])
        th = sa("th", [P, 2, L])
        xbc = sa("xbc", [P, CT, NB * L])
        xtok = sa("xtok", [P, 2, GI])
        btok = sa("btok", [P, 2, NS])
        gmask = sa("gmask", [P, P])
        am = sa("am", [P, 2, HG, P])
        em = sa("em", [P, 2, HG, P])
        dtx = sa("dtx", [P, 2, GI])
        xdec = sa("xdec", [P, 2, GI])
        xd = sa("xd", [P, 2, GI])
        state = sa("state", [P, GI])
        sdec = sa("sdec", [P, GI])
        yoff = sa("yoff", [P, GI])
        y = sa("y", [P, 2, GI])
        ysq = sa("ysq", [P, GI])
        ss = sa("ss", [P, 2])
        ssv = sa("ssv", [P, 2])
        rg = sa("rg", [P, 2])
        tg = sa("tg", [P, 2, GI])
        sg = sa("sg", [P, 2, GI])
        yn = sa("yn", [P, 2, GI])
        ynT = sa("ynT", [P, 2, GI])
        A.close()

        B = ExitStack()

        def sf(name, shape, dt=F32):
            return sb(name, shape, dt, B)

        gur = sf("gur", [P, KT, 2, 2, P], I32)
        gu = sf("gu", [P, KT, 2, 2, P])
        dnr = sf("dnr", [P, 2, DM], I32)
        dn = sf("dn", [P, 2, DM])
        gus = sf("gus", [P, 2, FT])
        fsc = sf("fsc", [P, 2, FT])
        fscg = sf("fscg", [P, 2, 2])
        dsb = sf("dsb", [P, DM])
        fth = sf("fth", [P, 2, L])
        fh = sf("fh", [P, 2, L])
        hid = sf("hid", [P, 2, NB * L])
        B.close()

        C = ExitStack()

        def sc(name, shape, dt=F32):
            return sb(name, shape, dt, C)

        awv = sc("awv", [P, KT, DM])
        awo = sc("awo", [P, KT, DM])
        awq = sc("awq", [P, KT, P])
        awk = sc("awk", [P, KT, P])
        abqk = sc("abqk", [P, 2, AT])
        abg = sc("abg", [P, 2])
        abv = sc("abv", [P, DM])
        abo = sc("abo", [P, DM])
        v = sc("v", [P, NT, DM])
        fold = sc("fold", [P, 2, HD])
        sel = sc("sel", [P, 4, P], F32R)
        identr = sc("identr", [P, P], F32R)
        future = sc("future", [P, P], F32R)
        futf = sc("futf", [P, P])
        qf = sc("qf", [P, 2, L])
        qh = sc("qh", [P, 2, L], F32R)
        ql = sc("ql", [P, 2, L], F32R)
        qs = sc("qs", [P, 4, L], F32R)
        ks = sc("ks", [P, 4, L], F32R)
        nmax = sc("nmax", [P, 2, 2])
        prob = sc("prob", [P, 2, 2, L])
        psum = sc("psum", [P, 2, HT])
        prec = sc("prec", [P, HT])
        pT = sc("pT", [P, 2, 2, L])
        att = sc("att", [P, NT, DM])
        attT = sc("attT", [P, 2, DM])
        C.close()

        D = ExitStack()

        def sd(name, shape, dt=F32):
            return sb(name, shape, dt, D)

        ew = sd("ew", [P, 2, KT, DM])
        rw = sd("rw", [P, KT, NE])
        lg = sd("lg", [P, NT, NE])
        top = sd("top", [P, NT, NE])
        topi = sd("topi", [P, NT, NE], U32)
        topf = sd("topf", [P, NT, NE])
        which = sd("which", [P, NE])
        rt = sd("rt", [P, 4, NT])
        oh = sd("oh", [P, 2, NT, NE])
        we = sd("we", [P, NT, NE])
        D.close()

        x_in = sem("x_in")
        small_in = sem("small_in")
        wconv_in, wgate_in, wout_in = sem("wconv_in"), sem("wgate_in"), sem("wout_in")
        consts = sem("consts")
        nsem = {}
        for q in range(5):
            for w in ("dve", "var", "rstd", "xn", "tr", "ev"):
                nsem[q, w] = sem(f"n{q}_{w}")
        dt_ps, dt_dve, dt_act, dt_cum = sem("dt_ps"), sem("dt_dve"), sem("dt_act"), sem("dt_cum")
        par_ready, cur_ready = sem("par_ready"), sem("cur_ready")
        acc_clear = sem("acc_clear")
        wout_scaled = sem("wout_scaled")
        h_ready, tap0, taps, tanh_ready, xbc_ready = (sem(s) for s in ("h_ready", "tap0", "taps", "tanh_ready", "xbc_ready"))
        x_tr, tp_out, gb_ready, gb_used, d_ready, e_ready = (sem(s) for s in ("x_tr", "tp_out", "gb_ready", "gb_used", "d_ready", "e_ready"))
        am_ready, xd_ready, xdec_ready, dtx_ready, sdec_ready = (sem(s) for s in ("am_ready", "xd_ready", "xdec_ready", "dtx_ready", "sdec_ready"))
        m_ready, yo_ready, yo_used, yi_ready, y_part, y_ready = (sem(s) for s in ("m_ready", "yo_ready", "yo_used", "yi_ready", "y_part", "y_ready"))
        st_ready, state_ready, ss_ready, ssv_ready, rg_ready = (sem(s) for s in ("st_ready", "state_ready", "ss_ready", "ssv_ready", "rg_ready"))
        gate_ready, tg_ready, gate_used, yn_ready, yn_tr, o_ready, out_added = (sem(s) for s in ("gate_ready", "tg_ready", "gate_used", "yn_ready", "yn_tr", "o_ready", "out_added"))

        gu_in, dn_in, gu_cast, dn_cast, f_small, f_dve, f_clear, fsc_ready = (sem(s) for s in ("gu_in", "dn_in", "gu_cast", "dn_cast", "f_small", "f_dve", "f_clear", "fsc_ready"))
        gate_ps, up_ps, f_tanh, f_part, hid_ready, down_ps, down_added = (sem(s) for s in ("gate_ps", "up_ps", "f_tanh", "f_part", "hid_ready", "down_ps", "down_added"))

        a_small, aw_in, awv_in, v_ps, v_ready, sel_ready = (sem(s) for s in ("a_small", "aw_in", "awv_in", "v_ps", "v_ready", "sel_ready"))
        qk_ps, qk_f, qk_h, qk_l, st_ps, st_out = (sem(s) for s in ("qk_ps", "qk_f", "qk_h", "qk_l", "st_ps", "st_out"))
        st_out2, qb_scaled, bias_ready = sem("st_out2"), sem("qb_scaled"), sem("bias_ready")
        s_ready, max_ready, exp_ready, pt_ps, pt_ready, pv_ps, prec_ready, att_ready = (sem(s) for s in ("s_ready", "max_ready", "exp_ready", "pt_ps", "pt_ready", "pv_ps", "prec_ready", "att_ready"))
        at_ps, at_out, ao_ps, ao_ready = (sem(s) for s in ("at_ps", "at_out", "ao_ps", "ao_ready"))

        r_in, lg_ps, r_dve, r_act, r_iota, d_clear, ex_ps, ex_added = (sem(s) for s in ("r_in", "lg_ps", "r_dve", "r_act", "r_iota", "d_clear", "ex_ps", "ex_added"))
        ew_in = [sem("ew_in0"), sem("ew_in1")]
        stored = sem("stored")

        block = ctx.enter_context(nc.Block())

        def block_done(eng, q):
            if q == 1:
                eng.wait_ge(out_added, 1 + G * NT)
            elif q == 2:
                eng.wait_ge(f_dve, 1 + NT)
            elif q == 3:
                eng.wait_ge(ao_ready, NT)
            elif q == 4:
                eng.wait_ge(ex_added, NT + NE * NT)

        def pair(ap):
            return ap.rearrange("p (h c) -> p h c", h=HG)

        def heads(row):
            return cur[:, row, :].unsqueeze(2).to_broadcast([P, HG, HP])

        @block.sync
        def _(sp):
            for i in range(NT):
                sp.dma_start(x[:, i, :], hidden[i * P:(i + 1) * P, :]).then_inc(x_in, 16)
            sp.dma_start(wdt[:, :, :], w_dt).then_inc(small_in, 16)
            sp.dma_start(bcast[:, 0, :], dt_bias.partition_broadcast(P)).then_inc(small_in, 16)
            sp.dma_start(bcast[:, 1, :], A_log.partition_broadcast(P)).then_inc(small_in, 16)
            sp.dma_start(per[:, 5 * NT, :], Dskip.partition_broadcast(P)).then_inc(small_in, 16)
            sp.dma_start(par[:, :, 0:CT * KC], conv_w).then_inc(small_in, 16)
            sp.dma_start(par[:, :, CT * KC:CT * KC + CT], conv_b).then_inc(small_in, 16)
            sp.dma_start(par[:, :, CT * KC + CT:], norm_w).then_inc(small_in, 16)
            sp.dma_start(wc[:, :, :], w_conv[0]).then_inc(wconv_in, 16)
            sp.dma_start(wg[:, :, :], w_gate[0]).then_inc(wgate_in, 16)
            sp.dma_start(wor[:, :, :], w_out[0]).then_inc(wout_in, 16)
            with sp.Fori(0, G - 1) as g:
                sp.wait_ge(wout_scaled, KT * g + KT)
                sp.dma_start(wor[:, :, :], w_out[bass.ds(g + 1, 1)]).then_inc(wout_in, 16)
                sp.wait_ge(h_ready, NB * CT * g + NB * CT)
                sp.dma_start(wc[:, :, :], w_conv[bass.ds(g + 1, 1)]).then_inc(wconv_in, 16)
                sp.wait_ge(gate_ready, NT * g + NT)
                sp.dma_start(wg[:, :, :], w_gate[bass.ds(g + 1, 1)]).then_inc(wgate_in, 16)
            if STAGES >= 2:
                block_done(sp, 1)
                sp.wait_ge(gate_ready, G * NT)
                sp.dma_start(gus[:, 0, :], gate_s).then_inc(f_small, 16)
                sp.dma_start(gus[:, 1, :], up_s).then_inc(f_small, 16)
                sp.dma_start(dsb[:, :], down_s.partition_broadcast(P)).then_inc(f_small, 16)
                sp.dma_start(gur[:, :, :, :, :], ff_gu[0]).then_inc(gu_in, 16)
                sp.dma_start(dnr[:, :, :], ff_dn[0]).then_inc(dn_in, 16)
                with sp.Fori(0, FP - 1) as f:
                    sp.wait_ge(gu_cast, KT * f + KT)
                    sp.dma_start(gur[:, :, :, :, :], ff_gu[bass.ds(f + 1, 1)]).then_inc(gu_in, 16)
                    sp.wait_ge(dn_cast, 2 * f + 2)
                    sp.dma_start(dnr[:, :, :], ff_dn[bass.ds(f + 1, 1)]).then_inc(dn_in, 16)
            if STAGES >= 3:
                block_done(sp, 2)
                sp.dma_start(awv[:, :, :], wv).then_inc(awv_in, 16)
                sp.dma_start(abqk[:, :, :], bqk).then_inc(a_small, 16)
                sp.dma_start(abv[:, :], bv.partition_broadcast(P)).then_inc(a_small, 16)
                sp.dma_start(abo[:, :], bo.partition_broadcast(P)).then_inc(a_small, 16)
                sp.dma_start(awo[:, :, :], wo).then_inc(a_small, 16)
                sp.dma_start(awq[:, :, :], wq[0]).then_inc(aw_in, 16)
                sp.dma_start(awk[:, :, :], wk[0]).then_inc(aw_in, 16)
                with sp.Fori(0, AT - 1) as t:
                    sp.wait_ge(qk_ps, 2 * NB * t + 2 * NB)
                    sp.dma_start(awq[:, :, :], wq[bass.ds(t + 1, 1)]).then_inc(aw_in, 16)
                    sp.dma_start(awk[:, :, :], wk[bass.ds(t + 1, 1)]).then_inc(aw_in, 16)
            if STAGES >= 4:
                block_done(sp, 3)
                sp.dma_start(rw[:, :, :], gate_w).then_inc(r_in, 16)
                sp.dma_start(ew[:, 0, :, :], expert_w[0]).then_inc(ew_in[0], 16)
                sp.dma_start(ew[:, 1, :, :], expert_w[1]).then_inc(ew_in[1], 16)
                with sp.Fori(0, NE // 2 - 1) as e:
                    for s in range(2):
                        sp.wait_ge(ex_ps, 2 * NT * e + NT * (s + 1))
                        sp.dma_start(ew[:, s, :, :], expert_w[bass.ds(2 * e + 2 + s, 1)]).then_inc(ew_in[s], 16)
            for i in range(NT):
                sp.wait_ge(nsem[STAGES, "xn"], i + 1)
                sp.dma_start(out[i * P:(i + 1) * P, :], x[:, i, :]).then_inc(stored, 16)
            sp.wait_ge(stored, 16 * NT)

        def norm_vector(q):
            d = Count(nsem[q, "dve"])

            def moments(src):
                for i in range(NT):
                    at = d.inc(nc.vector.bn_stats(stats[:, i, :], src[:, i, :]))
                nc.vector.wait_ge(d.sem, at)
                for i in range(NT):
                    at = d.inc(nc.vector.bn_aggr(mv[:, i, :], stats[:, i, :]))
                nc.vector.wait_ge(d.sem, at)
                nc.vector.tensor_scalar(ve[:, :], mv[:, :, 1], EPS, None, ALU.add).then_inc(nsem[q, "var"], 1)

            if q > 0:
                block_done(nc.vector, q)
                moments(acc)
                nc.vector.wait_ge(nsem[q, "rstd"], 1)
                for i in range(NT):
                    at = d.inc(nc.vector.tensor_scalar(acc[:, i, :], acc[:, i, :], mv[:, i, 0:1], rs[:, i:i + 1],
                                                       ALU.subtract, ALU.mult))
                    nc.vector.wait_ge(d.sem, at)
                    ins = nc.vector.tensor_tensor(x[:, i, :], x[:, i, :], acc[:, i, :], ALU.add)
                    if q == STAGES:
                        ins.then_inc(nsem[q, "xn"], 1)
                    else:
                        at = d.inc(ins)
                nc.vector.wait_ge(d.sem, d.n)
            else:
                nc.vector.wait_ge(x_in, 16 * NT)
            if q < STAGES:
                moments(x)
                nc.vector.wait_ge(nsem[q, "rstd"], 2 if q else 1)
                for i in range(NT):
                    if i >= 2:
                        nc.vector.wait_ge(nsem[q, "tr"], i - 1)
                    nc.vector.tensor_scalar(xn[:, i % 2, :], x[:, i, :], mv[:, i, 0:1], rs[:, i:i + 1],
                                            ALU.subtract, ALU.mult).then_inc(nsem[q, "xn"], 1)

        def norm_pool(q):
            for r in range((q > 0) + (q < STAGES)):
                nc.gpsimd.wait_ge(nsem[q, "var"], r + 1)
                nc.gpsimd.tensor_tensor(rs[:, :], ve[:, :], mhalf[:, :], ALU.pow).then_inc(nsem[q, "rstd"], 1)

        def norm_tensor(q):
            for i in range(NT):
                nc.tensor.wait_ge(nsem[q, "xn"], i + 1)
                if i >= 2:
                    nc.tensor.wait_ge(nsem[q, "ev"], i - 1)
                for k in range(KT):
                    mmi = nc.tensor.transpose(bk(i % 2)[:, k * P:(k + 1) * P], xn[:, i % 2, k * P:(k + 1) * P], ident[:, :])
                mmi.then_inc(nsem[q, "tr"], 1)

        def norm_scalar(q):
            for i in range(NT):
                nc.scalar.wait_ge(nsem[q, "tr"], i + 1)
                nc.scalar.copy(xT[:, :, i * P:(i + 1) * P],
                               bk(i % 2).rearrange("p (k t) -> p k t", k=KT)).then_inc(nsem[q, "ev"], 1)

        @block.gpsimd
        def _(pool):
            pool.memset(ones[:, :], 1.0).then_inc(consts, 1)
            pool.memset(mhalf[:, :], -0.5).then_inc(consts, 1)
            pool.memset(epsc[:, :], EPS).then_inc(consts, 1)
            pool.wait_ge(consts, 3)
            pool.affine_select(out=ident[:, :], in_=ones[:, :], compare_op=ALU.is_equal, fill=0.0, base=0,
                               pattern=[[-1, P]], channel_multiplier=1).then_inc(consts, 1)
            pool.affine_select(out=upto[:, :], in_=ones[:, :], compare_op=ALU.is_ge, fill=0.0, base=0,
                               pattern=[[1, P]], channel_multiplier=-1).then_inc(consts, 1)
            pool.affine_select(out=after[:, :], in_=ones[:, :], compare_op=ALU.is_gt, fill=0.0, base=0,
                               pattern=[[-1, P]], channel_multiplier=1).then_inc(consts, 1)
            pool.memset(acc[:, :, :], 0.0).then_inc(acc_clear, 1)
            norm_pool(0)

            def decays(i):
                pool.tensor_tensor(am[:, i % 2, :, :], cur[:, i, :].unsqueeze(2).to_broadcast([P, HG, P]),
                                   upto[:, :].unsqueeze(1).to_broadcast([P, HG, P]), ALU.mult).then_inc(am_ready, 1)

            pool.wait_ge(consts, 6)
            with pool.Fori(0, G) as g:
                pool.wait_ge(cur_ready, g + 1)
                decays(0)
                for s in range(NT + 1):
                    i, c = s - 1, (s - 1) % CH
                    if s >= 1 and 1 <= c < CH - 1:
                        pool.wait_ge(state_ready, (CH - 1) * NB * g + (CH - 1) * (i // CH) + c)
                        pool.tensor_tensor(pair(sdec[:, :]), pair(state[:, :]), heads(4 * NT + i),
                                           ALU.mult).then_inc(sdec_ready, 1)
                    if s < NT:
                        pool.wait_ge(tp_out, 2 * NT * g + (s if s < 2 else 2 * s - 2) + 2)
                        src = pair(xtok[:, s % 2, :])
                        if s >= 2:
                            pool.wait_ge(y_ready, NT * g + s)
                        pool.tensor_tensor(pair(xd[:, s % 2, :]), src, heads(5 * NT), ALU.mult).then_inc(xd_ready, 1)
                        if s % CH < CH - 1:
                            pool.tensor_tensor(pair(xdec[:, s % 2, :]), src, heads(3 * NT + s),
                                               ALU.mult).then_inc(xdec_ready, 1)
                        pool.tensor_tensor(pair(dtx[:, s % 2, :]), src, heads(NT + s), ALU.mult).then_inc(dtx_ready, 1)
                        if s + 1 < NT:
                            decays(s + 1)
                    if s >= 1:
                        pool.wait_ge(ss_ready, NT * g + i + 1)
                        pool.tensor_tensor(ssv[:, i % 2:i % 2 + 1], ss[:, i % 2:i % 2 + 1], epsc[:, :],
                                           ALU.add).then_inc(ssv_ready, 1)
                        pool.wait_ge(ssv_ready, NT * g + i + 1)
                        pool.tensor_tensor(rg[:, i % 2:i % 2 + 1], ssv[:, i % 2:i % 2 + 1], mhalf[:, 0:1],
                                           ALU.pow).then_inc(rg_ready, 1)
            norm_pool(1)
            if STAGES >= 2:
                pool.wait_ge(nsem[1, "xn"], 1)
                pool.memset(acc[:, :, :], 0.0).then_inc(f_clear, 1)
                norm_pool(2)
            if STAGES >= 3:
                pool.memset(futf[:, :], 0.0).then_inc(sel_ready, 1)
                pool.wait_ge(sel_ready, 1)
                pool.affine_select(out=futf[:, :], in_=futf[:, :], compare_op=ALU.is_ge, fill=-1e30, base=0,
                                   pattern=[[-1, P]], channel_multiplier=1).then_inc(sel_ready, 1)
                norm_pool(3)
            if STAGES >= 4:
                pool.wait_ge(nsem[3, "xn"], 1)
                pool.iota(which[:, :], pattern=[[1, NE]], base=0, channel_multiplier=0,
                          allow_small_or_imprecise_dtypes=True).then_inc(r_iota, 1)
                pool.memset(acc[:, :, :], 0.0).then_inc(d_clear, 1)
                norm_pool(4)

        @block.scalar
        def _(act):
            act.sem_inc(tp_out, 1)
            act.sem_inc(e_ready, 1)
            norm_scalar(0)
            act.wait_ge(dt_dve, 2)
            nc.scalar.activation(z[:, 2, :], z[:, 1, :], ACT.Exp).then_inc(dt_act, 1)
            nc.scalar.activation(bcast[:, 1, :], bcast[:, 1, :], ACT.Exp).then_inc(dt_act, 1)
            act.wait_ge(dt_act, 1)
            nc.scalar.activation(z[:, 1, :], z[:, 2, :], ACT.Ln, bias=1.0).then_inc(dt_act, 1)
            for n, row in enumerate((2, 3, 4)):
                act.wait_ge(dt_cum, n + 1)
                nc.scalar.activation(per[:, row * NT:(row + 1) * NT, :],
                                     bk(n).rearrange("p (c h) -> p c h", c=NT), ACT.Exp).then_inc(dt_act, 1)
            with act.Fori(0, G) as g:
                act.wait_ge(par_ready, g + 1)
                for q in range(NB * CT + 1):
                    b, j = q // CT, q % CT
                    if q < NB * CT:
                        act.wait_ge(h_ready, NB * CT * g + q + 1)
                        act.wait_ge(xbc_ready, NB * CT * g + q + 1)
                        nc.scalar.activation(tap[:, q % 2, :], bk(q % 2), ACT.Identity,
                                             bias=parg[:, CT * KC + j:CT * KC + j + 1],
                                             scale=parg[:, KC * j + KC - 1:KC * j + KC]).then_inc(tap0, 1)
                    if q >= 1:
                        act.wait_ge(taps, 3 * (NB * CT) * g + 3 * q)
                        nc.scalar.activation(th[:, (q - 1) % 2, :], tap[:, (q - 1) % 2, :],
                                             ACT.Tanh).then_inc(tanh_ready, 1)
                act.wait_ge(wout_in, 16 * g + 16)
                for k in range(KT):
                    nc.scalar.activation(wos[:, k, :], wor[:, k, :], ACT.Copy,
                                         scale=parg[:, CT * KC + CT + k:CT * KC + CT + k + 1]).then_inc(wout_scaled, 1)
                for s in range(NT + 2):
                    if s < NT:
                        act.wait_ge(x_tr, NT * g + s + 1)
                        nc.scalar.copy(xtok[:, s % 2, :], bk(4)).then_inc(tp_out, 1)
                        act.wait_ge(d_ready, NT * g + s + 1)
                        nc.scalar.activation(em[:, s % 2, :, :], banks[:, 2:4, :].rearrange("p b (h t) -> p (b h) t", t=P),
                                             ACT.Exp).then_inc(e_ready, 1)
                    if 1 <= s <= NT:
                        act.wait_ge(y_ready, NT * g + s + 1)
                        nc.scalar.activation(ysq[:, :], y[:, (s - 1) % 2, :], ACT.Square, scale=float(GI) ** -0.5,
                                             accum_out=ss[:, (s - 1) % 2:(s - 1) % 2 + 1]).then_inc(ss_ready, 1)
                    if s >= 2:
                        act.wait_ge(yn_tr, NT * g + s - 1)
                        nc.scalar.copy(ynT[:, s % 2, :], bk(4)).then_inc(tp_out, 1)
                    if s < NT:
                        act.wait_ge(gate_ready, NT * g + s + 1)
                        nc.scalar.activation(tg[:, s % 2, :], bk(0), ACT.Tanh, scale=0.5).then_inc(tg_ready, 1)
            norm_scalar(1) if STAGES >= 2 else None
            if STAGES >= 2:
                with act.Fori(0, FP) as f:
                    act.wait_ge(up_ps, 4 * f + 1)
                    act.wait_ge(gu_in, 16 * f + 16)
                    for k in range(KT):
                        nc.scalar.copy(gu[:, k, :, :, :], gur[:, k, :, :, :]).then_inc(gu_cast, 1)
                    act.wait_ge(fsc_ready, f + 1)
                    for q in range(4):
                        act.wait_ge(gate_ps, 4 * f + q + 1)
                        nc.scalar.activation(fth[:, q % 2, :], bk(q % 2), ACT.Tanh,
                                             scale=fscg[:, 0, q % 2:q % 2 + 1]).then_inc(f_tanh, 1)
                        if q == 0:
                            act.wait_ge(dn_in, 16 * f + 16)
                            for k in range(2):
                                nc.scalar.copy(dn[:, k, :], dnr[:, k, :]).then_inc(dn_cast, 1)
                norm_scalar(2) if STAGES >= 3 else None
            if STAGES >= 3:
                with act.Fori(0, AT) as t:
                    act.wait_ge(bias_ready, t + 1)
                    for b in range(NB):
                        n = NB * t + b
                        for w in range(2):
                            act.wait_ge(qk_ps, 2 * n + w + 1)
                            nc.scalar.activation(qf[:, w, :], bk(w), ACT.Identity,
                                                 bias=abg[:, w:w + 1],
                                                 scale=HD ** -0.5 if w == 0 else 1.0).then_inc(qk_f, 1)
                            act.wait_ge(qk_f, 2 * n + w + 1)
                            nc.scalar.copy(qh[:, w, :], qf[:, w, :]).then_inc(qk_h, 1)
                        for m in range(0, 8, 2):
                            act.wait_ge(st_ps, 8 * n + m + 1)
                            nc.scalar.copy((qs, ks)[m // 4][:, m % 4, :], bk(m % 2)).then_inc(st_out, 1)
                        for u in range(16):
                            qi = u // 4
                            kw = (qi + 1) * P
                            act.wait_ge(max_ready, 16 * n + u + 1)
                            if u >= 2:
                                act.wait_ge(pt_ps, 16 * n + u - 1)
                            for j in range(2):
                                e = nc.scalar.activation(prob[:, u % 2, j, 0:kw], bk(2 * (u % 2) + j)[:, 0:kw], ACT.Exp,
                                                         bias=nmax[:, u % 2, j:j + 1],
                                                         accum_out=psum[:, qi % 2, 2 * (u % 4) + j:2 * (u % 4) + j + 1])
                            e.then_inc(exp_ready, 1)
                for i in range(NT):
                    act.wait_ge(at_ps, i + 1)
                    nc.scalar.copy(attT[:, i % 2, :], bk(i % 2)).then_inc(at_out, 1)
                norm_scalar(3) if STAGES >= 4 else None
            if STAGES >= 4:
                act.wait_ge(r_dve, 2 + 2 * NT)
                nc.scalar.activation(rt[:, 1, :], rt[:, 0, :], ACT.Exp).then_inc(r_act, 1)

        @block.vector
        def _(dve):
            dve.sem_inc(xbc_ready, 2)
            dve.sem_inc(gb_used, 1)
            dve.sem_inc(yo_used, 1)
            dve.sem_inc(y_ready, 1)
            dve.sem_inc(gate_used, 1)
            dve.sem_inc(out_added, 1)
            norm_vector(0)
            dve.wait_ge(dt_ps, 1)
            dve.wait_ge(small_in, 16 * 7)
            d = Count(dt_dve)

            def chain(ins):
                d.inc(ins)
                dve.wait_ge(dt_dve, d.n)

            chain(nc.vector.tensor_tensor(z[:, 0, :].rearrange("p (c h) -> p c h", c=NT),
                                          bk(0).rearrange("p (c h) -> p c h", c=NT),
                                          bcast[:, 0, :].unsqueeze(1).to_broadcast([P, NT, H]), ALU.add))
            chain(nc.vector.scalar_tensor_tensor(z[:, 1, :], z[:, 0, :], -1.0, z[:, 0, :], ALU.mult, ALU.min))
            dve.wait_ge(dt_act, 3)
            chain(nc.vector.tensor_scalar(z[:, 3, :], z[:, 2, :], 1.0, None, ALU.add))
            chain(nc.vector.tensor_scalar(z[:, 3, :], z[:, 3, :], -1.0, None, ALU.add))
            chain(nc.vector.tensor_tensor(z[:, 3, :], z[:, 2, :], z[:, 3, :], ALU.subtract))
            chain(nc.vector.tensor_tensor(z[:, 3, :], z[:, 1, :], z[:, 3, :], ALU.add))
            dtall = per[:, NT:2 * NT, :].rearrange("p c h -> p (c h)")
            chain(nc.vector.scalar_tensor_tensor(dtall, z[:, 0, :], 0.0, z[:, 3, :], ALU.max, ALU.add))
            chain(nc.vector.scalar_tensor_tensor(per[:, 0:NT, :], per[:, NT:2 * NT, :], -1.0,
                                                 bcast[:, 1, :].unsqueeze(1).to_broadcast([P, NT, H]), ALU.mult, ALU.mult))
            dve.wait_ge(dt_act, 6)
            chain(nc.vector.tensor_tensor(per[:, 3 * NT:4 * NT, :], per[:, 3 * NT:4 * NT, :], per[:, NT:2 * NT, :], ALU.mult))
            chain(nc.vector.tensor_scalar(par[:, :, :], par[:, :, :], 0.5, None, ALU.mult))
            with dve.Fori(0, G) as g:
                n0 = NT * g
                nc.vector.tensor_copy(parg[:, :], par[:, bass.ds(g, 1), :].rearrange("p a b -> p (a b)")).then_inc(par_ready, 1)
                nc.vector.tensor_copy(cur[:, :, :], per[:, :, bass.ds(HG * g, HG)]).then_inc(cur_ready, 1)
                for q in range(NB * CT + 1):
                    b, j = q // CT, q % CT
                    if q < NB * CT:
                        dve.wait_ge(tap0, NB * CT * g + q + 1)
                        for k in range(KC - 2, -1, -1):
                            sh = KC - 1 - k
                            if sh > 1:
                                dve.wait_ge(taps, 3 * NB * CT * g + 3 * q + sh - 1)
                            nc.vector.scalar_tensor_tensor(
                                tap[:, q % 2, sh:L], bk(q % 2)[:, 0:L - sh],
                                parg[:, KC * j + k:KC * j + k + 1],
                                tap[:, q % 2, sh:L], ALU.mult, ALU.add).then_inc(taps, 1)
                    if q >= 1:
                        b, j = (q - 1) // CT, (q - 1) % CT
                        dve.wait_ge(tanh_ready, NB * CT * g + q)
                        nc.vector.scalar_tensor_tensor(xbc[:, j, b * L:(b + 1) * L], th[:, (q - 1) % 2, :], 1.0,
                                                       tap[:, (q - 1) % 2, :], ALU.add, ALU.mult).then_inc(xbc_ready, 1)
                for s in range(NT + 2):
                    i = s - 2
                    if s >= 2:
                        dve.wait_ge(rg_ready, NT * g + i + 1)
                        nc.vector.scalar_tensor_tensor(yn[:, i % 2, :], y[:, i % 2, :], rg[:, i % 2:i % 2 + 1],
                                                       sg[:, i % 2, :], ALU.mult, ALU.mult).then_inc(yn_ready, 1)
                    i, c = s - 1, (s - 1) % CH
                    if 1 <= s <= NT:
                        m = (CH - 1) * NB * g + (CH - 1) * (i // CH)
                        if c > 0:
                            dve.wait_ge(yo_ready, m + c)
                            nc.vector.tensor_tensor(pair(yoff[:, :]), pair(bk(6)), heads(2 * NT + i), ALU.mult).then_inc(yo_used, 1)
                        dve.wait_ge(yi_ready, NT * g + i + 1)
                        dve.wait_ge(xd_ready, NT * g + i + 1)
                        ins = nc.vector.tensor_tensor(y[:, i % 2, :], bk(7), xd[:, i % 2, :], ALU.add)
                        if c > 0:
                            ins.then_inc(y_part, 1)
                            dve.wait_ge(y_part, m + c)
                            dve.wait_ge(yo_used, m + c + 1)
                            nc.vector.tensor_tensor(y[:, i % 2, :], y[:, i % 2, :], yoff[:, :], ALU.add).then_inc(y_ready, 1)
                        else:
                            ins.then_inc(y_ready, 1)
                        if c < CH - 1:
                            dve.wait_ge(st_ready, m + c + 1)
                            if c == 0:
                                nc.vector.tensor_copy(state[:, :], bk(6)).then_inc(state_ready, 1)
                            else:
                                dve.wait_ge(sdec_ready, (CH - 2) * NB * g + (CH - 2) * (i // CH) + c)
                                nc.vector.tensor_tensor(state[:, :], bk(6), sdec[:, :], ALU.add).then_inc(state_ready, 1)
                    if s < NT:
                        dve.wait_ge(gb_ready, NT * g + s + 1)
                        nc.vector.tensor_copy(btok[:, s % 2, :], bk(5)[:, P:2 * P])
                        nc.vector.tensor_tensor(gmask[:, :], bk(5)[:, 0:P], upto[:, :], ALU.mult).then_inc(gb_used, 1)
                        dve.wait_ge(e_ready, NT * g + s + 2)
                        dve.wait_ge(gb_used, NT * g + s + 2)
                        nc.vector.tensor_tensor(em[:, s % 2, :, :], em[:, s % 2, :, :],
                                                gmask[:, :].unsqueeze(1).to_broadcast([P, HG, P]), ALU.mult).then_inc(m_ready, 1)
                        dve.wait_ge(tg_ready, NT * g + s + 1)
                        nc.vector.scalar_tensor_tensor(sg[:, s % 2, :], tg[:, s % 2, :], 1.0, bk(0), ALU.add,
                                                       ALU.mult).then_inc(gate_used, 1)
                    i = s - 2
                    if s >= 2:
                        dve.wait_ge(o_ready, NT * g + i + 1)
                        nc.vector.tensor_tensor(acc[:, i, :], acc[:, i, :], bk(1), ALU.add).then_inc(out_added, 1)
            norm_vector(1)
            if STAGES >= 2:
                dve.wait_ge(f_small, 48)
                nc.vector.tensor_scalar(fsc[:, 0, :], gus[:, 0, :], 0.5, None, ALU.mult).then_inc(f_dve, 1)
                dve.wait_ge(f_dve, 1)
                nc.vector.tensor_tensor(fsc[:, 1, :], fsc[:, 0, :], gus[:, 1, :], ALU.mult).then_inc(f_part, 1)
                dve.wait_ge(f_part, 1)
                dve.sem_inc(down_added, 4)
                dve.wait_ge(f_clear, 1)
                with dve.Fori(0, FP) as f:
                    nc.vector.tensor_copy(fscg[:, :, :], fsc[:, :, bass.ds(2 * f, 2)]).then_inc(fsc_ready, 1)
                    for q in range(4):
                        b = q // 2
                        dve.wait_ge(f_tanh, 4 * f + q + 1)
                        nc.vector.scalar_tensor_tensor(fh[:, q % 2, :], fth[:, q % 2, :], 1.0, bk(q % 2), ALU.add,
                                                       ALU.mult).then_inc(f_part, 1)
                        dve.wait_ge(f_part, 4 * f + q + 2)
                        dve.wait_ge(up_ps, 4 * f + q + 2)
                        nc.vector.scalar_tensor_tensor(hid[:, q % 2, b * L:(b + 1) * L], fh[:, q % 2, :],
                                                       fscg[:, 1, q % 2:q % 2 + 1], bk(2 + q % 2),
                                                       ALU.mult, ALU.mult).then_inc(hid_ready, 1)
                    for i in range(NT):
                        dve.wait_ge(down_ps, NT * f + i + 1)
                        nc.vector.tensor_tensor(acc[:, i, :], acc[:, i, :], bk(4 + i % 4), ALU.add).then_inc(down_added, 1)
                dve.wait_ge(down_added, 4 + NT * FP)
                for i in range(NT):
                    nc.vector.tensor_tensor(acc[:, i, :], acc[:, i, :], dsb[:, :], ALU.mult).then_inc(f_dve, 1)
                norm_vector(2)
            if STAGES >= 3:
                dve.wait_ge(sel_ready, 2)
                s = Count(sel_ready)
                s.n = 2

                def step(ins):
                    s.inc(ins)
                    dve.wait_ge(sel_ready, s.n)

                flat = fold[:, :, :].rearrange("p a b -> p (a b)")
                step(nc.vector.tensor_tensor(flat, ident[:, 0:32], ident[:, 32:64], ALU.add))
                step(nc.vector.tensor_tensor(flat, flat, ident[:, 64:96], ALU.add))
                step(nc.vector.tensor_tensor(flat, flat, ident[:, 96:128], ALU.add))
                step(nc.vector.tensor_scalar(sel[:, :, :], ident[:, :].unsqueeze(1).to_broadcast([P, 4, P]), 0.0, None, ALU.mult))
                for m, reps in enumerate(((0, 2), (1, 3), (0, 1), (2, 3))):
                    dst = sel[:, m, :].rearrange("p (a r d) -> p a r d", a=2, r=4)
                    for r in reps:
                        step(nc.vector.tensor_copy(dst[:, :, r, :], fold[:, :, :]))
                step(nc.vector.tensor_copy(identr[:, :], ident[:, :]))
                step(nc.vector.tensor_copy(future[:, :], futf[:, :]))
                dve.sem_inc(v_ready, 2)
                dve.sem_inc(att_ready, 1)
                dve.wait_ge(a_small, 64)
                nc.vector.tensor_scalar(abqk[:, 0, :], abqk[:, 0, :], HD ** -0.5, None, ALU.mult).then_inc(qb_scaled, 1)
                for i in range(NT):
                    dve.wait_ge(v_ps, i + 1)
                    nc.vector.tensor_tensor(v[:, i, :], bk(i % 2), abv[:, :], ALU.add).then_inc(v_ready, 1)
                dve.wait_ge(qb_scaled, 1)
                with dve.Fori(0, AT) as t:
                    nc.vector.tensor_copy(abg[:, :], abqk[:, :, bass.ds(t, 1)].rearrange("p a b -> p (a b)")).then_inc(bias_ready, 1)
                    for b in range(NB):
                        n = NB * t + b
                        for w in range(2):
                            dve.wait_ge(qk_h, 2 * n + w + 1)
                            nc.vector.tensor_tensor(ql[:, w, :], qf[:, w, :], qh[:, w, :].bitcast(F32),
                                                    ALU.subtract).then_inc(qk_l, 1)
                        for m in range(1, 8, 2):
                            dve.wait_ge(st_ps, 8 * n + m + 1)
                            nc.vector.tensor_copy((qs, ks)[m // 4][:, m % 4, :], bk(m % 2)).then_inc(st_out2, 1)
                        for u in range(17):
                            if u < 16:
                                kw = (u // 4 + 1) * P
                                dve.wait_ge(s_ready, 16 * n + u + 1)
                                nc.vector.tensor_reduce(nmax[:, u % 2, :],
                                                        banks[:, 2 * (u % 2):2 * (u % 2) + 2, 0:kw],
                                                        AX, ALU.max, negate=True).then_inc(max_ready, 1)
                            w = u - 1
                            if u >= 1:
                                kw = (w // 4 + 1) * P
                                dve.wait_ge(pt_ps, 16 * n + w + 1)
                                nc.vector.tensor_copy(pT[:, w % 2, :, 0:kw], banks[:, 4:6, 0:kw]).then_inc(pt_ready, 1)
                                if w % 4 == 3:
                                    qi = w // 4
                                    dve.wait_ge(exp_ready, 16 * n + w + 1)
                                    nc.vector.reciprocal(prec[:, :], psum[:, qi % 2, :]).then_inc(prec_ready, 1)
                                    dve.wait_ge(prec_ready, 4 * n + qi + 1)
                                    dve.wait_ge(pv_ps, 4 * n + qi + 1)
                                    nc.vector.tensor_tensor(
                                        att[:, b * CH + qi, bass.ds(P * t, P)].rearrange("p (h d) -> p h d", d=HD),
                                        bk(6)[:, 0:P].rearrange("p (h d) -> p h d", d=HD),
                                        prec[:, :].unsqueeze(2).to_broadcast([P, HT, HD]), ALU.mult).then_inc(att_ready, 1)
                for i in range(NT):
                    dve.wait_ge(ao_ps, i + 1)
                    nc.vector.tensor_tensor(acc[:, i, :], bk(6 + i % 2), abo[:, :], ALU.add).then_inc(ao_ready, 1)
                norm_vector(3)
            if STAGES >= 4:
                dve.wait_ge(lg_ps, 1)
                r = Count(r_dve)

                def rstep(ins, wait=True):
                    r.inc(ins)
                    if wait:
                        dve.wait_ge(r_dve, r.n)

                rstep(nc.vector.tensor_copy(lg[:, :, :], bk(0)[:, 0:NT * NE].rearrange("p (a b) -> p a b", a=NT)))
                for i in range(NT):
                    rstep(nc.vector.max(top[:, i, :], lg[:, i, :]), i == NT - 1)
                for i in range(NT):
                    rstep(nc.vector.max_index(topi[:, i, :], top[:, i, :], lg[:, i, :]), i == NT - 1)
                rstep(nc.vector.tensor_tensor(rt[:, 0, :], top[:, :, 1], top[:, :, 0], ALU.subtract))
                rstep(nc.vector.tensor_copy(topf[:, :, :], topi[:, :, :]))
                dve.wait_ge(r_act, 1)
                dve.wait_ge(r_iota, 1)
                rstep(nc.vector.tensor_scalar(rt[:, 2, :], rt[:, 1, :], 1.0, None, ALU.add))
                rstep(nc.vector.reciprocal(rt[:, 2, :], rt[:, 2, :]))
                rstep(nc.vector.tensor_tensor(rt[:, 3, :], rt[:, 2, :], rt[:, 1, :], ALU.mult))
                for c in range(2):
                    rstep(nc.vector.tensor_tensor(oh[:, c, :, :], which[:, :].unsqueeze(1).to_broadcast([P, NT, NE]),
                                                  topf[:, :, c].unsqueeze(2).to_broadcast([P, NT, NE]), ALU.is_equal))
                    rstep(nc.vector.tensor_tensor(oh[:, c, :, :], oh[:, c, :, :],
                                                  rt[:, 2 + c, :].unsqueeze(2).to_broadcast([P, NT, NE]), ALU.mult))
                rstep(nc.vector.tensor_tensor(we[:, :, :], oh[:, 0, :, :], oh[:, 1, :, :], ALU.add))
                dve.wait_ge(d_clear, 1)
                dve.sem_inc(ex_added, NT)
                with dve.Fori(0, NE // 2) as e:
                    for s in range(2):
                        for i in range(NT):
                            dve.wait_ge(ex_ps, 2 * NT * e + NT * s + i + 1)
                            nc.vector.scalar_tensor_tensor(acc[:, i, :], bk(i), we[:, i, bass.ds(2 * e + s, 1)],
                                                           acc[:, i, :], ALU.mult, ALU.add).then_inc(ex_added, 1)
                norm_vector(4)

        @block.tensor
        def _(pe):
            mat = nc.tensor.matmul
            pe.sem_inc(up_ps, 1)
            pe.wait_ge(consts, 6)
            norm_tensor(0)
            pe.wait_ge(nsem[0, "ev"], NT)
            pe.wait_ge(small_in, 16 * 7)
            for i in range(NT):
                for k in range(KT):
                    m = mat(bk(0)[:, i * H:(i + 1) * H], xT[:, k, i * P:(i + 1) * P], wdt[:, k, :],
                            start=(k == 0), stop=(k == KT - 1))
            m.then_inc(dt_ps, 1)
            pe.wait_ge(dt_dve, 8)
            for n, mask in enumerate((upto, after, ones)):
                mat(bk(n), mask[:, :], per[:, 0:NT, :].rearrange("p c h -> p (c h)"), start=True, stop=True).then_inc(dt_cum, 1)
            pe.wait_ge(dt_act, 6)
            with pe.Fori(0, G) as g:
                pe.wait_ge(wconv_in, 16 * g + 16)
                for q in range(NB * CT):
                    b, j = q // CT, q % CT
                    if q == 0:
                        pe.wait_ge(gate_used, NT * g + 1)
                    elif q == 1:
                        pe.wait_ge(out_added, NT * g + 1)
                    else:
                        pe.wait_ge(taps, 3 * NB * CT * g + 3 * (q - 1))
                    for k in range(KT):
                        m = mat(bk(q % 2), wc[:, k, j * P:(j + 1) * P], xT[:, k, b * L:(b + 1) * L],
                                start=(k == 0), stop=(k == KT - 1))
                    m.then_inc(h_ready, 1)
                for s in range(NT + 2):
                    if s < NT:
                        b = s // CH
                        tok = slice(s * P, (s + 1) * P)
                        if s % CH == 0:
                            pe.wait_ge(xbc_ready, NB * CT * g + CT * (b + 1) + 2)
                        pe.wait_ge(tp_out, 2 * NT * g + (s if s < 2 else 2 * s - 2) + 1)
                        for j in range(KT):
                            m = pe.transpose(bk(4)[:, j * P:(j + 1) * P], xbc[:, j, tok], ident[:, :])
                        m.then_inc(x_tr, 1)
                        pe.wait_ge(gb_used, NT * g + s + 1)
                        pe.transpose(bk(5)[:, P:2 * P], xbc[:, JB, tok], ident[:, :])
                        mat(bk(5)[:, 0:P], xbc[:, JB, tok], xbc[:, JC, tok], start=True, stop=True).then_inc(gb_ready, 1)
                        pe.wait_ge(am_ready, NT * g + s + 1)
                        pe.wait_ge(e_ready, NT * g + s + 1)
                        for w in range(2):
                            m = mat(bk(2 + w), after[:, :],
                                    am[:, s % 2, 4 * w:4 * w + 4, :].rearrange("p h t -> p (h t)"), start=True, stop=True)
                        m.then_inc(d_ready, 1)
                    i, c = s - 1, (s - 1) % CH
                    if 1 <= s <= NT:
                        tok = slice(i * P, (i + 1) * P)
                        m0 = (CH - 1) * NB * g + (CH - 1) * (i // CH)
                        if c > 0:
                            pe.wait_ge(state_ready, m0 + c)
                            mat(bk(6), xbc[:, JC, tok], state[:, :], start=True, stop=True).then_inc(yo_ready, 1)
                        pe.wait_ge(m_ready, NT * g + i + 1)
                        pe.wait_ge(dtx_ready, NT * g + i + 1)
                        pe.wait_ge(y_ready, NT * g + i + 1)
                        for h in range(HG):
                            m = mat(bk(7)[:, h * HP:(h + 1) * HP], em[:, i % 2, h, :], dtx[:, i % 2, h * HP:(h + 1) * HP],
                                    start=True, stop=True)
                        m.then_inc(yi_ready, 1)
                        if c < CH - 1:
                            pe.wait_ge(xdec_ready, m0 + c + 1)
                            pe.wait_ge(yo_used, m0 + c + 1)
                            mat(bk(6), btok[:, i % 2, :], xdec[:, i % 2, :], start=True, stop=True).then_inc(st_ready, 1)
                    i = s - 2
                    if s >= 2:
                        pe.wait_ge(yn_ready, NT * g + i + 1)
                        u = 2 * s - 1 if s < NT else 2 * NT - 2 + (s - NT)
                        pe.wait_ge(tp_out, 2 * NT * g + u + 1)
                        for j in range(KT):
                            m = pe.transpose(bk(4)[:, j * P:(j + 1) * P], yn[:, i % 2, j * P:(j + 1) * P], ident[:, :])
                        m.then_inc(yn_tr, 1)
                    if s < NT:
                        if s == 0:
                            pe.wait_ge(wgate_in, 16 * g + 16)
                            pe.wait_ge(taps, 3 * NB * CT * g + 3 * NB * CT)
                        pe.wait_ge(gate_used, NT * g + s + 1)
                        for k in range(KT):
                            m = mat(bk(0), xT[:, k, s * P:(s + 1) * P], wg[:, k, :], start=(k == 0), stop=(k == KT - 1))
                        m.then_inc(gate_ready, 1)
                    if s >= 2:
                        if i == 0:
                            pe.wait_ge(wout_scaled, KT * g + KT)
                        pe.wait_ge(out_added, NT * g + i + 1)
                        pe.wait_ge(tp_out, 2 * NT * g + u + 2)
                        for k in range(KT):
                            m = mat(bk(1), ynT[:, i % 2, k * P:(k + 1) * P], wos[:, k, :], start=(k == 0), stop=(k == KT - 1))
                        m.then_inc(o_ready, 1)
            if STAGES >= 2:
                norm_tensor(1)
                pe.wait_ge(nsem[1, "ev"], NT)
                with pe.Fori(0, FP) as f:
                    for q in range(4):
                        b, ft = q // 2, q % 2
                        if q == 0:
                            pe.wait_ge(gu_cast, KT * f + KT)
                        if q >= 2:
                            pe.wait_ge(hid_ready, 4 * f + q - 1)
                        for w, s in ((0, gate_ps), (1, up_ps)):
                            for k in range(KT):
                                m = mat(bk(2 * w + q % 2), gu[:, k, ft, w, :], xT[:, k, b * L:(b + 1) * L],
                                        start=(k == 0), stop=(k == KT - 1))
                            m.then_inc(s, 1)
                    pe.wait_ge(dn_cast, 2 * f + 2)
                    for i in range(NT):
                        if i % CH == 0:
                            pe.wait_ge(hid_ready, 4 * f + 2 * (i // CH) + 2)
                        pe.wait_ge(down_added, NT * f + i + 1)
                        for k in range(2):
                            m = mat(bk(4 + i % 4), hid[:, k, i * P:(i + 1) * P], dn[:, k, :], start=(k == 0), stop=(k == 1))
                        m.then_inc(down_ps, 1)
            if STAGES >= 3:
                norm_tensor(2)
                pe.wait_ge(nsem[2, "ev"], NT)
                pe.wait_ge(awv_in, 16)
                for i in range(NT):
                    pe.wait_ge(v_ready, i + 1)
                    for k in range(KT):
                        m = mat(bk(i % 2), xT[:, k, i * P:(i + 1) * P], awv[:, k, :], start=(k == 0), stop=(k == KT - 1))
                    m.then_inc(v_ps, 1)
                pe.wait_ge(sel_ready, 2 + 4 + 8 + 2)
                pe.wait_ge(v_ready, 2 + NT)
                with pe.Fori(0, AT) as t:
                    for b in range(NB):
                        n = NB * t + b
                        if b == 0:
                            pe.wait_ge(aw_in, 32 * t + 32)
                        for w, wt in enumerate((awq, awk)):
                            for k in range(KT):
                                m = mat(bk(w), wt[:, k, :], xT[:, k, b * L:(b + 1) * L], start=(k == 0), stop=(k == KT - 1))
                            m.then_inc(qk_ps, 1)
                        pe.wait_ge(qk_l, 2 * n + 2)
                        for m8 in range(8):
                            w, pr = m8 // 4, m8 % 4
                            if m8 >= 2:
                                pe.wait_ge((st_out, st_out2)[m8 % 2], 4 * n + m8 // 2)
                            rows = slice(32 * pr, 32 * pr + 32)
                            mat(bk(m8 % 2), sel[rows, 2 * w, :], qh[rows, w, :], start=True, stop=False)
                            mat(bk(m8 % 2), sel[rows, 2 * w + 1, :], ql[rows, w, :], start=False, stop=True).then_inc(st_ps, 1)
                        for u in range(19):
                            if u < 16:
                                qi, pr = u // 4, u % 4
                                kw = (qi + 1) * P
                                if u == 0:
                                    pe.wait_ge(st_out, 4 * n + 4)
                                    pe.wait_ge(st_out2, 4 * n + 4)
                                if u >= 2:
                                    pe.wait_ge(exp_ready, 16 * n + u - 1)
                                for j in range(2):
                                    rows = slice(64 * j, 64 * j + 64)
                                    o = bk(2 * (u % 2) + j)
                                    mat(o[:, 0:kw], qs[rows, pr, qi * P:kw], ks[rows, pr, 0:kw], start=True, stop=False)
                                    m = mat(o[:, kw - P:kw], identr[:, :], future[:, :], start=False, stop=True)
                                m.then_inc(s_ready, 1)
                            w = u - 2
                            if 0 <= w < 16:
                                pe.wait_ge(exp_ready, 16 * n + w + 1)
                                if w >= 1:
                                    pe.wait_ge(pt_ready, 16 * n + w)
                                for j in range(2):
                                    for c in range(w // 4 + 1):
                                        m = pe.transpose(bk(4 + j)[:, c * P:(c + 1) * P], prob[:, w % 2, j, c * P:(c + 1) * P], ident[:, :])
                                m.then_inc(pt_ps, 1)
                            w = u - 3
                            if w >= 0:
                                qi, pr = w // 4, w % 4
                                pe.wait_ge(pt_ready, 16 * n + w + 1)
                                if w % 4 == 0:
                                    pe.wait_ge(att_ready, 4 * n + qi + 1)
                                for j in range(2):
                                    o = bk(6)[:, HD * (2 * pr + j):HD * (2 * pr + j + 1)]
                                    for c in range(qi + 1):
                                        m = mat(o, pT[:, w % 2, j, c * P:(c + 1) * P],
                                                v[:, b * CH + c, bass.ds(P * t + HD * (2 * pr + j), HD)],
                                                start=(c == 0), stop=(c == qi))
                                if pr == 3:
                                    m.then_inc(pv_ps, 1)
                for i in range(NT + 1):
                    if i < NT:
                        if i == 0:
                            pe.wait_ge(att_ready, 4 * NB * AT + 1)
                        if i >= 2:
                            pe.wait_ge(at_out, i - 1)
                        for k in range(KT):
                            m = pe.transpose(bk(i % 2)[:, k * P:(k + 1) * P], att[:, i, k * P:(k + 1) * P], ident[:, :])
                        m.then_inc(at_ps, 1)
                    if i >= 1:
                        j = i - 1
                        pe.wait_ge(at_out, j + 1)
                        if j >= 2:
                            pe.wait_ge(ao_ready, j - 1)
                        for k in range(KT):
                            m = mat(bk(6 + j % 2), attT[:, j % 2, k * P:(k + 1) * P], awo[:, k, :], start=(k == 0), stop=(k == KT - 1))
                        m.then_inc(ao_ps, 1)
            if STAGES >= 4:
                norm_tensor(3)
                pe.wait_ge(nsem[3, "ev"], NT)
                pe.wait_ge(r_in, 16)
                for i in range(NT):
                    for k in range(KT):
                        m = mat(bk(0)[:, i * NE:(i + 1) * NE], xT[:, k, i * P:(i + 1) * P], rw[:, k, :],
                                start=(k == 0), stop=(k == KT - 1))
                m.then_inc(lg_ps, 1)
                pe.wait_ge(r_dve, 1)
                with pe.Fori(0, NE // 2) as e:
                    for s in range(2):
                        pe.wait_ge(ew_in[s], 16 * e + 16)
                        for i in range(NT):
                            pe.wait_ge(ex_added, 2 * NT * e + NT * s + i + 1)
                            for k in range(KT):
                                m = mat(bk(i), xT[:, k, i * P:(i + 1) * P], ew[:, s, k, :], start=(k == 0), stop=(k == KT - 1))
                            m.then_inc(ex_ps, 1)


def kernel(**inputs):
    from concourse.bacc import Bacc
    from concourse.bass_utils import run_bass_kernel_spmd

    a = {k: np.asarray(v) for k, v in inputs.items()}

    def rows(w):
        return w.T.reshape(KT, P, -1).transpose(1, 0, 2)

    w_in = a["L0_attn_in_proj_w"]
    inner, gn = H * HP, G * NS
    gate_w, x_w, b_w, c_w, dt_w = np.split(w_in, [inner, 2 * inner, 2 * inner + gn, 2 * inner + 2 * gn])

    def by_group(x, b, c):
        return np.concatenate([m.reshape(G, -1, *m.shape[1:]) for m in (x, b, c)], 1)

    conv = by_group(x_w, b_w, c_w)
    cw = by_group(*np.split(a["L0_attn_conv_weight"], [inner, inner + gn])).reshape(G, CT, P, KC)
    cb = by_group(*np.split(a["L0_attn_conv_bias"], [inner, inner + gn])).reshape(G, CT, P)
    gu = np.stack([a["L0_ffn_gate_t"], a["L0_ffn_up_t"]]).reshape(2, FP, 2, P, KT, P)
    arrays = {
        "hidden": a["L0_attn_hidden_states"].reshape(NB * L, DM),
        "w_conv": np.stack([rows(m) for m in conv]),
        "w_gate": np.stack([rows(m) for m in gate_w.reshape(G, GI, DM)]),
        "w_dt": rows(dt_w),
        "conv_w": cw.transpose(2, 0, 1, 3),
        "conv_b": cb.transpose(2, 0, 1),
        "dt_bias": a["L0_attn_dt_bias"],
        "A_log": a["L0_attn_A_log"],
        "Dskip": a["L0_attn_D"],
        "norm_w": a["L0_attn_norm_weight"].reshape(G, KT, P).transpose(2, 0, 1),
        "w_out": a["L0_attn_out_proj_w"].reshape(DM, G, KT, P).transpose(1, 3, 2, 0),
        "ff_gu": gu.transpose(1, 5, 4, 2, 0, 3),
        "ff_dn": a["L0_ffn_down_t"].reshape(DM, FP, 2, P).transpose(1, 3, 2, 0),
        "gate_s": a["L0_ffn_gate_s"].reshape(FT, P).T,
        "up_s": a["L0_ffn_up_s"].reshape(FT, P).T,
        "down_s": a["L0_ffn_down_s"],
        "wq": a["L1_attn_Wq"].reshape(AT, P, KT, P).transpose(0, 3, 2, 1),
        "wk": a["L1_attn_Wk"].reshape(AT, P, KT, P).transpose(0, 3, 2, 1),
        "bqk": np.stack([a["L1_attn_bq"], a["L1_attn_bk"]]).reshape(2, AT, P).transpose(2, 0, 1),
        "wv": rows(a["L1_attn_Wv"]),
        "bv": a["L1_attn_bv"],
        "wo": rows(a["L1_attn_Wo"]),
        "bo": a["L1_attn_bo"],
        "gate_w": a["L1_ffn_gate_w"].reshape(KT, P, NE).transpose(1, 0, 2),
        "expert_w": a["L1_ffn_expert_w"].reshape(NE, KT, P, DM).transpose(0, 2, 1, 3),
    }
    arrays = {k: np.ascontiguousarray(v) for k, v in arrays.items()}
    nc = Bacc("TRN2", target_bir_lowering=False, num_devices=1)
    args = {k: nc.dram_tensor(f"in_{k}", v.shape, mybir.dt.from_np(v.dtype), kind="ExternalInput").ap()
            for k, v in arrays.items()}
    out = nc.dram_tensor("out", (NB * L, DM), F32, kind="ExternalOutput").ap()
    program(nc, out=out, **args)
    r = run_bass_kernel_spmd(nc, [{f"in_{k}": v for k, v in arrays.items()}], core_ids=[0])
    return r.results[0]["out"].reshape(NB, L, DM)
```

```python
import numpy as np
import concourse.bass as bass
from concourse import mybir
from concourse.alu_op_type import AluOpType as ALU
from contextlib import ExitStack

F32 = mybir.dt.float32
F32R = mybir.dt.float32r
BF16 = mybir.dt.bfloat16
I32 = mybir.dt.int32
U32 = mybir.dt.uint32
ACT = mybir.ActivationFunctionType
AX = mybir.AxisListType.X

P = 128
DM = 512
KT = DM // P
NB, L = 2, 512
NT = NB * L // P
CH = L // P
EPS = 1e-5
H, HP, NS, G, KC = 64, 64, 128, 8, 4
HG = H // G
GI = HG * HP
CT = GI // P + 2
JB, JC = CT - 2, CT - 1
FF = 1792
FT = FF // P
FP = FT // 2
AH, HD = 32, 16
AT = DM // P
HT = P // HD
NE = 8
STAGES = 4


class Count:

    def __init__(self, sem):
        self.sem, self.n = sem, 0

    def inc(self, instruction):
        self.n += 1
        instruction.then_inc(self.sem, 1)
        return self.n


def program(nc, hidden, w_conv, w_gate, w_dt, conv_w, conv_b, dt_bias, A_log, Dskip, norm_w, w_out,
            ff_gu, ff_dn, gate_s, up_s, down_s, wq, wk, bqk, wv, bv, wo, bo, gate_w, expert_w, out):
    ctx = ExitStack()
    with ctx:

        def sb(name, shape, dt=F32, stack=ctx):
            return stack.enter_context(nc.sbuf_tensor(name, shape, dt))

        def sem(name):
            return ctx.enter_context(nc.semaphore(name))

        banks = ctx.enter_context(nc.psum_tensor("banks", [P, 8, 512], F32))

        def bk(i):
            return banks[:, i, :]

        x = sb("x", [P, NT, DM])
        acc = sb("acc", [P, NT, DM])
        xTh = sb("xTh", [P, KT, NB * L], F32R)
        xTl = sb("xTl", [P, KT, NB * L], F32R)
        ident = sb("ident", [P, P])
        ones = sb("ones", [P, P])
        upto = sb("upto", [P, P])
        after = sb("after", [P, P])
        mhalf = sb("mhalf", [P, NT])
        epsc = sb("epsc", [P, 1])
        stats = sb("stats", [P, NT, 6])
        mv = sb("mv", [P, NT, 2])
        ve = sb("ve", [P, NT])
        rs = sb("rs", [P, NT])

        A = ExitStack()

        def sa(name, shape, dt=F32):
            return sb(name, shape, dt, A)

        wch = sa("wch", [P, KT, CT * P], F32R)
        wcl = sa("wcl", [P, KT, CT * P], F32R)
        wgh = sa("wgh", [P, KT, GI], F32R)
        wgl = sa("wgl", [P, KT, GI], F32R)
        woh = sa("woh", [P, KT, DM], F32R)
        wol = sa("wol", [P, KT, DM], F32R)
        wdth, wdtl = woh[:, :, 0:H], wol[:, :, 0:H]
        par = sa("par", [P, G, CT * KC + CT + KT])
        parg = sa("parg", [P, CT * KC + CT + KT])
        bcast = sa("bcast", [P, 2, H])
        per = sa("per", [P, 5 * NT + 1, H])
        cur = sa("cur", [P, 5 * NT + 1, HG])
        th = sa("th", [P, 2, L])
        xbc = sa("xbc", [P, CT, NB * L])
        xtok = sa("xtok", [P, 2, GI])
        btok = sa("btok", [P, 2, NS])
        gmask = sa("gmask", [P, P])
        am = sa("am", [P, 2, HG, P])
        em = sa("em", [P, 2, HG, P])
        wdt = em[:, 0, :, :].rearrange("p h t -> p (h t)")[:, 0:KT * H].rearrange("p (k h) -> p k h", k=KT)
        z = am[:, :, :, :].rearrange("p a h t -> p (a h t)").rearrange("p (n c) -> p n c", n=4)
        tap = em[:, :, :, :].rearrange("p a h t -> p (a h t)").rearrange("p (n c) -> p n c", n=4)
        dtx = sa("dtx", [P, GI])
        xdec = sa("xdec", [P, GI])
        xd = sa("xd", [P, GI])
        state = sa("state", [P, GI])
        sdec = sa("sdec", [P, GI])
        y = sa("y", [P, GI])
        ss = sa("ss", [P, 2])
        ssv = sa("ssv", [P, 2])
        rg = sa("rg", [P, 2])
        tg = sa("tg", [P, GI])
        yn = sa("yn", [P, 2, GI])
        sg = th
        ynTh = sa("ynTh", [P, GI], F32R)
        ynTl = sa("ynTl", [P, GI], F32R)
        A.close()

        B = ExitStack()

        def sf(name, shape, dt=F32):
            return sb(name, shape, dt, B)

        gur = sf("gur", [P, KT, 2, 2, P], I32)
        dnr = sf("dnr", [P, 2, DM], I32)
        gu = sf("gu", [P, KT, 2, 2, P], F32R)
        dn = sf("dn", [P, 2, DM], F32R)
        gus = sf("gus", [P, 2, FT])
        fsc = sf("fsc", [P, 2, FT])
        fscg = sf("fscg", [P, 2, 2])
        dsb = sf("dsb", [P, DM])
        fth = sf("fth", [P, 2, L])
        fh = sf("fh", [P, 2, L])
        hidf = sf("hidf", [P, 2, L])
        hidh = sf("hidh", [P, 2, NB * L], F32R)
        hidl = sf("hidl", [P, 2, NB * L], F32R)
        B.close()

        C = ExitStack()

        def sc(name, shape, dt=F32):
            return sb(name, shape, dt, C)

        qs = sc("qs", [P, 2, 4, L], F32R)
        ks = sc("ks", [P, 2, 4, L], F32R)
        prob = sc("prob", [P, 2, 2, L])
        pTh = sc("pTh", [P, 2, 2, L], F32R)
        pTl = sc("pTl", [P, 2, 2, L], F32R)
        attTh, attTl = pTh[:, :, 0, :], pTl[:, :, 0, :]
        att = acc
        awr = prob[:, :, :, :].rearrange("p a b l -> p (a b) l")
        qf = sc("qf", [P, 2, L])
        qh = sc("qh", [P, 2, L], F32R)
        ql = sc("ql", [P, 2, L], F32R)
        v = sc("v", [P, NT, AH, 2, HD], F32R)
        fold = sc("fold", [P, 2, HD])
        sel = sc("sel", [P, 4, P], F32R)
        identb = sc("identb", [P, P], BF16)
        future = sc("future", [P, P], BF16)
        futf = sc("futf", [P, P])
        nmax = sc("nmax", [P, 2, 2])
        psum = sc("psum", [P, 2, HT])
        prec = sc("prec", [P, HT])
        osum = sc("osum", [P, HT, HD])
        abqk = sc("abqk", [P, 2, AT])
        abg = sc("abg", [P, 2])
        abv = sc("abv", [P, DM])
        abo = sc("abo", [P, DM])
        awh = sc("awh", [P, KT, DM], F32R)
        awl = sc("awl", [P, KT, DM], F32R)
        aqr = sc("aqr", [P, 2, KT, P])
        aqh = sc("aqh", [P, 2, KT, P], F32R)
        aql = sc("aql", [P, 2, KT, P], F32R)
        C.close()

        D = ExitStack()

        def sd(name, shape, dt=F32):
            return sb(name, shape, dt, D)

        ew = sd("ew", [P, 2, KT, DM])
        rw = sd("rw", [P, KT, NE])
        rwh = sd("rwh", [P, KT, NE], F32R)
        rwl = sd("rwl", [P, KT, NE], F32R)
        ewh = sd("ewh", [P, 2, KT, DM], F32R)
        ewl = sd("ewl", [P, 2, KT, DM], F32R)
        lg = sd("lg", [P, NT, NE])
        top = sd("top", [P, NT, NE])
        topi = sd("topi", [P, NT, NE], U32)
        topf = sd("topf", [P, NT, NE])
        which = sd("which", [P, NE])
        rt = sd("rt", [P, 4, NT])
        oh = sd("oh", [P, 2, NT, NE])
        we = sd("we", [P, NT, NE])
        D.close()

        x_in = sem("x_in")
        small_in = sem("small_in")
        wc_in, wg_in, wo_in, x_again = (sem(s) for s in ("wc_in", "wg_in", "wo_in", "x_again"))
        wc_hi, wc_lo, wg_hi, wg_lo, wo_hi, wo_lo, wo_scaled, wdt_hi, wdt_lo = (sem(s) for s in (
            "wc_hi", "wc_lo", "wg_hi", "wg_lo", "wo_hi", "wo_lo", "wo_scaled", "wdt_hi", "wdt_lo"))
        ynT_lo = sem("ynT_lo")
        consts = sem("consts")
        nsem = {w: sem(f"norm_{w}") for w in ("dve", "var", "rstd", "xn", "tr", "hi", "lo")}
        dt_ps, dt_dve, dt_act, dt_cum = sem("dt_ps"), sem("dt_dve"), sem("dt_act"), sem("dt_cum")
        par_ready, cur_ready = sem("par_ready"), sem("cur_ready")
        acc_clear = sem("acc_clear")
        h_ready, tap0, taps, tanh_done, tanh_ready, xbc_ready = (sem(s) for s in ("h_ready", "tap0", "taps", "tanh_done", "tanh_ready", "xbc_ready"))
        x_tr, tp_out, gb_ready, gb_used, d_ready, e_ready = (sem(s) for s in ("x_tr", "tp_out", "gb_ready", "gb_used", "d_ready", "e_ready"))
        am_ready, xd_ready, xdec_ready, dtx_ready, sdec_ready = (sem(s) for s in ("am_ready", "xd_ready", "xdec_ready", "dtx_ready", "sdec_ready"))
        m_ready, yo_ready, yo_used, yi_ready, y_part, y_ready = (sem(s) for s in ("m_ready", "yo_ready", "yo_used", "yi_ready", "y_part", "y_ready"))
        st_ready, state_ready, ss_ready, ssv_ready, rg_ready = (sem(s) for s in ("st_ready", "state_ready", "ss_ready", "ssv_ready", "rg_ready"))
        gate_ready, tg_ready, gate_used, yn_ready, yn_tr, o_ready, out_added = (sem(s) for s in ("gate_ready", "tg_ready", "gate_used", "yn_ready", "yn_tr", "o_ready", "out_added"))

        gu_in, dn_in, gu_cast, dn_cast, f_small, f_dve, f_clear, fsc_ready = (sem(s) for s in ("gu_in", "dn_in", "gu_cast", "dn_cast", "f_small", "f_dve", "f_clear", "fsc_ready"))
        hid_f, hid_hi = sem("hid_f"), sem("hid_hi")
        gate_ps, up_ps, f_tanh, f_part, hid_ready, down_ps, down_added = (sem(s) for s in ("gate_ps", "up_ps", "f_tanh", "f_part", "hid_ready", "down_ps", "down_added"))

        a_small, aq_in, awr_in, v_ps, v_f, v_hi, v_ready, sel_ready = (sem(s) for s in (
            "a_small", "aq_in", "awr_in", "v_ps", "v_f", "v_hi", "v_ready", "sel_ready"))
        osum_ready = sem("osum_ready")
        aw_hi, aw_lo, aq_hi, aq_lo = (sem(s) for s in ("aw_hi", "aw_lo", "aq_hi", "aq_lo"))
        qk_ps, qk_f, qk_h, qk_l, st_ps, st_out = (sem(s) for s in ("qk_ps", "qk_f", "qk_h", "qk_l", "st_ps", "st_out"))
        st_out2, qb_scaled, bias_ready = sem("st_out2"), sem("qb_scaled"), sem("bias_ready")
        s_ready, max_ready, exp_ready, pt_ps, pt_hi, pt_lo, pv_ps, prec_ready, att_ready = (sem(s) for s in (
            "s_ready", "max_ready", "exp_ready", "pt_ps", "pt_hi", "pt_lo", "pv_ps", "prec_ready", "att_ready"))
        at_ps, at_hi, at_lo, ao_ps, ao_ready = (sem(s) for s in ("at_ps", "at_hi", "at_lo", "ao_ps", "ao_ready"))

        r_in, lg_ps, r_dve, r_act, r_iota, d_clear, ex_ps, ex_added = (sem(s) for s in ("r_in", "lg_ps", "r_dve", "r_act", "r_iota", "d_clear", "ex_ps", "ex_added"))
        ew_in = [sem("ew_in0"), sem("ew_in1")]
        e_hi, e_lo, rw_hi, rw_lo = (sem(s) for s in ("e_hi", "e_lo", "rw_hi", "rw_lo"))
        stored = sem("stored")

        block = ctx.enter_context(nc.Block())

        def block_done(eng, q):
            if q == 1:
                eng.wait_ge(out_added, 1 + G * NT)
            elif q == 2:
                eng.wait_ge(f_dve, 1 + NT)
            elif q == 3:
                eng.wait_ge(ao_ready, NT)
            elif q == 4:
                eng.wait_ge(ex_added, NT + NE * NT)

        def norm_wait(eng, q, what, n):
            eng.wait_ge(nsem[what], (max(2 * q - 1, 0) if what in ("var", "rstd") else NT * q) + n)

        norm_steps = Count(nsem["dve"])

        def conv_stage(group):
            t = xbc[:, :, :].rearrange("p a b -> p (a b)") if group == 0 else x[:, :, :].rearrange("p a b -> p (a b)")
            return t[:, 0:KT * CT * P].rearrange("p (k c) -> p k c", k=KT)

        gate_stage, out_stage = x[:, 0:KT, :], x[:, KT:2 * KT, :]

        def pair(ap):
            return ap.rearrange("p (h c) -> p h c", h=HG)

        def products(o, terms, first=True, last=True):
            terms = [t for ah, al, bh, bl in terms for t in ((ah, bh), (ah, bl), (al, bh))]
            for n, (a, b) in enumerate(terms):
                m = nc.tensor.matmul(o, a, b, start=first and n == 0, stop=last and n == len(terms) - 1)
            return m

        def low(eng, o, full, high):
            return eng.tensor_tensor(o, full, high.bitcast(F32), ALU.subtract)

        def hid_part(t, q):
            return t[:, q % 2, q // 2 * L:(q // 2 + 1) * L]

        CB = (0, 1, 6, 7)

        UNITS = 16 * NB
        PREP = {s + 1: s for s in range(10)}

        def stacked(b, n):
            return (qs, ks)[n // 4][:, b, n % 4, :]

        def passes_ahead(t, s, last):
            piece = PREP.get(s % 16) if s < UNITS else None
            if piece is None or (last and s >= 16):
                return None
            return ((t, 1) if s < 16 else (t + 1, 0)) + (piece,)

        def evacuation(s):
            return 2 * s - 1 if s < NT else 2 * NT - 2 + (s - NT)

        def heads(row):
            return cur[:, row, :].unsqueeze(2).to_broadcast([P, HG, HP])

        @block.sync
        def _(sp):
            for i in range(NT):
                sp.dma_start(x[:, i, :], hidden[i * P:(i + 1) * P, :]).then_inc(x_in, 16)
            sp.dma_start(wdt[:, :, :], w_dt).then_inc(small_in, 16)
            sp.dma_start(bcast[:, 0, :], dt_bias.partition_broadcast(P)).then_inc(small_in, 16)
            sp.dma_start(bcast[:, 1, :], A_log.partition_broadcast(P)).then_inc(small_in, 16)
            sp.dma_start(per[:, 5 * NT, :], Dskip.partition_broadcast(P)).then_inc(small_in, 16)
            sp.dma_start(par[:, :, 0:CT * KC], conv_w).then_inc(small_in, 16)
            sp.dma_start(par[:, :, CT * KC:CT * KC + CT], conv_b).then_inc(small_in, 16)
            sp.dma_start(par[:, :, CT * KC + CT:], norm_w).then_inc(small_in, 16)
            sp.dma_start(conv_stage(0), w_conv[0]).then_inc(wc_in, 16)
            norm_wait(sp, 0, "xn", NT)
            sp.dma_start(gate_stage, w_gate[0]).then_inc(wg_in, 16)
            sp.dma_start(out_stage, w_out[0]).then_inc(wo_in, 16)
            with sp.Fori(0, G - 1) as g:
                sp.wait_ge(wg_lo, KT * g + KT)
                sp.wait_ge(wo_lo, KT * g + KT)
                sp.dma_start(conv_stage(1), w_conv[bass.ds(g + 1, 1)]).then_inc(wc_in, 16)
                sp.wait_ge(wc_lo, KT * g + 2 * KT)
                sp.dma_start(gate_stage, w_gate[bass.ds(g + 1, 1)]).then_inc(wg_in, 16)
                sp.dma_start(out_stage, w_out[bass.ds(g + 1, 1)]).then_inc(wo_in, 16)
            sp.wait_ge(wg_lo, KT * G)
            sp.wait_ge(wo_lo, KT * G)
            for i in range(NT):
                sp.dma_start(x[:, i, :], hidden[i * P:(i + 1) * P, :]).then_inc(x_again, 16)
            if STAGES >= 2:
                sp.wait_ge(h_ready, NB * CT * G)
                sp.dma_start(gur[:, :, :, :, :], ff_gu[0]).then_inc(gu_in, 16)
                sp.dma_start(dnr[:, :, :], ff_dn[0]).then_inc(dn_in, 16)
                block_done(sp, 1)
                sp.dma_start(gus[:, 0, :], gate_s).then_inc(f_small, 16)
                sp.dma_start(gus[:, 1, :], up_s).then_inc(f_small, 16)
                sp.dma_start(dsb[:, :], down_s.partition_broadcast(P)).then_inc(f_small, 16)
                with sp.Fori(0, FP - 1) as f:
                    sp.wait_ge(gu_cast, KT * f + KT)
                    sp.dma_start(gur[:, :, :, :, :], ff_gu[bass.ds(f + 1, 1)]).then_inc(gu_in, 16)
                    sp.wait_ge(dn_cast, 2 * f + 2)
                    sp.dma_start(dnr[:, :, :], ff_dn[bass.ds(f + 1, 1)]).then_inc(dn_in, 16)
            if STAGES >= 3:
                sp.wait_ge(down_ps, NT * FP)
                sp.dma_start(awr, wv).then_inc(awr_in, 16)
                sp.dma_start(aqr[:, 0, :, :], wq[0]).then_inc(aq_in, 16)
                sp.dma_start(aqr[:, 1, :, :], wk[0]).then_inc(aq_in, 16)
                sp.dma_start(abqk[:, :, :], bqk).then_inc(a_small, 16)
                sp.dma_start(abv[:, :], bv.partition_broadcast(P)).then_inc(a_small, 16)
                sp.dma_start(abo[:, :], bo.partition_broadcast(P)).then_inc(a_small, 16)
                sp.wait_ge(aw_lo, KT)
                sp.dma_start(awr, wo).then_inc(awr_in, 16)
                with sp.Fori(0, AT - 1) as t:
                    sp.wait_ge(aq_lo, 2 * t + 2)
                    sp.dma_start(aqr[:, 0, :, :], wq[bass.ds(t + 1, 1)]).then_inc(aq_in, 16)
                    sp.dma_start(aqr[:, 1, :, :], wk[bass.ds(t + 1, 1)]).then_inc(aq_in, 16)
            if STAGES >= 4:
                sp.wait_ge(s_ready, 16 * NB * AT)
                sp.dma_start(rw[:, :, :], gate_w).then_inc(r_in, 16)
                sp.dma_start(ew[:, 0, :, :], expert_w[0]).then_inc(ew_in[0], 16)
                sp.dma_start(ew[:, 1, :, :], expert_w[1]).then_inc(ew_in[1], 16)
                with sp.Fori(0, NE // 2 - 1) as e:
                    for s in range(2):
                        sp.wait_ge(e_lo, 2 * KT * e + KT * (s + 1))
                        sp.dma_start(ew[:, s, :, :], expert_w[bass.ds(2 * e + 2 + s, 1)]).then_inc(ew_in[s], 16)
            for i in range(NT):
                norm_wait(sp, STAGES, "xn", i + 1)
                sp.dma_start(out[i * P:(i + 1) * P, :], x[:, i, :]).then_inc(stored, 16)
            sp.wait_ge(stored, 16 * NT)

        def norm_vector(q):
            d = norm_steps

            def moments(src):
                for i in range(NT):
                    at = d.inc(nc.vector.bn_stats(stats[:, i, :], src[:, i, :]))
                nc.vector.wait_ge(d.sem, at)
                for i in range(NT):
                    at = d.inc(nc.vector.bn_aggr(mv[:, i, :], stats[:, i, :]))
                nc.vector.wait_ge(d.sem, at)
                nc.vector.tensor_scalar(ve[:, :], mv[:, :, 1], EPS, None, ALU.add).then_inc(nsem["var"], 1)

            if q > 0:
                block_done(nc.vector, q)
                moments(acc)
                if q == 1:
                    nc.vector.wait_ge(x_again, 16 * NT)
                norm_wait(nc.vector, q, "rstd", 1)
                for i in range(NT):
                    at = d.inc(nc.vector.tensor_scalar(acc[:, i, :], acc[:, i, :], mv[:, i, 0:1], rs[:, i:i + 1],
                                                       ALU.subtract, ALU.mult))
                    nc.vector.wait_ge(d.sem, at)
                    ins = nc.vector.tensor_tensor(x[:, i, :], x[:, i, :], acc[:, i, :], ALU.add)
                    if q == STAGES:
                        ins.then_inc(nsem["xn"], 1)
                    else:
                        at = d.inc(ins)
                nc.vector.wait_ge(d.sem, d.n)
            else:
                nc.vector.wait_ge(x_in, 16 * NT)
            if q < STAGES:
                moments(x)
                norm_wait(nc.vector, q, "rstd", 2 if q else 1)
                for i in range(NT + 1):
                    if i < NT:
                        nc.vector.tensor_scalar(acc[:, i, :], x[:, i, :], mv[:, i, 0:1], rs[:, i:i + 1],
                                                ALU.subtract, ALU.mult).then_inc(nsem["xn"], 1)
                    if i >= 1:
                        norm_wait(nc.vector, q, "hi", i)
                        low(nc.vector, xTl[:, :, (i - 1) * P:i * P], bk((i - 1) % 2).rearrange("p (k t) -> p k t", k=KT),
                            xTh[:, :, (i - 1) * P:i * P]).then_inc(nsem["lo"], 1)

        def norm_pool(q):
            for r in range((q > 0) + (q < STAGES)):
                norm_wait(nc.gpsimd, q, "var", r + 1)
                nc.gpsimd.tensor_tensor(rs[:, :], ve[:, :], mhalf[:, :], ALU.pow).then_inc(nsem["rstd"], 1)

        def norm_tensor(q):
            for i in range(NT):
                norm_wait(nc.tensor, q, "xn", i + 1)
                if i >= 2:
                    norm_wait(nc.tensor, q, "lo", i - 1)
                for k in range(KT):
                    mmi = nc.tensor.transpose(bk(i % 2)[:, k * P:(k + 1) * P], acc[:, i, k * P:(k + 1) * P], ident[:, :])
                mmi.then_inc(nsem["tr"], 1)

        def norm_scalar(q):
            for i in range(NT):
                norm_wait(nc.scalar, q, "tr", i + 1)
                nc.scalar.copy(xTh[:, :, i * P:(i + 1) * P],
                               bk(i % 2).rearrange("p (k t) -> p k t", k=KT)).then_inc(nsem["hi"], 1)

        @block.gpsimd
        def _(pool):
            pool.memset(ones[:, :], 1.0).then_inc(consts, 1)
            pool.memset(mhalf[:, :], -0.5).then_inc(consts, 1)
            pool.memset(epsc[:, :], EPS).then_inc(consts, 1)
            pool.wait_ge(consts, 3)
            pool.affine_select(out=ident[:, :], in_=ones[:, :], compare_op=ALU.is_equal, fill=0.0, base=0,
                               pattern=[[-1, P]], channel_multiplier=1).then_inc(consts, 1)
            pool.affine_select(out=upto[:, :], in_=ones[:, :], compare_op=ALU.is_ge, fill=0.0, base=0,
                               pattern=[[1, P]], channel_multiplier=-1).then_inc(consts, 1)
            pool.affine_select(out=after[:, :], in_=ones[:, :], compare_op=ALU.is_gt, fill=0.0, base=0,
                               pattern=[[-1, P]], channel_multiplier=1).then_inc(consts, 1)
            norm_pool(0)
            pool.sem_inc(xbc_ready, 4)

            def decays(i):
                pool.tensor_tensor(am[:, i % 2, :, :], cur[:, i, :].unsqueeze(2).to_broadcast([P, HG, P]),
                                   upto[:, :].unsqueeze(1).to_broadcast([P, HG, P]), ALU.mult).then_inc(am_ready, 1)

            pool.wait_ge(consts, 6)
            for k in range(KT):
                pool.wait_ge(wc_hi, k + 1)
                low(pool, wcl[:, k, :], conv_stage(0)[:, k, :], wch[:, k, :]).then_inc(wc_lo, 1)
            norm_wait(pool, 0, "tr", NT)
            pool.memset(acc[:, :, :], 0.0).then_inc(acc_clear, 1)

            def group(g, last):
                pool.wait_ge(cur_ready, g + 1)
                decays(0)
                for q in range(NB * CT):
                    b, j = q // CT, q % CT
                    pool.wait_ge(tanh_ready, NB * CT * g + q + 1)
                    pool.tensor_tensor(xbc[:, j, b * L:(b + 1) * L], th[:, q % 2, :], tap[:, q % 4, :],
                                       ALU.mult).then_inc(xbc_ready, 1)
                    if q < KT:
                        pool.wait_ge(wg_hi, KT * g + q + 1)
                        low(pool, wgl[:, q, :], gate_stage[:, q, :], wgh[:, q, :]).then_inc(wg_lo, 1)
                    elif q < 2 * KT:
                        k = q - KT
                        pool.wait_ge(wo_hi, KT * g + k + 1)
                        low(pool, wol[:, k, :], out_stage[:, k, :], woh[:, k, :]).then_inc(wo_lo, 1)
                for s in range(NT + 1):
                    i, c = s - 1, (s - 1) % CH
                    if s >= 1 and 1 <= c < CH - 1:
                        pool.wait_ge(state_ready, (CH - 1) * NB * g + (CH - 1) * (i // CH) + c)
                        pool.tensor_tensor(pair(sdec[:, :]), pair(state[:, :]), heads(4 * NT + i),
                                           ALU.mult).then_inc(sdec_ready, 1)
                    if s < NT:
                        pool.wait_ge(tp_out, 2 * NT * g + (s if s < 2 else 2 * s - 2) + 2)
                        src = pair(xtok[:, s % 2, :])
                        if s + 1 < NT:
                            decays(s + 1)
                        if s >= 1:
                            pool.wait_ge(yi_ready, NT * g + s)
                        pool.tensor_tensor(pair(dtx[:, :]), src, heads(NT + s), ALU.mult).then_inc(dtx_ready, 1)
                        if s % CH < CH - 1:
                            m = (CH - 1) * NB * g + (CH - 1) * (s // CH) + s % CH
                            if s % CH:
                                pool.wait_ge(st_ready, m)
                            pool.tensor_tensor(pair(xdec[:, :]), src, heads(3 * NT + s), ALU.mult).then_inc(xdec_ready, 1)
                        if s >= 1:
                            pool.wait_ge(y_ready, NT * g + s + 1)
                        pool.tensor_tensor(pair(xd[:, :]), src, heads(5 * NT), ALU.mult).then_inc(xd_ready, 1)
                    if s >= 1:
                        pool.wait_ge(ss_ready, NT * g + i + 1)
                        pool.tensor_tensor(ssv[:, i % 2:i % 2 + 1], ss[:, i % 2:i % 2 + 1], epsc[:, :],
                                           ALU.add).then_inc(ssv_ready, 1)
                        pool.wait_ge(ssv_ready, NT * g + i + 1)
                        pool.tensor_tensor(rg[:, i % 2:i % 2 + 1], ssv[:, i % 2:i % 2 + 1], mhalf[:, 0:1],
                                           ALU.pow).then_inc(rg_ready, 1)
                    if 1 <= s <= KT and not last:
                        pool.wait_ge(wc_hi, KT * g + KT + s)
                        low(pool, wcl[:, s - 1, :], conv_stage(1)[:, s - 1, :], wch[:, s - 1, :]).then_inc(wc_lo, 1)

            with pool.Fori(0, G - 1) as g:
                group(g, False)
            group(G - 1, True)
            norm_pool(1)
            if STAGES >= 2:
                norm_wait(pool, 1, "tr", NT)
                pool.memset(acc[:, :, :], 0.0).then_inc(f_clear, 1)
                norm_pool(2)
            if STAGES >= 3:
                pool.memset(futf[:, :], 0.0).then_inc(sel_ready, 1)
                pool.wait_ge(sel_ready, 1)
                pool.affine_select(out=futf[:, :], in_=futf[:, :], compare_op=ALU.is_ge, fill=-1e30, base=0,
                                   pattern=[[-1, P]], channel_multiplier=1).then_inc(sel_ready, 1)
                for k in range(KT):
                    pool.wait_ge(aw_hi, k + 1)
                    low(pool, awl[:, k, :], awr[:, k, :], awh[:, k, :]).then_inc(aw_lo, 1)
                for t in range(AT):
                    for w in range(2):
                        pool.wait_ge(aq_hi, 2 * t + w + 1)
                        low(pool, aql[:, w, :, :], aqr[:, w, :, :], aqh[:, w, :, :]).then_inc(aq_lo, 1)
                    if t == 0:
                        for k in range(KT):
                            pool.wait_ge(aw_hi, KT + k + 1)
                            low(pool, awl[:, k, :], awr[:, k, :], awh[:, k, :]).then_inc(aw_lo, 1)
                norm_pool(3)
            if STAGES >= 4:
                norm_wait(pool, 3, "tr", NT)
                pool.wait_ge(rw_hi, 1)
                low(pool, rwl[:, :, :], rw[:, :, :], rwh[:, :, :]).then_inc(rw_lo, 1)
                pool.iota(which[:, :], pattern=[[1, NE]], base=0, channel_multiplier=0,
                          allow_small_or_imprecise_dtypes=True).then_inc(r_iota, 1)
                pool.memset(acc[:, :, :], 0.0).then_inc(d_clear, 1)
                with pool.Fori(0, NE // 2) as e:
                    for s in range(2):
                        for k in range(KT):
                            pool.wait_ge(e_hi, 2 * KT * e + KT * s + k + 1)
                            low(pool, ewl[:, s, k, :], ew[:, s, k, :], ewh[:, s, k, :]).then_inc(e_lo, 1)
                norm_pool(4)

        @block.scalar
        def _(act):
            act.sem_inc(tp_out, 1)
            act.sem_inc(e_ready, 1)
            act.wait_ge(wc_in, 16)
            for k in range(KT):
                nc.scalar.copy(wch[:, k, :], conv_stage(0)[:, k, :]).then_inc(wc_hi, 1)
            act.wait_ge(small_in, 16 * 7)
            nc.scalar.copy(wdth, wdt).then_inc(wdt_hi, 1)
            norm_scalar(0)
            act.wait_ge(dt_dve, 2)
            nc.scalar.activation(z[:, 2, :], z[:, 1, :], ACT.Exp).then_inc(dt_act, 1)
            nc.scalar.activation(bcast[:, 1, :], bcast[:, 1, :], ACT.Exp).then_inc(dt_act, 1)
            act.wait_ge(dt_act, 1)
            nc.scalar.activation(z[:, 1, :], z[:, 2, :], ACT.Ln, bias=1.0).then_inc(dt_act, 1)
            for n, row in enumerate((2, 3, 4)):
                act.wait_ge(dt_cum, n + 1)
                nc.scalar.activation(per[:, row * NT:(row + 1) * NT, :],
                                     bk(n).rearrange("p (c h) -> p c h", c=NT), ACT.Exp).then_inc(dt_act, 1)

            def group(g, last):
                act.wait_ge(par_ready, g + 1)
                for q in range(NB * CT + 1):
                    j = q % CT
                    if q < NB * CT:
                        act.wait_ge(h_ready, NB * CT * g + q + 1)
                        act.wait_ge(xbc_ready, NB * CT * g + q + 1)
                        nc.scalar.activation(tap[:, q % 4, :], bk(CB[q % 4]), ACT.Identity,
                                             bias=parg[:, CT * KC + j:CT * KC + j + 1],
                                             scale=parg[:, KC * j + KC - 1:KC * j + KC]).then_inc(tap0, 1)
                    if q >= 1:
                        act.wait_ge(taps, 3 * (NB * CT) * g + 3 * q)
                        act.wait_ge(xbc_ready, NB * CT * g + q + 2)
                        nc.scalar.activation(th[:, (q - 1) % 2, :], tap[:, (q - 1) % 4, :],
                                             ACT.Tanh).then_inc(tanh_done, 1)
                        act.wait_ge(tanh_done, NB * CT * g + q)
                        nc.scalar.activation(th[:, (q - 1) % 2, :], th[:, (q - 1) % 2, :], ACT.Copy,
                                             bias=1.0).then_inc(tanh_ready, 1)
                    k = q - 1
                    if 0 <= k < KT:
                        act.wait_ge(wg_in, 16 * g + 16)
                        nc.scalar.copy(wgh[:, k, :], gate_stage[:, k, :]).then_inc(wg_hi, 1)
                        act.wait_ge(wo_in, 16 * g + 16)
                        nc.scalar.activation(out_stage[:, k, :], out_stage[:, k, :], ACT.Copy,
                                             scale=parg[:, CT * KC + CT + k:CT * KC + CT + k + 1]).then_inc(wo_scaled, 1)
                    k = q - 1 - KT
                    if 0 <= k < KT:
                        act.wait_ge(wo_scaled, KT * g + k + 1)
                        nc.scalar.copy(woh[:, k, :], out_stage[:, k, :]).then_inc(wo_hi, 1)
                for s in range(NT + 2):
                    if s < NT:
                        act.wait_ge(x_tr, NT * g + s + 1)
                        nc.scalar.copy(xtok[:, s % 2, :], bk(4)).then_inc(tp_out, 1)
                        if s == 0:
                            act.wait_ge(xbc_ready, NB * CT * g + NB * CT + 4)
                        act.wait_ge(d_ready, NT * g + s + 1)
                        nc.scalar.activation(em[:, s % 2, :, :], banks[:, 2:4, :].rearrange("p b (h t) -> p (b h) t", t=P),
                                             ACT.Exp).then_inc(e_ready, 1)
                    if 1 <= s <= NT:
                        act.wait_ge(y_ready, NT * g + s + 1)
                        nc.scalar.activation(tg[:, :], y[:, :], ACT.Square, scale=float(GI) ** -0.5,
                                             accum_out=ss[:, (s - 1) % 2:(s - 1) % 2 + 1]).then_inc(ss_ready, 1)
                    if s >= 2:
                        act.wait_ge(yn_tr, NT * g + s - 1)
                        nc.scalar.copy(ynTh[:, :], bk(4)).then_inc(tp_out, 1)
                    if s < NT:
                        if s >= 1:
                            act.wait_ge(ss_ready, NT * g + s)
                        act.wait_ge(gate_ready, NT * g + s + 1)
                        nc.scalar.activation(tg[:, :], bk(0), ACT.Tanh, scale=0.5).then_inc(tg_ready, 1)
                    if 1 <= s <= KT and not last:
                        act.wait_ge(wc_in, 16 * g + 32)
                        nc.scalar.copy(wch[:, s - 1, :], conv_stage(1)[:, s - 1, :]).then_inc(wc_hi, 1)

            with act.Fori(0, G - 1) as g:
                group(g, False)
            group(G - 1, True)
            norm_scalar(1) if STAGES >= 2 else None
            if STAGES >= 2:
                def hidden_pair(f):
                    act.wait_ge(up_ps, 4 * f + 1)
                    act.wait_ge(gu_in, 16 * f + 16)
                    for k in range(KT):
                        nc.scalar.copy(gu[:, k, :, :, :], gur[:, k, :, :, :]).then_inc(gu_cast, 1)
                    act.wait_ge(fsc_ready, f + 1)
                    for q in range(4):
                        act.wait_ge(gate_ps, 4 * f + q + 1)
                        nc.scalar.activation(fth[:, q % 2, :], bk(q % 2), ACT.Tanh,
                                             scale=fscg[:, 0, q % 2:q % 2 + 1]).then_inc(f_tanh, 1)
                        if q == 2:
                            act.wait_ge(dn_in, 16 * f + 16)
                            for k in range(2):
                                nc.scalar.copy(dn[:, k, :], dnr[:, k, :]).then_inc(dn_cast, 1)
                        if q % 2:
                            for r in (q - 1, q):
                                act.wait_ge(hid_f, 4 * f + r + 1)
                                nc.scalar.copy(hid_part(hidh, r), hidf[:, r % 2, :]).then_inc(hid_hi, 1)

                with act.Fori(0, FP) as f:
                    hidden_pair(f)
            if STAGES >= 3:
                def weights(t):
                    act.wait_ge(qk_ps, 4 * t) if not isinstance(t, int) else None
                    act.wait_ge(aq_in, 32 * t + 32)
                    for w in range(2):
                        nc.scalar.copy(aqh[:, w, :, :], aqr[:, w, :, :]).then_inc(aq_hi, 1)

                act.wait_ge(awr_in, 16)
                for k in range(KT):
                    nc.scalar.copy(awh[:, k, :], awr[:, k, :]).then_inc(aw_hi, 1)
                weights(0)
                norm_scalar(2)
                for i in range(NT):
                    act.wait_ge(v_f, i + 1)
                    nc.scalar.copy(v[:, i, :, 0, :], qf[:, i % 2, :].rearrange("p (h d) -> p h d", d=HD)).then_inc(v_hi, 1)
                act.wait_ge(v_ps, NT)
                act.wait_ge(awr_in, 32)
                for k in range(KT):
                    nc.scalar.copy(awh[:, k, :], awr[:, k, :]).then_inc(aw_hi, 1)

                def prepare(t, b, piece):
                    m = NB * t + b
                    if piece < 2:
                        if piece == 0:
                            act.wait_ge(bias_ready, t + 1)
                        act.wait_ge(qk_ps, 2 * m + piece + 1)
                        nc.scalar.activation(qf[:, piece, :], bk(7), ACT.Identity, bias=abg[:, piece:piece + 1],
                                             scale=HD ** -0.5 if piece == 0 else 1.0).then_inc(qk_f, 1)
                    elif piece % 2 == 0:
                        act.wait_ge(st_ps, 8 * m + piece - 1)
                        nc.scalar.copy(stacked(b, piece - 2), bk(7)).then_inc(st_out, 1)

                def tile(t, last):
                    for s in range(UNITS + 2):
                        w = s - 2
                        if w >= 0:
                            kw = (w % 16 // 4 + 1) * P
                            for j in range(2):
                                act.wait_ge(pt_ps, 2 * UNITS * t + 2 * w + j + 1)
                                nc.scalar.copy(pTh[:, w % 2, j, 0:kw], bk(4 + j)[:, 0:kw]).then_inc(pt_hi, 1)
                        if s < UNITS:
                            gq, qi = s // 4, s % 16 // 4
                            kw = (qi + 1) * P
                            act.wait_ge(max_ready, UNITS * t + s + 1)
                            if s % 4 == 0:
                                act.wait_ge(prec_ready, 8 * t + gq + 1)
                            for j in range(2):
                                e = nc.scalar.activation(prob[:, s % 2, j, 0:kw], bk(2 * (s % 2) + j)[:, 0:kw], ACT.Exp,
                                                         bias=nmax[:, s % 2, j:j + 1],
                                                         accum_out=psum[:, gq % 2, 2 * (s % 4) + j:2 * (s % 4) + j + 1])
                            e.then_inc(exp_ready, 1)
                        ahead = passes_ahead(t, s, last)
                        if ahead:
                            prepare(*ahead)
                        if s == 6 and not last:
                            weights(t + 1)

                for piece in range(10):
                    prepare(0, 0, piece)
                act.wait_ge(aw_lo, 2 * KT)
                with act.Fori(0, AT - 1) as t:
                    tile(t, False)
                tile(AT - 1, True)
                for i in range(NT):
                    act.wait_ge(at_ps, i + 1)
                    nc.scalar.copy(attTh[:, i % 2, :], bk(i % 2)).then_inc(at_hi, 1)
            if STAGES >= 4:
                act.wait_ge(r_in, 16)
                nc.scalar.copy(rwh[:, :, :], rw[:, :, :]).then_inc(rw_hi, 1)
                for s in range(2):
                    act.wait_ge(ew_in[s], 16)
                    for k in range(KT):
                        nc.scalar.copy(ewh[:, s, k, :], ew[:, s, k, :]).then_inc(e_hi, 1)
                norm_scalar(3)
                act.wait_ge(r_dve, 2 + 2 * NT)
                nc.scalar.activation(rt[:, 1, :], rt[:, 0, :], ACT.Exp).then_inc(r_act, 1)
                with act.Fori(0, NE // 2 - 1) as e:
                    for s in range(2):
                        act.wait_ge(ex_ps, 2 * NT * e + NT * (s + 1))
                        act.wait_ge(ew_in[s], 16 * e + 32)
                        for k in range(KT):
                            nc.scalar.copy(ewh[:, s, k, :], ew[:, s, k, :]).then_inc(e_hi, 1)

        @block.vector
        def _(dve):
            dve.sem_inc(gb_used, 1)
            dve.sem_inc(yo_used, 1)
            dve.sem_inc(y_ready, 1)
            dve.sem_inc(gate_used, 1)
            dve.sem_inc(out_added, 1)
            dve.sem_inc(ynT_lo, 1)
            norm_vector(0)
            dve.wait_ge(wdt_hi, 1)
            low(nc.vector, wdtl, wdt, wdth).then_inc(wdt_lo, 1)
            dve.wait_ge(dt_ps, 1)
            dve.wait_ge(small_in, 16 * 7)
            d = Count(dt_dve)

            def chain(ins):
                d.inc(ins)
                dve.wait_ge(dt_dve, d.n)

            chain(nc.vector.tensor_tensor(z[:, 0, :].rearrange("p (c h) -> p c h", c=NT),
                                          bk(0).rearrange("p (c h) -> p c h", c=NT),
                                          bcast[:, 0, :].unsqueeze(1).to_broadcast([P, NT, H]), ALU.add))
            chain(nc.vector.scalar_tensor_tensor(z[:, 1, :], z[:, 0, :], -1.0, z[:, 0, :], ALU.mult, ALU.min))
            dve.wait_ge(dt_act, 3)
            chain(nc.vector.tensor_scalar(z[:, 3, :], z[:, 2, :], 1.0, None, ALU.add))
            chain(nc.vector.tensor_scalar(z[:, 3, :], z[:, 3, :], -1.0, None, ALU.add))
            chain(nc.vector.tensor_tensor(z[:, 3, :], z[:, 2, :], z[:, 3, :], ALU.subtract))
            chain(nc.vector.tensor_tensor(z[:, 3, :], z[:, 1, :], z[:, 3, :], ALU.add))
            dtall = per[:, NT:2 * NT, :].rearrange("p c h -> p (c h)")
            chain(nc.vector.scalar_tensor_tensor(dtall, z[:, 0, :], 0.0, z[:, 3, :], ALU.max, ALU.add))
            chain(nc.vector.scalar_tensor_tensor(per[:, 0:NT, :], per[:, NT:2 * NT, :], -1.0,
                                                 bcast[:, 1, :].unsqueeze(1).to_broadcast([P, NT, H]), ALU.mult, ALU.mult))
            dve.wait_ge(dt_act, 6)
            chain(nc.vector.tensor_tensor(per[:, 3 * NT:4 * NT, :], per[:, 3 * NT:4 * NT, :], per[:, NT:2 * NT, :], ALU.mult))
            chain(nc.vector.tensor_scalar(par[:, :, :], par[:, :, :], 0.5, None, ALU.mult))
            dve.wait_ge(acc_clear, 1)

            def group(g):
                nc.vector.tensor_copy(parg[:, :], par[:, bass.ds(g, 1), :].rearrange("p a b -> p (a b)")).then_inc(par_ready, 1)
                nc.vector.tensor_copy(cur[:, :, :], per[:, :, bass.ds(HG * g, HG)]).then_inc(cur_ready, 1)
                for q in range(NB * CT):
                    j = q % CT
                    dve.wait_ge(tap0, NB * CT * g + q + 1)
                    for k in range(KC - 2, -1, -1):
                        sh = KC - 1 - k
                        if sh > 1:
                            dve.wait_ge(taps, 3 * NB * CT * g + 3 * q + sh - 1)
                        nc.vector.scalar_tensor_tensor(
                            tap[:, q % 4, sh:L], bk(CB[q % 4])[:, 0:L - sh],
                            parg[:, KC * j + k:KC * j + k + 1],
                            tap[:, q % 4, sh:L], ALU.mult, ALU.add).then_inc(taps, 1)
                for s in range(NT + 2):
                    i = s - 2
                    if s >= 2:
                        dve.wait_ge(rg_ready, NT * g + i + 1)
                        nc.vector.scalar_tensor_tensor(yn[:, i % 2, :], y[:, :], rg[:, i % 2:i % 2 + 1],
                                                       sg[:, i % 2, :], ALU.mult, ALU.mult).then_inc(yn_ready, 1)
                    i, c = s - 1, (s - 1) % CH
                    if 1 <= s <= NT:
                        m = (CH - 1) * NB * g + (CH - 1) * (i // CH)
                        if i >= 1:
                            dve.wait_ge(yn_ready, NT * g + i)
                        if c > 0:
                            dve.wait_ge(yo_ready, m + c)
                            nc.vector.tensor_tensor(pair(y[:, :]), pair(bk(6)), heads(2 * NT + i), ALU.mult).then_inc(yo_used, 1)
                            dve.wait_ge(yi_ready, NT * g + i + 1)
                            dve.wait_ge(yo_used, m + c + 1)
                            nc.vector.tensor_tensor(y[:, :], y[:, :], bk(7), ALU.add).then_inc(y_part, 1)
                            dve.wait_ge(xd_ready, NT * g + i + 1)
                            dve.wait_ge(y_part, m + c)
                            nc.vector.tensor_tensor(y[:, :], y[:, :], xd[:, :], ALU.add).then_inc(y_ready, 1)
                        else:
                            dve.wait_ge(yi_ready, NT * g + i + 1)
                            dve.wait_ge(xd_ready, NT * g + i + 1)
                            nc.vector.tensor_tensor(y[:, :], bk(7), xd[:, :], ALU.add).then_inc(y_ready, 1)
                        if c < CH - 1:
                            dve.wait_ge(st_ready, m + c + 1)
                            if c == 0:
                                nc.vector.tensor_copy(state[:, :], bk(6)).then_inc(state_ready, 1)
                            else:
                                dve.wait_ge(sdec_ready, (CH - 2) * NB * g + (CH - 2) * (i // CH) + c)
                                nc.vector.tensor_tensor(state[:, :], bk(6), sdec[:, :], ALU.add).then_inc(state_ready, 1)
                    if s < NT:
                        dve.wait_ge(gb_ready, NT * g + s + 1)
                        nc.vector.tensor_copy(btok[:, s % 2, :], bk(5)[:, P:2 * P])
                        nc.vector.tensor_tensor(gmask[:, :], bk(5)[:, 0:P], upto[:, :], ALU.mult).then_inc(gb_used, 1)
                        dve.wait_ge(e_ready, NT * g + s + 2)
                        dve.wait_ge(gb_used, NT * g + s + 2)
                        nc.vector.tensor_tensor(em[:, s % 2, :, :], em[:, s % 2, :, :],
                                                gmask[:, :].unsqueeze(1).to_broadcast([P, HG, P]), ALU.mult).then_inc(m_ready, 1)
                    if s >= 2:
                        dve.wait_ge(tp_out, 2 * NT * g + evacuation(s) + 2)
                        low(nc.vector, ynTl[:, :], bk(4), ynTh[:, :]).then_inc(ynT_lo, 1)
                    if s < NT:
                        dve.wait_ge(tg_ready, NT * g + s + 1)
                        nc.vector.scalar_tensor_tensor(sg[:, s % 2, :], tg[:, :], 1.0, bk(0), ALU.add,
                                                       ALU.mult).then_inc(gate_used, 1)
                    i = s - 2
                    if s >= 2:
                        dve.wait_ge(o_ready, NT * g + i + 1)
                        nc.vector.tensor_tensor(acc[:, i, :], acc[:, i, :], bk(1), ALU.add).then_inc(out_added, 1)

            with dve.Fori(0, G) as g:
                group(g)
            norm_vector(1)
            if STAGES >= 2:
                dve.wait_ge(f_small, 48)
                nc.vector.tensor_scalar(fsc[:, 0, :], gus[:, 0, :], 0.5, None, ALU.mult).then_inc(f_dve, 1)
                dve.wait_ge(f_dve, 1)
                nc.vector.tensor_tensor(fsc[:, 1, :], fsc[:, 0, :], gus[:, 1, :], ALU.mult).then_inc(f_part, 1)
                dve.wait_ge(f_part, 1)
                dve.sem_inc(down_added, 4)
                dve.wait_ge(f_clear, 1)

                def add_down(f, b):
                    for i in range(b * CH, (b + 1) * CH):
                        dve.wait_ge(down_ps, NT * f + i + 1)
                        nc.vector.tensor_tensor(acc[:, i, :], acc[:, i, :], bk(4 + i % 4), ALU.add).then_inc(down_added, 1)

                def hid_low(f, q):
                    dve.wait_ge(hid_hi, 4 * f + q + 1)
                    low(nc.vector, hid_part(hidl, q), hidf[:, q % 2, :], hid_part(hidh, q)).then_inc(hid_ready, 1)

                def hidden_pair(f, first):
                    if not first:
                        dve.wait_ge(hid_ready, 4 * f)
                    nc.vector.tensor_copy(fscg[:, :, :], fsc[:, :, bass.ds(2 * f, 2)]).then_inc(fsc_ready, 1)
                    for q in range(4):
                        dve.wait_ge(f_tanh, 4 * f + q + 1)
                        if not (first and q < 2):
                            dve.wait_ge(hid_ready, 4 * f + q - 1)
                        nc.vector.scalar_tensor_tensor(fh[:, q % 2, :], fth[:, q % 2, :], 1.0, bk(q % 2), ALU.add,
                                                       ALU.mult).then_inc(f_part, 1)
                        dve.wait_ge(f_part, 4 * f + q + 2)
                        dve.wait_ge(up_ps, 4 * f + q + 2)
                        nc.vector.scalar_tensor_tensor(hidf[:, q % 2, :], fh[:, q % 2, :],
                                                       fscg[:, 1, q % 2:q % 2 + 1], bk(2 + q % 2),
                                                       ALU.mult, ALU.mult).then_inc(hid_f, 1)
                        if q % 2:
                            hid_low(f, q - 1)
                            hid_low(f, q)
                        if q == 1 and not first:
                            add_down(f - 1, 1)
                    add_down(f, 0)

                hidden_pair(0, True)
                with dve.Fori(1, FP) as f:
                    hidden_pair(f, False)
                add_down(FP - 1, 1)
                dve.wait_ge(down_added, 4 + NT * FP)
                for i in range(NT):
                    nc.vector.tensor_tensor(acc[:, i, :], acc[:, i, :], dsb[:, :], ALU.mult).then_inc(f_dve, 1)
                norm_vector(2)
            if STAGES >= 3:
                dve.wait_ge(sel_ready, 2)
                s = Count(sel_ready)
                s.n = 2

                def step(ins):
                    s.inc(ins)
                    dve.wait_ge(sel_ready, s.n)

                flat = fold[:, :, :].rearrange("p a b -> p (a b)")
                step(nc.vector.tensor_tensor(flat, ident[:, 0:32], ident[:, 32:64], ALU.add))
                step(nc.vector.tensor_tensor(flat, flat, ident[:, 64:96], ALU.add))
                step(nc.vector.tensor_tensor(flat, flat, ident[:, 96:128], ALU.add))
                step(nc.vector.tensor_scalar(sel[:, :, :], ident[:, :].unsqueeze(1).to_broadcast([P, 4, P]), 0.0, None, ALU.mult))
                for m, reps in enumerate(((0, 2), (1, 3), (0, 1), (2, 3))):
                    dst = sel[:, m, :].rearrange("p (a r d) -> p a r d", a=2, r=4)
                    for r in reps:
                        step(nc.vector.tensor_copy(dst[:, :, r, :], fold[:, :, :]))
                step(nc.vector.tensor_copy(identb[:, :], ident[:, :]))
                step(nc.vector.tensor_copy(future[:, :], futf[:, :]))
                dve.sem_inc(exp_ready, 2)
                dve.sem_inc(pt_lo, 2)
                dve.sem_inc(osum_ready, 1)
                dve.sem_inc(att_ready, 1)
                dve.sem_inc(prec_ready, 2)
                dve.wait_ge(a_small, 48)
                nc.vector.tensor_scalar(abqk[:, 0, :], abqk[:, 0, :], HD ** -0.5, None, ALU.mult).then_inc(qb_scaled, 1)
                for i in range(NT + 1):
                    if i < NT:
                        dve.wait_ge(v_ps, i + 1)
                        if i >= 2:
                            dve.wait_ge(v_ready, i - 1)
                        nc.vector.tensor_tensor(qf[:, i % 2, :], bk(i % 2), abv[:, :], ALU.add).then_inc(v_f, 1)
                    if i >= 1:
                        j = i - 1
                        dve.wait_ge(v_hi, i)
                        nc.vector.tensor_tensor(v[:, j, :, 1, :], qf[:, j % 2, :].rearrange("p (h d) -> p h d", d=HD),
                                                v[:, j, :, 0, :].bitcast(F32), ALU.subtract).then_inc(v_ready, 1)
                dve.wait_ge(qb_scaled, 1)
                dve.wait_ge(v_ready, NT)

                def biases(t):
                    dve.wait_ge(qk_f, 4 * t) if not isinstance(t, int) else None
                    nc.vector.tensor_copy(abg[:, :], abqk[:, :, bass.ds(t, 1)].rearrange("p a b -> p (a b)")).then_inc(bias_ready, 1)

                def prepare(t, b, piece):
                    m = NB * t + b
                    if piece < 2:
                        dve.wait_ge(qk_f, 2 * m + piece + 1)
                        nc.vector.tensor_copy(qh[:, piece, :], qf[:, piece, :]).then_inc(qk_h, 1)
                        dve.wait_ge(qk_h, 2 * m + piece + 1)
                        low(nc.vector, ql[:, piece, :], qf[:, piece, :], qh[:, piece, :]).then_inc(qk_l, 1)
                    elif piece % 2:
                        dve.wait_ge(st_ps, 8 * m + piece - 1)
                        nc.vector.tensor_copy(stacked(b, piece - 2), bk(7)).then_inc(st_out2, 1)

                def tile(t, last):
                    for s in range(UNITS + 4):
                        w = s - 4
                        if w >= 0:
                            if w % 4 == 0:
                                dve.wait_ge(att_ready, 8 * t + w // 4 + 1)
                            dve.wait_ge(pv_ps, UNITS * t + w + 1)
                            o = bk(6).rearrange("p (j h w d) -> p j h d w", j=2, h=HT, w=2)
                            pr = w % 4
                            for j in range(2):
                                ins = nc.vector.tensor_reduce(osum[:, 2 * pr + j, :], o[:, j, 2 * pr + j, :, :], AX, ALU.add)
                            ins.then_inc(osum_ready, 1)
                        if s < UNITS:
                            kw = (s % 16 // 4 + 1) * P
                            dve.wait_ge(s_ready, UNITS * t + s + 1)
                            nc.vector.tensor_reduce(nmax[:, s % 2, :], banks[:, 2 * (s % 2):2 * (s % 2) + 2, 0:kw],
                                                    AX, ALU.max, negate=True).then_inc(max_ready, 1)
                        w = s - 2
                        if 0 <= w < UNITS:
                            kw = (w % 16 // 4 + 1) * P
                            for j in range(2):
                                dve.wait_ge(pt_hi, 2 * UNITS * t + 2 * w + j + 1)
                                low(nc.vector, pTl[:, w % 2, j, 0:kw], bk(4 + j)[:, 0:kw],
                                    pTh[:, w % 2, j, 0:kw]).then_inc(pt_lo, 1)
                        gq = s // 4 - 1
                        if s % 4 == 1 and gq >= 0:
                            dve.wait_ge(exp_ready, UNITS * t + s - 1 + 2)
                            dve.wait_ge(att_ready, 8 * t + gq + 1)
                            nc.vector.reciprocal(prec[:, :], psum[:, gq % 2, :]).then_inc(prec_ready, 1)
                        if s % 4 == 3 and gq >= 0:
                            dve.wait_ge(osum_ready, UNITS * t + s - 4 + 1 + 1)
                            dve.wait_ge(prec_ready, 8 * t + gq + 3)
                            nc.vector.tensor_tensor(
                                att[:, gq, bass.ds(P * t, P)].rearrange("p (h d) -> p h d", d=HD), osum[:, :, :],
                                prec[:, :].unsqueeze(2).to_broadcast([P, HT, HD]), ALU.mult).then_inc(att_ready, 1)
                        if s == 16 and not last:
                            biases(t + 1)
                        ahead = passes_ahead(t, s, last)
                        if ahead:
                            prepare(*ahead)

                biases(0)
                for piece in range(10):
                    prepare(0, 0, piece)
                with dve.Fori(0, AT - 1) as t:
                    tile(t, False)
                tile(AT - 1, True)
                for i in range(NT + 1):
                    if i < NT:
                        dve.wait_ge(at_hi, i + 1)
                        low(nc.vector, attTl[:, i % 2, :], bk(i % 2), attTh[:, i % 2, :]).then_inc(at_lo, 1)
                    if i >= 1:
                        dve.wait_ge(ao_ps, i)
                        nc.vector.tensor_tensor(acc[:, i - 1, :], bk(6 + (i - 1) % 2), abo[:, :], ALU.add).then_inc(ao_ready, 1)
                norm_vector(3)
            if STAGES >= 4:
                dve.wait_ge(lg_ps, 1)
                r = Count(r_dve)

                def rstep(ins, wait=True):
                    r.inc(ins)
                    if wait:
                        dve.wait_ge(r_dve, r.n)

                rstep(nc.vector.tensor_copy(lg[:, :, :], bk(0)[:, 0:NT * NE].rearrange("p (a b) -> p a b", a=NT)))
                for i in range(NT):
                    rstep(nc.vector.max(top[:, i, :], lg[:, i, :]), i == NT - 1)
                for i in range(NT):
                    rstep(nc.vector.max_index(topi[:, i, :], top[:, i, :], lg[:, i, :]), i == NT - 1)
                rstep(nc.vector.tensor_tensor(rt[:, 0, :], top[:, :, 1], top[:, :, 0], ALU.subtract))
                rstep(nc.vector.tensor_copy(topf[:, :, :], topi[:, :, :]))
                dve.wait_ge(r_act, 1)
                dve.wait_ge(r_iota, 1)
                rstep(nc.vector.tensor_scalar(rt[:, 2, :], rt[:, 1, :], 1.0, None, ALU.add))
                rstep(nc.vector.reciprocal(rt[:, 2, :], rt[:, 2, :]))
                rstep(nc.vector.tensor_tensor(rt[:, 3, :], rt[:, 2, :], rt[:, 1, :], ALU.mult))
                for c in range(2):
                    rstep(nc.vector.tensor_tensor(oh[:, c, :, :], which[:, :].unsqueeze(1).to_broadcast([P, NT, NE]),
                                                  topf[:, :, c].unsqueeze(2).to_broadcast([P, NT, NE]), ALU.is_equal))
                    rstep(nc.vector.tensor_tensor(oh[:, c, :, :], oh[:, c, :, :],
                                                  rt[:, 2 + c, :].unsqueeze(2).to_broadcast([P, NT, NE]), ALU.mult))
                rstep(nc.vector.tensor_tensor(we[:, :, :], oh[:, 0, :, :], oh[:, 1, :, :], ALU.add))
                dve.wait_ge(d_clear, 1)
                dve.sem_inc(ex_added, NT)
                with dve.Fori(0, NE // 2) as e:
                    for s in range(2):
                        for i in range(NT):
                            dve.wait_ge(ex_ps, 2 * NT * e + NT * s + i + 1)
                            nc.vector.scalar_tensor_tensor(acc[:, i, :], bk(i), we[:, i, bass.ds(2 * e + s, 1)],
                                                           acc[:, i, :], ALU.mult, ALU.add).then_inc(ex_added, 1)
                norm_vector(4)

        @block.tensor
        def _(pe):
            mat = nc.tensor.matmul
            pe.sem_inc(up_ps, 1)
            pe.wait_ge(consts, 6)
            norm_tensor(0)
            norm_wait(pe, 0, "lo", NT)
            pe.wait_ge(wdt_lo, 1)
            for i in range(NT):
                tok = slice(i * P, (i + 1) * P)
                m = products(bk(0)[:, i * H:(i + 1) * H],
                             [(xTh[:, k, tok], xTl[:, k, tok], wdth[:, k, :], wdtl[:, k, :]) for k in range(KT)])
            m.then_inc(dt_ps, 1)
            pe.wait_ge(dt_dve, 8)
            for n, mask in enumerate((upto, after, ones)):
                mat(bk(n), mask[:, :], per[:, 0:NT, :].rearrange("p c h -> p (c h)"), start=True, stop=True).then_inc(dt_cum, 1)
            pe.wait_ge(dt_act, 6)
            with pe.Fori(0, G) as g:
                pe.wait_ge(wc_lo, KT * g + KT)
                for q in range(NB * CT):
                    b, j = q // CT, q % CT
                    if q == 0:
                        pe.wait_ge(gate_used, NT * g + 1)
                    elif q == 1:
                        pe.wait_ge(out_added, NT * g + 1)
                    elif q == 2:
                        pe.wait_ge(yo_used, (CH - 1) * NB * g + 1)
                    elif q == 3:
                        pe.wait_ge(y_ready, NT * g + 1)
                    else:
                        pe.wait_ge(taps, 3 * NB * CT * g + 3 * (q - 3))
                    ch, tok = slice(j * P, (j + 1) * P), slice(b * L, (b + 1) * L)
                    products(bk(CB[q % 4]), [(wch[:, k, ch], wcl[:, k, ch], xTh[:, k, tok], xTl[:, k, tok])
                                         for k in range(KT)]).then_inc(h_ready, 1)
                for s in range(NT + 2):
                    if s < NT:
                        b = s // CH
                        tok = slice(s * P, (s + 1) * P)
                        if s % CH == 0:
                            pe.wait_ge(xbc_ready, NB * CT * g + CT * (b + 1) + 4)
                        if s in (1, 2):
                            pe.wait_ge(tp_out, 2 * NT * g + s + 1)
                        else:
                            pe.wait_ge(ynT_lo, NT * g + max(s - 2, 0) + 1)
                        for j in range(KT):
                            m = pe.transpose(bk(4)[:, j * P:(j + 1) * P], xbc[:, j, tok], ident[:, :])
                        m.then_inc(x_tr, 1)
                        pe.wait_ge(gb_used, NT * g + s + 1)
                        pe.transpose(bk(5)[:, P:2 * P], xbc[:, JB, tok], ident[:, :])
                        mat(bk(5)[:, 0:P], xbc[:, JB, tok], xbc[:, JC, tok], start=True, stop=True).then_inc(gb_ready, 1)
                        pe.wait_ge(am_ready, NT * g + s + 1)
                        pe.wait_ge(e_ready, NT * g + s + 1)
                        for w in range(2):
                            m = mat(bk(2 + w), after[:, :],
                                    am[:, s % 2, 4 * w:4 * w + 4, :].rearrange("p h t -> p (h t)"), start=True, stop=True)
                        m.then_inc(d_ready, 1)
                    i, c = s - 1, (s - 1) % CH
                    if 1 <= s <= NT:
                        tok = slice(i * P, (i + 1) * P)
                        m0 = (CH - 1) * NB * g + (CH - 1) * (i // CH)
                        if c > 0:
                            pe.wait_ge(state_ready, m0 + c)
                            mat(bk(6), xbc[:, JC, tok], state[:, :], start=True, stop=True).then_inc(yo_ready, 1)
                        pe.wait_ge(m_ready, NT * g + i + 1)
                        pe.wait_ge(dtx_ready, NT * g + i + 1)
                        pe.wait_ge(y_ready, NT * g + i + 1)
                        for h in range(HG):
                            m = mat(bk(7)[:, h * HP:(h + 1) * HP], em[:, i % 2, h, :], dtx[:, h * HP:(h + 1) * HP],
                                    start=True, stop=True)
                        m.then_inc(yi_ready, 1)
                        if c < CH - 1:
                            pe.wait_ge(xdec_ready, m0 + c + 1)
                            pe.wait_ge(yo_used, m0 + c + 1)
                            mat(bk(6), btok[:, i % 2, :], xdec[:, :], start=True, stop=True).then_inc(st_ready, 1)
                    i = s - 2
                    if s >= 2:
                        pe.wait_ge(yn_ready, NT * g + i + 1)
                        if s < NT:
                            pe.wait_ge(tp_out, 2 * NT * g + evacuation(s) + 1)
                        else:
                            pe.wait_ge(ynT_lo, NT * g + i + 1)
                        for j in range(KT):
                            m = pe.transpose(bk(4)[:, j * P:(j + 1) * P], yn[:, i % 2, j * P:(j + 1) * P], ident[:, :])
                        m.then_inc(yn_tr, 1)
                    if s < NT:
                        if s == 0:
                            pe.wait_ge(wg_lo, KT * g + KT)
                            pe.wait_ge(taps, 3 * NB * CT * g + 3 * NB * CT)
                        tok = slice(s * P, (s + 1) * P)
                        pe.wait_ge(gate_used, NT * g + s + 1)
                        products(bk(0), [(xTh[:, k, tok], xTl[:, k, tok], wgh[:, k, :], wgl[:, k, :])
                                         for k in range(KT)]).then_inc(gate_ready, 1)
                    if s >= 2:
                        if i == 0:
                            pe.wait_ge(wo_lo, KT * g + KT)
                        pe.wait_ge(out_added, NT * g + i + 1)
                        pe.wait_ge(ynT_lo, NT * g + i + 2)
                        products(bk(1), [(ynTh[:, k * P:(k + 1) * P], ynTl[:, k * P:(k + 1) * P], woh[:, k, :], wol[:, k, :])
                                         for k in range(KT)]).then_inc(o_ready, 1)
            if STAGES >= 2:
                norm_tensor(1)
                norm_wait(pe, 1, "lo", NT)

                def gate_up(f, b, first):
                    tok = slice(b * L, (b + 1) * L)
                    for ft in range(2):
                        q = 2 * b + ft
                        if not (first and q < 2):
                            pe.wait_ge(hid_f, 4 * f + q - 1)
                        for w, done in ((0, gate_ps), (1, up_ps)):
                            for k in range(KT):
                                for part in (xTh, xTl):
                                    m = mat(bk(2 * w + ft), gu[:, k, ft, w, :], part[:, k, tok],
                                            start=(k == 0 and part is xTh), stop=(k == KT - 1 and part is xTl))
                            m.then_inc(done, 1)

                def down(f, b):
                    pe.wait_ge(hid_ready, 4 * f + 2 * b + 2)
                    for i in range(b * CH, (b + 1) * CH):
                        pe.wait_ge(down_added, NT * f + i + 1)
                        for k in range(2):
                            for part in (hidh, hidl):
                                m = mat(bk(4 + i % 4), part[:, k, i * P:(i + 1) * P], dn[:, k, :],
                                        start=(k == 0 and part is hidh), stop=(k == 1 and part is hidl))
                        m.then_inc(down_ps, 1)

                def hidden_pair(f, first):
                    pe.wait_ge(gu_cast, KT * f + KT)
                    gate_up(f, 0, first)
                    if not first:
                        down(f - 1, 1)
                    gate_up(f, 1, first)
                    pe.wait_ge(dn_cast, 2 * f + 2)
                    down(f, 0)

                hidden_pair(0, True)
                with pe.Fori(1, FP) as f:
                    hidden_pair(f, False)
                down(FP - 1, 1)
            if STAGES >= 3:
                norm_tensor(2)
                norm_wait(pe, 2, "lo", NT)
                pe.wait_ge(aw_lo, KT)
                for i in range(NT):
                    if i >= 2:
                        pe.wait_ge(v_f, i - 1)
                    tok = slice(i * P, (i + 1) * P)
                    products(bk(i % 2), [(xTh[:, k, tok], xTl[:, k, tok], awh[:, k, :], awl[:, k, :])
                                         for k in range(KT)]).then_inc(v_ps, 1)
                pe.wait_ge(sel_ready, 2 + 4 + 8 + 2)

                def prepare(t, b, piece):
                    m = NB * t + b
                    first = isinstance(t, int)
                    if piece < 2:
                        if piece:
                            pe.wait_ge(qk_f, 2 * m + 1)
                        elif not first:
                            pe.wait_ge(st_out2, 4 * m)
                        if piece == 0 and b == 0:
                            pe.wait_ge(aq_lo, 2 * t + 2)
                        tok = slice(b * L, (b + 1) * L)
                        products(bk(7), [(aqh[:, piece, k, :], aql[:, piece, k, :], xTh[:, k, tok], xTl[:, k, tok])
                                         for k in range(KT)]).then_inc(qk_ps, 1)
                    else:
                        w, pr = (piece - 2) // 4, (piece - 2) % 4
                        if piece == 2:
                            pe.wait_ge(qk_l, 2 * m + 2)
                        else:
                            pe.wait_ge((st_out, st_out2)[(piece - 1) % 2], 4 * m + (piece - 1) // 2)
                        rows = slice(32 * pr, 32 * pr + 32)
                        mat(bk(7), sel[rows, 2 * w, :], qh[rows, w, :], start=True, stop=False)
                        mat(bk(7), sel[rows, 2 * w + 1, :], ql[rows, w, :], start=False, stop=True).then_inc(st_ps, 1)

                def tile(t, last):
                    for s in range(UNITS + 3):
                        if s < UNITS:
                            b, qi, pr = s // 16, s % 16 // 4, s % 4
                            kw = (qi + 1) * P
                            if s % 16 == 0:
                                pe.wait_ge(st_out, 4 * (NB * t + b) + 4)
                                pe.wait_ge(st_out2, 4 * (NB * t + b) + 4)
                            pe.wait_ge(exp_ready, UNITS * t + s + 1)
                            for j in range(2):
                                rows = slice(64 * j, 64 * j + 64)
                                o = bk(2 * (s % 2) + j)
                                mat(o[:, 0:kw], qs[rows, b, pr, qi * P:kw], ks[rows, b, pr, 0:kw], start=True, stop=False)
                                m = mat(o[:, kw - P:kw], identb[:, :], future[:, :], start=False, stop=True)
                            m.then_inc(s_ready, 1)
                        w = s - 2
                        if 0 <= w < UNITS:
                            pe.wait_ge(exp_ready, UNITS * t + w + 1 + 2)
                            for j in range(2):
                                pe.wait_ge(pt_lo, 2 * UNITS * t + 2 * w + j + 1)
                                for c in range(w % 16 // 4 + 1):
                                    m = pe.transpose(bk(4 + j)[:, c * P:(c + 1) * P], prob[:, w % 2, j, c * P:(c + 1) * P], ident[:, :])
                                m.then_inc(pt_ps, 1)
                        w = s - 3
                        if w >= 0:
                            b, qi = w // 16, w % 16 // 4
                            pe.wait_ge(pt_lo, 2 * UNITS * t + 2 * w + 2 + 2)
                            pe.wait_ge(osum_ready, UNITS * t + w + 1)
                            for j in range(2):
                                o = bk(6)[:, 2 * P * j:2 * P * (j + 1)]
                                for c in range(qi + 1):
                                    vals = v[:, b * CH + c, bass.ds(HT * t, HT), :, :].rearrange("p h w d -> p (h w d)")
                                    for part in (pTh, pTl):
                                        m = mat(o, part[:, w % 2, j, c * P:(c + 1) * P], vals,
                                                start=(c == 0 and part is pTh), stop=(c == qi and part is pTl))
                            m.then_inc(pv_ps, 1)
                        ahead = passes_ahead(t, s, last)
                        if ahead:
                            prepare(*ahead)

                for piece in range(10):
                    prepare(0, 0, piece)
                with pe.Fori(0, AT - 1) as t:
                    tile(t, False)
                tile(AT - 1, True)
                for i in range(NT + 1):
                    if i < NT:
                        if i == 0:
                            pe.wait_ge(att_ready, 8 * AT + 1)
                        if i >= 2:
                            pe.wait_ge(at_lo, i - 1)
                        for k in range(KT):
                            m = pe.transpose(bk(i % 2)[:, k * P:(k + 1) * P], att[:, i, k * P:(k + 1) * P], ident[:, :])
                        m.then_inc(at_ps, 1)
                    if i >= 1:
                        j = i - 1
                        pe.wait_ge(at_lo, j + 1)
                        pe.wait_ge(aw_lo, 2 * KT)
                        if j >= 2:
                            pe.wait_ge(ao_ready, j - 1)
                        cols = [slice(k * P, (k + 1) * P) for k in range(KT)]
                        products(bk(6 + j % 2), [(attTh[:, j % 2, c], attTl[:, j % 2, c], awh[:, k, :], awl[:, k, :])
                                                 for k, c in enumerate(cols)]).then_inc(ao_ps, 1)
            if STAGES >= 4:
                norm_tensor(3)
                norm_wait(pe, 3, "lo", NT)
                pe.wait_ge(rw_lo, 1)

                def stream(i):
                    return lambda wh, wl: [(xTh[:, k, i * P:(i + 1) * P], xTl[:, k, i * P:(i + 1) * P], wh[:, k, :], wl[:, k, :])
                                           for k in range(KT)]

                for i in range(NT):
                    m = products(bk(0)[:, i * NE:(i + 1) * NE], stream(i)(rwh, rwl))
                m.then_inc(lg_ps, 1)
                pe.wait_ge(r_dve, 1)
                with pe.Fori(0, NE // 2) as e:
                    for s in range(2):
                        pe.wait_ge(e_lo, 2 * KT * e + KT * (s + 1))
                        for i in range(NT):
                            pe.wait_ge(ex_added, 2 * NT * e + NT * s + i + 1)
                            products(bk(i), stream(i)(ewh[:, s], ewl[:, s])).then_inc(ex_ps, 1)


def kernel(**inputs):
    from concourse.bacc import Bacc
    from concourse.bass_utils import run_bass_kernel_spmd

    a = {k: np.asarray(v) for k, v in inputs.items()}

    def rows(w):
        return w.T.reshape(KT, P, -1).transpose(1, 0, 2)

    w_in = a["L0_attn_in_proj_w"]
    inner, gn = H * HP, G * NS
    gate_w, x_w, b_w, c_w, dt_w = np.split(w_in, [inner, 2 * inner, 2 * inner + gn, 2 * inner + 2 * gn])

    def by_group(x, b, c):
        return np.concatenate([m.reshape(G, -1, *m.shape[1:]) for m in (x, b, c)], 1)

    conv = by_group(x_w, b_w, c_w)
    cw = by_group(*np.split(a["L0_attn_conv_weight"], [inner, inner + gn])).reshape(G, CT, P, KC)
    cb = by_group(*np.split(a["L0_attn_conv_bias"], [inner, inner + gn])).reshape(G, CT, P)
    gu = np.stack([a["L0_ffn_gate_t"], a["L0_ffn_up_t"]]).reshape(2, FP, 2, P, KT, P)
    arrays = {
        "hidden": a["L0_attn_hidden_states"].reshape(NB * L, DM),
        "w_conv": np.stack([rows(m) for m in conv]),
        "w_gate": np.stack([rows(m) for m in gate_w.reshape(G, GI, DM)]),
        "w_dt": rows(dt_w),
        "conv_w": cw.transpose(2, 0, 1, 3),
        "conv_b": cb.transpose(2, 0, 1),
        "dt_bias": a["L0_attn_dt_bias"],
        "A_log": a["L0_attn_A_log"],
        "Dskip": a["L0_attn_D"],
        "norm_w": a["L0_attn_norm_weight"].reshape(G, KT, P).transpose(2, 0, 1),
        "w_out": a["L0_attn_out_proj_w"].reshape(DM, G, KT, P).transpose(1, 3, 2, 0),
        "ff_gu": gu.transpose(1, 5, 4, 2, 0, 3),
        "ff_dn": a["L0_ffn_down_t"].reshape(DM, FP, 2, P).transpose(1, 3, 2, 0),
        "gate_s": a["L0_ffn_gate_s"].reshape(FT, P).T,
        "up_s": a["L0_ffn_up_s"].reshape(FT, P).T,
        "down_s": a["L0_ffn_down_s"],
        "wq": a["L1_attn_Wq"].reshape(AT, P, KT, P).transpose(0, 3, 2, 1),
        "wk": a["L1_attn_Wk"].reshape(AT, P, KT, P).transpose(0, 3, 2, 1),
        "bqk": np.stack([a["L1_attn_bq"], a["L1_attn_bk"]]).reshape(2, AT, P).transpose(2, 0, 1),
        "wv": rows(a["L1_attn_Wv"]),
        "bv": a["L1_attn_bv"],
        "wo": rows(a["L1_attn_Wo"]),
        "bo": a["L1_attn_bo"],
        "gate_w": a["L1_ffn_gate_w"].reshape(KT, P, NE).transpose(1, 0, 2),
        "expert_w": a["L1_ffn_expert_w"].reshape(NE, KT, P, DM).transpose(0, 2, 1, 3),
    }
    arrays = {k: np.ascontiguousarray(v) for k, v in arrays.items()}
    nc = Bacc("TRN2", target_bir_lowering=False, num_devices=1)
    args = {k: nc.dram_tensor(f"in_{k}", v.shape, mybir.dt.from_np(v.dtype), kind="ExternalInput").ap()
            for k, v in arrays.items()}
    out = nc.dram_tensor("out", (NB * L, DM), F32, kind="ExternalOutput").ap()
    program(nc, out=out, **args)
    r = run_bass_kernel_spmd(nc, [{f"in_{k}": v for k, v in arrays.items()}], core_ids=[0])
    return r.results[0]["out"].reshape(NB, L, DM)
```

```python
import numpy as np
import concourse.bass as bass
from concourse import mybir
from concourse.alu_op_type import AluOpType as ALU
from contextlib import ExitStack

F32 = mybir.dt.float32
F32R = mybir.dt.float32r
BF16 = mybir.dt.bfloat16
I32 = mybir.dt.int32
U32 = mybir.dt.uint32
ACT = mybir.ActivationFunctionType
AX = mybir.AxisListType.X

P = 128
DM = 512
KT = DM // P
NB, L = 2, 512
NT = NB * L // P
CH = L // P
EPS = 1e-5
H, HP, NS, G, KC = 64, 64, 128, 8, 4
HG = H // G
GI = HG * HP
CT = GI // P + 2
JB, JC = CT - 2, CT - 1
FF = 1792
FT = FF // P
FP = FT // 2
AH, HD = 32, 16
AT = DM // P
HT = P // HD
NE = 8
STAGES = 4


class Count:

    def __init__(self, sem):
        self.sem, self.n = sem, 0

    def inc(self, instruction):
        self.n += 1
        instruction.then_inc(self.sem, 1)
        return self.n


def program(nc, hidden, w_conv, w_gate, w_dt, conv_w, conv_b, dt_bias, A_log, Dskip, norm_w, w_out,
            ff_gu, ff_dn, gate_s, up_s, down_s, wq, wk, bqk, wv, bv, wo, bo, gate_w, expert_w, out):
    ctx = ExitStack()
    with ctx:

        def sb(name, shape, dt=F32, stack=ctx):
            return stack.enter_context(nc.sbuf_tensor(name, shape, dt))

        def sem(name):
            return ctx.enter_context(nc.semaphore(name))

        banks = ctx.enter_context(nc.psum_tensor("banks", [P, 8, 512], F32))

        def bk(i):
            return banks[:, i, :]

        x = sb("x", [P, NT, DM])
        acc = sb("acc", [P, NT, DM])
        xTh = sb("xTh", [P, KT, NB * L], F32R)
        xTl = sb("xTl", [P, KT, NB * L], F32R)
        ident = sb("ident", [P, P])
        ones = sb("ones", [P, P])
        upto = sb("upto", [P, P])
        after = sb("after", [P, P], F32R)
        mhalf = sb("mhalf", [P, NT])
        epsc = sb("epsc", [P, 1])
        stats = sb("stats", [P, 2, NT, 6])
        mv = sb("mv", [P, 2, NT, 2])
        ve = sb("ve", [P, 2, NT])
        rs = sb("rs", [P, 2, NT])

        A = ExitStack()

        def sa(name, shape, dt=F32):
            return sb(name, shape, dt, A)

        wch = sa("wch", [P, KT, CT * P], F32R)
        wcl = sa("wcl", [P, KT, CT * P], F32R)
        wgh = sa("wgh", [P, KT, GI], F32R)
        wgl = sa("wgl", [P, KT, GI], F32R)
        woh = sa("woh", [P, KT, DM], F32R)
        wol = sa("wol", [P, KT, DM], F32R)
        wdth, wdtl = woh[:, :, 0:H], wol[:, :, 0:H]
        par = sa("par", [P, G, CT * KC + CT + KT])
        parg = sa("parg", [P, CT * KC + CT + KT])
        per = sa("per", [P, 5 * NT + 1, H])
        cur = sa("cur", [P, 5 * NT + 1, HG])
        tap = sa("tap", [P, 2, L])
        th = sa("th", [P, L])
        xbc = sa("xbc", [P, CT, NB * L])
        xtok = sa("xtok", [P, 2, GI])
        btok = sa("btok", [P, 2, NS])
        gmask = sa("gmask", [P, P])
        am = sa("am", [P, 2, HG, P], F32R)
        ah = sa("ah", [P, NT, HG], F32R)
        al = sa("al", [P, NT, HG], F32R)
        em = sa("em", [P, 2, HG, P])
        z = em[:, :, :, :].rearrange("p a h t -> p (a h t)").rearrange("p (n c) -> p n c", n=4)
        dtx = sa("dtx", [P, GI])
        xdec = sa("xdec", [P, GI])
        wdt = xdec[:, 0:KT * H].rearrange("p (k h) -> p k h", k=KT)
        xd = sa("xd", [P, GI])
        bcast = xd[:, 0:2 * H].rearrange("p (a h) -> p a h", a=2)
        state = sa("state", [P, GI])
        y = sa("y", [P, GI])
        ss = sa("ss", [P, 2])
        ssv = sa("ssv", [P, 2])
        rg = sa("rg", [P, 2])
        yn = sa("yn", [P, GI])
        sg = sa("sg", [P, 2, GI])
        ynTh = sa("ynTh", [P, GI], F32R)
        ynTl = sa("ynTl", [P, GI], F32R)
        A.close()

        B = ExitStack()

        def sf(name, shape, dt=F32):
            return sb(name, shape, dt, B)

        gur = sf("gur", [P, KT, 2, 2, P], I32)
        dnr = sf("dnr", [P, 2, DM], I32)
        gu = sf("gu", [P, KT, 2, 2, P], F32R)
        dn = sf("dn", [P, 2, DM], F32R)
        gus = sf("gus", [P, 2, FT])
        fsc = sf("fsc", [P, 2, FT])
        fscg = sf("fscg", [P, 2, 2])
        dsb = sf("dsb", [P, DM])
        fth = sf("fth", [P, 2, L])
        fh = sf("fh", [P, 2, L])
        hidf = sf("hidf", [P, 2, L])
        hidh = sf("hidh", [P, 2, NB * L], F32R)
        hidl = sf("hidl", [P, 2, NB * L], F32R)
        B.close()

        C = ExitStack()

        def sc(name, shape, dt=F32):
            return sb(name, shape, dt, C)

        qs = sc("qs", [P, 2, 4, L], F32R)
        ks = sc("ks", [P, 2, 4, L], F32R)
        prob = sc("prob", [P, 2, 2, L])
        pTh = sc("pTh", [P, 2, 2, L], F32R)
        pTl = sc("pTl", [P, 2, 2, L], F32R)
        attTh, attTl = pTh[:, :, 0, :], pTl[:, :, 0, :]
        att = acc
        awr = prob[:, :, :, :].rearrange("p a b l -> p (a b) l")
        qh = sc("qh", [P, 2, L], F32R)
        ql = sc("ql", [P, 2, L], F32R)
        v = sc("v", [P, NT, AH, 2, HD], F32R)
        fold = sc("fold", [P, 2, HD])
        sel = sc("sel", [P, 4, P], F32R)
        identb = sc("identb", [P, P], BF16)
        future = sc("future", [P, P], BF16)
        futf = sc("futf", [P, P])
        nmax = sc("nmax", [P, 2, 2])
        psum = sc("psum", [P, 2, HT])
        prec = sc("prec", [P, HT])
        osum = sc("osum", [P, HT, HD])
        vf = sc("vf", [P, 2, L])
        abqk = sc("abqk", [P, 2, AT])
        abg = sc("abg", [P, 2])
        abv = sc("abv", [P, DM])
        abo = abv
        awh = sc("awh", [P, KT, DM], F32R)
        awl = sc("awl", [P, KT, DM], F32R)
        aqr = sc("aqr", [P, 2, KT, P])
        aqh = sc("aqh", [P, 2, KT, P], F32R)
        aql = sc("aql", [P, 2, KT, P], F32R)
        C.close()

        D = ExitStack()

        def sd(name, shape, dt=F32):
            return sb(name, shape, dt, D)

        ew = sd("ew", [P, 2, KT, DM])
        rw = sd("rw", [P, KT, NE])
        rwh = sd("rwh", [P, KT, NE], F32R)
        rwl = sd("rwl", [P, KT, NE], F32R)
        ewh = sd("ewh", [P, 2, KT, DM], F32R)
        ewl = sd("ewl", [P, 2, KT, DM], F32R)
        lgT = sd("lgT", [P, NB, L])
        lg = sd("lg", [P, NT, NE])
        top = sd("top", [P, NT, NE])
        topi = sd("topi", [P, NT, NE], U32)
        topf = sd("topf", [P, NT, NE])
        which = sd("which", [P, NE])
        rt = sd("rt", [P, 4, NT])
        oh = sd("oh", [P, 2, NT, NE])
        we = sd("we", [P, NT, NE])
        D.close()

        x_in = sem("x_in")
        small_in = sem("small_in")
        wc_in, wg_in, wo_in, x_again = (sem(s) for s in ("wc_in", "wg_in", "wo_in", "x_again"))
        wc_hi, wc_lo, wg_hi, wg_lo, wo_hi, wo_lo, wo_scaled, wdt_hi, wdt_lo = (sem(s) for s in (
            "wc_hi", "wc_lo", "wg_hi", "wg_lo", "wo_hi", "wo_lo", "wo_scaled", "wdt_hi", "wdt_lo"))
        ynT_lo, wc_lo2 = sem("ynT_lo"), sem("wc_lo2")
        consts = sem("consts")
        nsem = {w: sem(f"norm_{w}") for w in ("dve", "var0", "var1", "rstd0", "rstd1", "out", "x", "xn", "tr", "hi", "lo")}
        dt_t, dt_tr, lg_t, lg_tr = (sem(s) for s in ("dt_t", "dt_tr", "lg_t", "lg_tr"))
        dt_ps, dt_dve, dt_act, dt_cum = sem("dt_ps"), sem("dt_dve"), sem("dt_act"), sem("dt_cum")
        par_ready, cur_ready = sem("par_ready"), sem("cur_ready")
        acc_clear = sem("acc_clear")
        h_ready, tap0, taps, tanh_ready, xbc_ready = (sem(s) for s in ("h_ready", "tap0", "taps", "tanh_ready", "xbc_ready"))
        ah_ready, a_ready, x_out, ynT_hi, grown_ready = (sem(s) for s in ("ah_ready", "a_ready", "x_out", "ynT_hi", "grown_ready"))
        x_tr, gb_ready, gb_used, d_ready, e_ready = (sem(s) for s in ("x_tr", "gb_ready", "gb_used", "d_ready", "e_ready"))
        am_ready, xd_ready, xdec_ready, dtx_ready, sdec_ready = (sem(s) for s in ("am_ready", "xd_ready", "xdec_ready", "dtx_ready", "sdec_ready"))
        m_ready, yo_ready, yo_used, yi_ready, y_part, y_ready = (sem(s) for s in ("m_ready", "yo_ready", "yo_used", "yi_ready", "y_part", "y_ready"))
        st_ready, state_ready, ss_ready, ssv_ready, rg_ready = (sem(s) for s in ("st_ready", "state_ready", "ss_ready", "ssv_ready", "rg_ready"))
        gate_ready, tg_ready, gate_used, yn_ready, yn_tr, o_ready, out_added = (sem(s) for s in ("gate_ready", "tg_ready", "gate_used", "yn_ready", "yn_tr", "o_ready", "out_added"))

        gu_in, dn_in, gu_cast, dn_cast, f_small, f_scaled, f_dve, f_clear, fsc_ready = (sem(s) for s in ("gu_in", "dn_in", "gu_cast", "dn_cast", "f_small", "f_scaled", "f_dve", "f_clear", "fsc_ready"))
        hid_f, hid_hi = sem("hid_f"), sem("hid_hi")
        gate_ps, up_ps, f_tanh, f_part, hid_ready, down_ps, down_added = (sem(s) for s in ("gate_ps", "up_ps", "f_tanh", "f_part", "hid_ready", "down_ps", "down_added"))

        a_small, aq_in, awr_in, v_ps, v_f, v_hi, v_ready, sel_ready = (sem(s) for s in (
            "a_small", "aq_in", "awr_in", "v_ps", "v_f", "v_hi", "v_ready", "sel_ready"))
        osum_ready = sem("osum_ready")
        aw_hi, aw_lo, aq_hi, aq_lo = (sem(s) for s in ("aw_hi", "aw_lo", "aq_hi", "aq_lo"))
        abo_in = sem("abo_in")
        qk_ps, qk_h, qk_l, st_ps, st_out = (sem(s) for s in ("qk_ps", "qk_h", "qk_l", "st_ps", "st_out"))
        st_out2, bias_ready = sem("st_out2"), sem("bias_ready")
        s_ready, max_ready, exp_ready, pt_ps, pt_hi, pt_lo, pv_ps, prec_ready, att_ready = (sem(s) for s in (
            "s_ready", "max_ready", "exp_ready", "pt_ps", "pt_hi", "pt_lo", "pv_ps", "prec_ready", "att_ready"))
        at_ps, at_hi, at_lo, ao_ps, ao_ready = (sem(s) for s in ("at_ps", "at_hi", "at_lo", "ao_ps", "ao_ready"))

        r_in, lg_ps, r_dve, r_act, r_iota, d_clear, ex_ps, ex_added = (sem(s) for s in ("r_in", "lg_ps", "r_dve", "r_act", "r_iota", "d_clear", "ex_ps", "ex_added"))
        ew_in = [sem("ew_in0"), sem("ew_in1")]
        e_hi, e_lo, rw_hi, rw_lo = (sem(s) for s in ("e_hi", "e_lo", "rw_hi", "rw_lo"))
        stored = sem("stored")

        block = ctx.enter_context(nc.Block())

        def tile_done(eng, q, i):
            if q == 1:
                eng.wait_ge(out_added, (G - 1) * NT + i + 1)
            elif q == 2:
                eng.wait_ge(f_scaled, i + 1)
            elif q == 3:
                eng.wait_ge(ao_ready, i + 1)
            elif q == 4:
                eng.wait_ge(ex_added, NE * NT + i + 1)

        def norm_wait(eng, q, what, n):
            eng.wait_ge(nsem[what], NT * (q - 1 if what in ("var0", "rstd0", "out", "x") else q) + n)

        norm_steps = Count(nsem["dve"])

        def conv_stage(group):
            t = xbc[:, :, :].rearrange("p a b -> p (a b)") if group == 0 else x[:, :, :].rearrange("p a b -> p (a b)")
            return t[:, 0:KT * CT * P].rearrange("p (k c) -> p k c", k=KT)

        gate_stage, out_stage = x[:, 0:KT, :], x[:, KT:2 * KT, :]

        def pair(ap):
            return ap.rearrange("p (h c) -> p h c", h=HG)

        def products(o, terms, first=True, last=True):
            terms = [t for ah, al, bh, bl in terms for t in ((ah, bh), (ah, bl), (al, bh))]
            for n, (a, b) in enumerate(terms):
                m = nc.tensor.matmul(o, a, b, start=first and n == 0, stop=last and n == len(terms) - 1)
            return m

        def low(eng, o, full, high):
            return eng.tensor_tensor(o, full, high.bitcast(F32), ALU.subtract)

        def hid_part(t, q):
            return t[:, q % 2, q // 2 * L:(q // 2 + 1) * L]

        def conv_tiles(s, last):
            if s in (0, 1, 2):
                return (CT + 2 * s, CT + 2 * s + 1)
            if s in (4, 5, 6) and not last:
                return (NB * CT + 2 * (s - 4), NB * CT + 2 * (s - 4) + 1)
            return ()

        CONV_BANKS = (0, 2)

        def conv_made(g, s, last):
            return NB * CT * g + CT + sum(len(conv_tiles(r, last)) for r in range(s))

        def entered(g, i):
            return (CH - 1) * NB * g + (CH - 1) * (i // CH)

        UNITS = 16 * NB
        PREP = {0: 0, 2: 1, 4: 2, 5: 3, 6: 4, 7: 5, 9: 6, 10: 7, 12: 8, 14: 9}

        def stacked(b, n):
            return (qs, ks)[n // 4][:, b, n % 4, :]

        def passes_ahead(t, s, last):
            piece = PREP.get(s % 16) if s < UNITS else None
            if piece is None or (last and s >= 16):
                return None
            return ((t, 1) if s < 16 else (t + 1, 0)) + (piece,)

        def group_steps(eng, step):
            for s in range(NT):
                step(0, s, True, False)
            with eng.Fori(1, G - 1) as g:
                for s in range(NT):
                    step(g, s, False, False)
            for s in range(NT + 2):
                step(G - 1, s, False, True)

        def heads(row):
            return cur[:, row, :].unsqueeze(2).to_broadcast([P, HG, HP])

        @block.sync
        def _(sp):
            for i in range(NT):
                sp.dma_start(x[:, i, :], hidden[i * P:(i + 1) * P, :]).then_inc(x_in, 16)
            sp.dma_start(wdt[:, :, :], w_dt).then_inc(small_in, 16)
            sp.dma_start(bcast[:, 0, :], dt_bias.partition_broadcast(P)).then_inc(small_in, 16)
            sp.dma_start(bcast[:, 1, :], A_log.partition_broadcast(P)).then_inc(small_in, 16)
            sp.dma_start(per[:, 5 * NT, :], Dskip.partition_broadcast(P)).then_inc(small_in, 16)
            sp.dma_start(par[:, :, 0:CT * KC], conv_w).then_inc(small_in, 16)
            sp.dma_start(par[:, :, CT * KC:CT * KC + CT], conv_b).then_inc(small_in, 16)
            sp.dma_start(par[:, :, CT * KC + CT:], norm_w).then_inc(small_in, 16)
            sp.dma_start(conv_stage(0), w_conv[0]).then_inc(wc_in, 16)
            norm_wait(sp, 0, "xn", NT)
            sp.dma_start(gate_stage, w_gate[0]).then_inc(wg_in, 16)
            sp.dma_start(out_stage, w_out[0]).then_inc(wo_in, 16)
            with sp.Fori(0, G - 1) as g:
                sp.wait_ge(wg_lo, KT * g + KT)
                sp.wait_ge(wo_lo, KT * g + KT)
                sp.dma_start(conv_stage(1), w_conv[bass.ds(g + 1, 1)]).then_inc(wc_in, 16)
                sp.wait_ge(wc_lo, 2 * g + KT + 2)
                sp.wait_ge(wc_lo2, 2 * g + KT + 2)
                sp.dma_start(gate_stage, w_gate[bass.ds(g + 1, 1)]).then_inc(wg_in, 16)
                sp.dma_start(out_stage, w_out[bass.ds(g + 1, 1)]).then_inc(wo_in, 16)
            sp.wait_ge(wg_lo, KT * G)
            sp.wait_ge(wo_lo, KT * G)
            for i in range(NT):
                sp.dma_start(x[:, i, :], hidden[i * P:(i + 1) * P, :]).then_inc(x_again, 16)
            if STAGES >= 2:
                sp.wait_ge(h_ready, NB * CT * G)
                sp.dma_start(gur[:, :, :, :, :], ff_gu[0]).then_inc(gu_in, 16)
                sp.dma_start(dnr[:, :, :], ff_dn[0]).then_inc(dn_in, 16)
                tile_done(sp, 1, NT - 1)
                sp.dma_start(gus[:, 0, :], gate_s).then_inc(f_small, 16)
                sp.dma_start(gus[:, 1, :], up_s).then_inc(f_small, 16)
                sp.dma_start(dsb[:, :], down_s.partition_broadcast(P)).then_inc(f_small, 16)
                with sp.Fori(0, FP - 1) as f:
                    sp.wait_ge(gu_cast, KT * f + KT)
                    sp.dma_start(gur[:, :, :, :, :], ff_gu[bass.ds(f + 1, 1)]).then_inc(gu_in, 16)
                    sp.wait_ge(dn_cast, 2 * f + 2)
                    sp.dma_start(dnr[:, :, :], ff_dn[bass.ds(f + 1, 1)]).then_inc(dn_in, 16)
            if STAGES >= 3:
                sp.wait_ge(down_ps, NT * FP)
                sp.dma_start(awr, wv).then_inc(awr_in, 16)
                sp.dma_start(aqr[:, 0, :, :], wq[0]).then_inc(aq_in, 16)
                sp.dma_start(aqr[:, 1, :, :], wk[0]).then_inc(aq_in, 16)
                sp.dma_start(abqk[:, :, :], bqk).then_inc(a_small, 16)
                sp.dma_start(abv[:, :], bv.partition_broadcast(P)).then_inc(a_small, 16)
                sp.wait_ge(aw_lo, KT)
                sp.dma_start(awr, wo).then_inc(awr_in, 16)
                sp.wait_ge(v_f, NT)
                sp.dma_start(abo[:, :], bo.partition_broadcast(P)).then_inc(abo_in, 16)
                with sp.Fori(0, AT - 1) as t:
                    sp.wait_ge(aq_lo, 2 * t + 2)
                    sp.dma_start(aqr[:, 0, :, :], wq[bass.ds(t + 1, 1)]).then_inc(aq_in, 16)
                    sp.dma_start(aqr[:, 1, :, :], wk[bass.ds(t + 1, 1)]).then_inc(aq_in, 16)
            if STAGES >= 4:
                sp.wait_ge(s_ready, 16 * NB * AT)
                sp.dma_start(rw[:, :, :], gate_w).then_inc(r_in, 16)
                sp.dma_start(ew[:, 0, :, :], expert_w[0]).then_inc(ew_in[0], 16)
                sp.dma_start(ew[:, 1, :, :], expert_w[1]).then_inc(ew_in[1], 16)
                with sp.Fori(0, NE // 2 - 1) as e:
                    for s in range(2):
                        sp.wait_ge(e_lo, 2 * KT * e + KT * (s + 1))
                        sp.dma_start(ew[:, s, :, :], expert_w[bass.ds(2 * e + 2 + s, 1)]).then_inc(ew_in[s], 16)
            for i in range(NT):
                norm_wait(sp, STAGES, "x", i + 1)
                sp.dma_start(out[i * P:(i + 1) * P, :], x[:, i, :]).then_inc(stored, 16)
            sp.wait_ge(stored, 16 * NT)

        def norm_round(q, n):
            d = norm_steps
            moments = []
            lag = 2 if q else 0
            if q and n < NT:
                tile_done(nc.vector, q, n)
                d.inc(nc.vector.bn_stats(stats[:, 0, n, :], acc[:, n, :]))
                moments.append((0, n))
            i = n - lag
            if q < STAGES and 0 <= i < NT:
                nc.vector.wait_ge(x_in, 16 * NT) if q == 0 else norm_wait(nc.vector, q, "x", i + 1)
                d.inc(nc.vector.bn_stats(stats[:, 1, i, :], x[:, i, :]))
                moments.append((1, i))
            at = d.n
            i = n - 1
            if q and 0 <= i < NT:
                norm_wait(nc.vector, q, "rstd0", i + 1)
                nc.vector.tensor_scalar(acc[:, i, :], acc[:, i, :], mv[:, 0, i, 0:1], rs[:, 0, i:i + 1],
                                        ALU.subtract, ALU.mult).then_inc(nsem["out"], 1)
            i = n - lag - 1
            if q < STAGES and 0 <= i < NT:
                norm_wait(nc.vector, q, "rstd1", i + 1)
                nc.vector.tensor_scalar(acc[:, i, :], x[:, i, :], mv[:, 1, i, 0:1], rs[:, 1, i:i + 1],
                                        ALU.subtract, ALU.mult).then_inc(nsem["xn"], 1)
            if moments:
                nc.vector.wait_ge(d.sem, at)
                for w, i in moments:
                    at = d.inc(nc.vector.bn_aggr(mv[:, w, i, :], stats[:, w, i, :]))
                nc.vector.wait_ge(d.sem, at)
                for w, i in moments:
                    nc.vector.tensor_scalar(ve[:, w, i:i + 1], mv[:, w, i, 1:2], EPS, None,
                                            ALU.add).then_inc(nsem[("var0", "var1")[w]], 1)

        ROUNDS = NT + 3

        def norm_low(q, i):
            norm_wait(nc.vector, q, "hi", i + 1)
            low(nc.vector, xTl[:, :, i * P:(i + 1) * P], bk(i % 2).rearrange("p (k t) -> p k t", k=KT),
                xTh[:, :, i * P:(i + 1) * P]).then_inc(nsem["lo"], 1)

        def norm_vector(q, start=0):
            lag, made = 4 if q else 2, 0
            for n in range(start, NT + lag):
                norm_round(q, n)
                while q < STAGES and made <= n - lag and made < (NT if n == NT + lag - 1 else 2 * (n - start) + 2):
                    norm_low(q, made)
                    made += 1

        def norm_pool(q, n):
            i = n - 1
            if q and n < NT:
                norm_wait(nc.gpsimd, q, "var0", n + 1)
                nc.gpsimd.tensor_tensor(rs[:, 0, n:n + 1], ve[:, 0, n:n + 1], mhalf[:, 0:1], ALU.pow).then_inc(nsem["rstd0"], 1)
            if q and 0 <= i < NT:
                norm_wait(nc.gpsimd, q, "out", i + 1)
                nc.gpsimd.tensor_tensor(x[:, i, :], x[:, i, :], acc[:, i, :], ALU.add).then_inc(nsem["x"], 1)
            i = n - 2 if q else n
            if q < STAGES and 0 <= i < NT:
                norm_wait(nc.gpsimd, q, "var1", i + 1)
                nc.gpsimd.tensor_tensor(rs[:, 1, i:i + 1], ve[:, 1, i:i + 1], mhalf[:, 0:1], ALU.pow).then_inc(nsem["rstd1"], 1)

        def norm_tensor(q):
            for i in range(NT):
                norm_wait(nc.tensor, q, "xn", i + 1)
                if i >= 2:
                    norm_wait(nc.tensor, q, "lo", i - 1)
                for k in range(KT):
                    mmi = nc.tensor.transpose(bk(i % 2)[:, k * P:(k + 1) * P], acc[:, i, k * P:(k + 1) * P], ident[:, :])
                mmi.then_inc(nsem["tr"], 1)

        def norm_scalar(q):
            for i in range(NT):
                norm_wait(nc.scalar, q, "tr", i + 1)
                nc.scalar.copy(xTh[:, :, i * P:(i + 1) * P],
                               bk(i % 2).rearrange("p (k t) -> p k t", k=KT)).then_inc(nsem["hi"], 1)

        @block.gpsimd
        def _(pool):
            pool.memset(ones[:, :], 1.0).then_inc(consts, 1)
            pool.memset(mhalf[:, :], -0.5).then_inc(consts, 1)
            pool.memset(epsc[:, :], EPS).then_inc(consts, 1)
            pool.wait_ge(consts, 3)
            pool.affine_select(out=ident[:, :], in_=ones[:, :], compare_op=ALU.is_equal, fill=0.0, base=0,
                               pattern=[[-1, P]], channel_multiplier=1).then_inc(consts, 1)
            pool.affine_select(out=upto[:, :], in_=ones[:, :], compare_op=ALU.is_ge, fill=0.0, base=0,
                               pattern=[[1, P]], channel_multiplier=-1).then_inc(consts, 1)
            pool.affine_select(out=after[:, :], in_=ones[:, :], compare_op=ALU.is_gt, fill=0.0, base=0,
                               pattern=[[-1, P]], channel_multiplier=1).then_inc(consts, 1)
            for n in range(NT):
                norm_pool(0, n)
            def decays(i):
                for part, a in enumerate((ah, al)):
                    m = pool.tensor_tensor(am[:, part, :, :], a[:, i, :].bitcast(F32).unsqueeze(2).to_broadcast([P, HG, P]),
                                           upto[:, :].unsqueeze(1).to_broadcast([P, HG, P]), ALU.mult)
                m.then_inc(am_ready, 1)

            pool.wait_ge(consts, 6)
            for k in range(KT):
                pool.wait_ge(wc_hi, k + 1)
                low(pool, wcl[:, k, :], conv_stage(0)[:, k, :], wch[:, k, :]).then_inc(wc_lo, 1)
            norm_wait(pool, 0, "tr", NT)
            pool.memset(acc[:, :, :], 0.0).then_inc(acc_clear, 1)

            def step(g, s, first, last):
                if s < NT and not (last and s == NT - 1):
                    pool.wait_ge(d_ready, NT * g + s + 1)
                    if s == NT - 1:
                        pool.wait_ge(ah_ready, g + 2)
                    decays((s + 1) % NT)
                if s == 2:
                    for k in range(KT):
                        pool.wait_ge(wo_hi, KT * g + k + 1)
                        low(pool, wol[:, k, :], out_stage[:, k, :], woh[:, k, :]).then_inc(wo_lo, 1)
                i = s - 1
                c = i % CH
                if s >= 1 and 1 <= c < CH - 1:
                    pool.wait_ge(yo_ready, entered(g, i) + c)
                    pool.tensor_tensor(pair(state[:, :]), pair(state[:, :]), heads(4 * NT + i),
                                       ALU.mult).then_inc(sdec_ready, 1)
                if s == 0:
                    pool.wait_ge(cur_ready, g + 1)
                if s < NT:
                    pool.wait_ge(x_out, NT * g + s + 1)
                    src = pair(xtok[:, s % 2, :])
                    if not (first and s == 0):
                        pool.wait_ge(yi_ready, NT * g + s)
                    pool.tensor_tensor(pair(dtx[:, :]), src, heads(NT + s), ALU.mult).then_inc(dtx_ready, 1)
                    if s % CH < CH - 1:
                        m = entered(g, s) + s % CH
                        if not (first and s == 0):
                            pool.wait_ge(st_ready, m)
                        pool.tensor_tensor(pair(xdec[:, :]), src, heads(3 * NT + s), ALU.mult).then_inc(xdec_ready, 1)
                if s < NT:
                    if not (first and s == 0):
                        pool.wait_ge(y_ready, NT * g + s)
                    pool.tensor_tensor(pair(xd[:, :]), src, heads(5 * NT), ALU.mult).then_inc(xd_ready, 1)
                if not (first and s == 0) and s <= NT:
                    n = NT * g + s
                    pool.wait_ge(ss_ready, n)
                    pool.tensor_tensor(ssv[:, i % 2:i % 2 + 1], ss[:, i % 2:i % 2 + 1], epsc[:, :],
                                       ALU.add).then_inc(ssv_ready, 1)
                    pool.wait_ge(ssv_ready, n)
                    pool.tensor_tensor(rg[:, i % 2:i % 2 + 1], ssv[:, i % 2:i % 2 + 1], mhalf[:, 0:1],
                                       ALU.pow).then_inc(rg_ready, 1)
                if s == 3 and not last:
                    for k in (2, 3):
                        pool.wait_ge(wc_hi, KT * g + KT + k + 1)
                        low(pool, wcl[:, k, :], conv_stage(1)[:, k, :], wch[:, k, :]).then_inc(wc_lo, 1)
                if s == NT - 1 and not last:
                    gate_low(g + 1)
                if last and s >= 3:
                    if s == 3:
                        pool.wait_ge(x_again, 16 * NT)
                    norm_pool(1, s - 3)

            def gate_low(g):
                for k in range(KT):
                    pool.wait_ge(wg_hi, KT * g + k + 1)
                    low(pool, wgl[:, k, :], gate_stage[:, k, :], wgh[:, k, :]).then_inc(wg_lo, 1)

            pool.wait_ge(ah_ready, 1)
            decays(0)
            gate_low(0)
            group_steps(pool, step)
            for n in range(NT - 1, ROUNDS):
                norm_pool(1, n)
            if STAGES >= 2:
                norm_wait(pool, 1, "tr", NT)
                pool.memset(acc[:, :, :], 0.0).then_inc(f_clear, 1)
                for n in range(-2, ROUNDS):
                    if n >= 0:
                        norm_pool(2, n)
                    i = n + 2
                    if i < NT:
                        pool.wait_ge(down_added, 4 + NT * (FP - 1) + i + 1)
                        pool.tensor_tensor(acc[:, i, :], acc[:, i, :], dsb[:, :], ALU.mult).then_inc(f_scaled, 1)
            if STAGES >= 3:
                pool.memset(futf[:, :], 0.0).then_inc(sel_ready, 1)
                pool.wait_ge(sel_ready, 1)
                pool.affine_select(out=futf[:, :], in_=futf[:, :], compare_op=ALU.is_ge, fill=-1e30, base=0,
                                   pattern=[[-1, P]], channel_multiplier=1).then_inc(sel_ready, 1)
                for k in range(KT):
                    pool.wait_ge(aw_hi, k + 1)
                    low(pool, awl[:, k, :], awr[:, k, :], awh[:, k, :]).then_inc(aw_lo, 1)
                for t in range(AT):
                    for w in range(2):
                        pool.wait_ge(aq_hi, 2 * t + w + 1)
                        low(pool, aql[:, w, :, :], aqr[:, w, :, :], aqh[:, w, :, :]).then_inc(aq_lo, 1)
                    if t == 0:
                        for k in range(KT):
                            pool.wait_ge(aw_hi, KT + k + 1)
                            low(pool, awl[:, k, :], awr[:, k, :], awh[:, k, :]).then_inc(aw_lo, 1)
                for n in range(ROUNDS):
                    norm_pool(3, n)
            if STAGES >= 4:
                norm_wait(pool, 3, "tr", NT)
                pool.wait_ge(rw_hi, 1)
                low(pool, rwl[:, :, :], rw[:, :, :], rwh[:, :, :]).then_inc(rw_lo, 1)
                pool.iota(which[:, :], pattern=[[1, NE]], base=0, channel_multiplier=0,
                          allow_small_or_imprecise_dtypes=True).then_inc(r_iota, 1)
                pool.memset(acc[:, :, :], 0.0).then_inc(d_clear, 1)
                with pool.Fori(0, NE // 2) as e:
                    for s in range(2):
                        for k in range(KT):
                            pool.wait_ge(e_hi, 2 * KT * e + KT * s + k + 1)
                            low(pool, ewl[:, s, k, :], ew[:, s, k, :], ewh[:, s, k, :]).then_inc(e_lo, 1)
                for n in range(ROUNDS):
                    norm_pool(4, n)

        @block.scalar
        def _(act):
            act.wait_ge(wc_in, 16)
            for k in range(KT):
                nc.scalar.copy(wch[:, k, :], conv_stage(0)[:, k, :]).then_inc(wc_hi, 1)
            act.wait_ge(small_in, 16 * 7)
            nc.scalar.copy(wdth, wdt).then_inc(wdt_hi, 1)
            norm_scalar(0)
            def first_tap(n, q):
                act.wait_ge(h_ready, n + 1)
                if not (isinstance(n, int) and n < 2):
                    act.wait_ge(xbc_ready, n - 1)
                nc.scalar.activation(tap[:, q % 2, :], bk(CONV_BANKS[q % 2]), ACT.Identity,
                                     bias=parg[:, CT * KC + q:CT * KC + q + 1],
                                     scale=parg[:, KC * q + KC - 1:KC * q + KC]).then_inc(tap0, 1)

            def tanh(n, q):
                act.wait_ge(taps, 3 * n + 3)
                if not (isinstance(n, int) and n < 1):
                    act.wait_ge(xbc_ready, n)
                nc.scalar.activation(th[:, :], tap[:, q % 2, :], ACT.Tanh).then_inc(tanh_ready, 1)

            def step(g, s, first, last):
                n0 = NB * CT * g
                tiles = conv_tiles(s, last)
                if s == 4 and tiles:
                    act.wait_ge(par_ready, g + 2)
                if s == 2:
                    if not first:
                        act.wait_ge(o_ready, NT * g)
                    act.wait_ge(wo_scaled, KT * g + KT)
                    for k in range(KT):
                        nc.scalar.copy(woh[:, k, :], out_stage[:, k, :]).then_inc(wo_hi, 1)
                if s < NT:
                    act.wait_ge(x_tr, NT * g + s + 1)
                    if not (first and s < 2):
                        act.wait_ge(xd_ready, NT * g + s - 1)
                    nc.scalar.copy(xtok[:, s % 2, :], bk(4)).then_inc(x_out, 1)
                if s == 3 and not last:
                    act.wait_ge(wc_in, 16 * g + 32)
                    for k in (0, 1):
                        nc.scalar.copy(wch[:, k, :], conv_stage(1)[:, k, :]).then_inc(wc_hi, 1)
                if s < NT:
                    act.wait_ge(d_ready, NT * g + s + 1)
                    nc.scalar.activation(em[:, s % 2, :, :], banks[:, 2:4, :].rearrange("p b (h t) -> p (b h) t", t=P),
                                         ACT.Exp).then_inc(e_ready, 1)
                if s == 3 and not last:
                    act.wait_ge(wc_in, 16 * g + 32)
                    for k in (2, 3):
                        nc.scalar.copy(wch[:, k, :], conv_stage(1)[:, k, :]).then_inc(wc_hi, 1)
                if tiles:
                    first_tap(n0 + tiles[0], tiles[0] % CT)
                if not (first and s < 2):
                    act.wait_ge(yn_tr, NT * g + s - 1)
                    nc.scalar.copy(ynTh[:, :], bk(4)).then_inc(ynT_hi, 1)
                if tiles:
                    tanh(n0 + tiles[0], tiles[0] % CT)
                    first_tap(n0 + tiles[1], tiles[1] % CT)
                if not (first and s == 0) and s <= NT:
                    act.wait_ge(y_ready, NT * g + s)
                    nc.scalar.activation(sg[:, s % 2, :], y[:, :], ACT.Square, scale=float(GI) ** -0.5,
                                         accum_out=ss[:, (s - 1) % 2:(s - 1) % 2 + 1]).then_inc(ss_ready, 1)
                if s < NT:
                    if not (first and s == 0):
                        act.wait_ge(ss_ready, NT * g + s)
                    act.wait_ge(gate_ready, NT * g + s + 1)
                    nc.scalar.activation(sg[:, s % 2, :], bk(0), ACT.Tanh, scale=0.5).then_inc(tg_ready, 1)
                if tiles:
                    tanh(n0 + tiles[1], tiles[1] % CT)
                if s == NT - 1 and not last:
                    gate_high(g + 1)

            def gate_high(g):
                act.wait_ge(wg_in, 16 * g + 16)
                for k in range(KT):
                    nc.scalar.copy(wgh[:, k, :], gate_stage[:, k, :]).then_inc(wg_hi, 1)
                act.wait_ge(wo_in, 16 * g + 16)
                for k in range(KT):
                    nc.scalar.activation(out_stage[:, k, :], out_stage[:, k, :], ACT.Copy,
                                         scale=parg[:, CT * KC + CT + k:CT * KC + CT + k + 1]).then_inc(wo_scaled, 1)

            for b in range(NB):
                act.wait_ge(dt_ps, b + 1)
                nc.scalar.copy(sg[0:H, b, :], bk(5 + b)[0:H, :]).then_inc(dt_t, 1)
            act.wait_ge(par_ready, 1)
            first_tap(0, 0)
            act.wait_ge(dt_dve, 3)
            nc.scalar.activation(z[:, 2, :], z[:, 1, :], ACT.Exp).then_inc(dt_act, 1)
            nc.scalar.activation(bcast[:, 1, :], bcast[:, 1, :], ACT.Exp).then_inc(dt_act, 1)
            act.wait_ge(dt_act, 1)
            nc.scalar.activation(z[:, 1, :], z[:, 2, :], ACT.Ln, bias=1.0).then_inc(dt_act, 1)
            first_tap(1, 1)
            tanh(0, 0)
            for n, row in enumerate((2, 3, 4)):
                act.wait_ge(dt_cum, n + 1)
                nc.scalar.activation(per[:, row * NT:(row + 1) * NT, :],
                                     bk(3 + n).rearrange("p (c h) -> p c h", c=NT), ACT.Exp).then_inc(dt_act, 1)
            for q in range(1, CT):
                if q + 1 < CT:
                    first_tap(q + 1, q + 1)
                tanh(q, q)
            gate_high(0)
            group_steps(act, step)
            norm_scalar(1) if STAGES >= 2 else None
            if STAGES >= 2:
                def hidden_pair(f):
                    act.wait_ge(up_ps, 4 * f + 1)
                    act.wait_ge(gu_in, 16 * f + 16)
                    for k in range(KT):
                        nc.scalar.copy(gu[:, k, :, :, :], gur[:, k, :, :, :]).then_inc(gu_cast, 1)
                    act.wait_ge(fsc_ready, f + 1)
                    for q in range(4):
                        act.wait_ge(gate_ps, 4 * f + q + 1)
                        nc.scalar.activation(fth[:, q % 2, :], bk(q % 2), ACT.Tanh,
                                             scale=fscg[:, 0, q % 2:q % 2 + 1]).then_inc(f_tanh, 1)
                        if q == 2:
                            act.wait_ge(dn_in, 16 * f + 16)
                            for k in range(2):
                                nc.scalar.copy(dn[:, k, :], dnr[:, k, :]).then_inc(dn_cast, 1)
                        if q % 2:
                            for r in (q - 1, q):
                                act.wait_ge(hid_f, 4 * f + r + 1)
                                nc.scalar.copy(hid_part(hidh, r), hidf[:, r % 2, :]).then_inc(hid_hi, 1)

                with act.Fori(0, FP) as f:
                    hidden_pair(f)
            if STAGES >= 3:
                def weights(t):
                    act.wait_ge(qk_ps, 4 * t) if not isinstance(t, int) else None
                    act.wait_ge(aq_in, 32 * t + 32)
                    for w in range(2):
                        nc.scalar.copy(aqh[:, w, :, :], aqr[:, w, :, :]).then_inc(aq_hi, 1)

                act.wait_ge(awr_in, 16)
                for k in range(KT):
                    nc.scalar.copy(awh[:, k, :], awr[:, k, :]).then_inc(aw_hi, 1)
                weights(0)
                norm_scalar(2)
                def prepare(t, b, piece):
                    m = NB * t + b
                    if piece < 2:
                        if piece == 0:
                            act.wait_ge(bias_ready, t + 1)
                        act.wait_ge(qk_ps, 2 * m + piece + 1)
                        nc.scalar.activation(qh[:, piece, :], bk(7), ACT.Identity,
                                             bias=abg[:, piece:piece + 1]).then_inc(qk_h, 1)
                    elif piece % 2 == 0:
                        act.wait_ge(st_ps, 8 * m + piece - 1)
                        nc.scalar.copy(stacked(b, piece - 2), bk(7)).then_inc(st_out, 1)

                def tile(t, last):
                    for s in range(UNITS + 2):
                        w = s - 2
                        if w >= 0:
                            kw = (w % 16 // 4 + 1) * P
                            for j in range(2):
                                act.wait_ge(pt_ps, 2 * UNITS * t + 2 * w + j + 1)
                                nc.scalar.copy(pTh[:, w % 2, j, 0:kw], bk(4 + j)[:, 0:kw]).then_inc(pt_hi, 1)
                        if s < UNITS:
                            gq, qi = s // 4, s % 16 // 4
                            kw = (qi + 1) * P
                            act.wait_ge(max_ready, UNITS * t + s + 1)
                            if s % 4 == 0:
                                act.wait_ge(prec_ready, 8 * t + gq + 1)
                            for j in range(2):
                                e = nc.scalar.activation(prob[:, s % 2, j, 0:kw], bk(2 * (s % 2) + j)[:, 0:kw], ACT.Exp,
                                                         bias=nmax[:, s % 2, j:j + 1],
                                                         accum_out=psum[:, gq % 2, 2 * (s % 4) + j:2 * (s % 4) + j + 1])
                            e.then_inc(exp_ready, 1)
                        ahead = passes_ahead(t, s, last)
                        if ahead:
                            prepare(*ahead)
                        if s == 6 and not last:
                            weights(t + 1)

                for i in range(10):
                    if i < NT:
                        act.wait_ge(v_f, i + 1)
                        nc.scalar.copy(v[:, i, :, 0, :], vf[:, i % 2, :].rearrange("p (h d) -> p h d", d=HD)).then_inc(v_hi, 1)
                    prepare(0, 0, i)
                    if i == NT - 1:
                        act.wait_ge(awr_in, 32)
                        for k in range(KT):
                            nc.scalar.copy(awh[:, k, :], awr[:, k, :]).then_inc(aw_hi, 1)
                act.wait_ge(aw_lo, 2 * KT)
                with act.Fori(0, AT - 1) as t:
                    tile(t, False)
                tile(AT - 1, True)
                for i in range(NT):
                    act.wait_ge(at_ps, i + 1)
                    nc.scalar.copy(attTh[:, i % 2, :], bk(i % 2)).then_inc(at_hi, 1)
            if STAGES >= 4:
                act.wait_ge(r_in, 16)
                nc.scalar.copy(rwh[:, :, :], rw[:, :, :]).then_inc(rw_hi, 1)
                for s in range(2):
                    act.wait_ge(ew_in[s], 16)
                    for k in range(KT):
                        nc.scalar.copy(ewh[:, s, k, :], ew[:, s, k, :]).then_inc(e_hi, 1)
                norm_scalar(3)
                for b in range(NB):
                    act.wait_ge(lg_ps, b + 1)
                    nc.scalar.copy(lgT[0:NE, b, :], bk(b)[0:NE, :]).then_inc(lg_t, 1)
                act.wait_ge(r_dve, 2 + 2 * NT)
                nc.scalar.activation(rt[:, 1, :], rt[:, 0, :], ACT.Exp).then_inc(r_act, 1)
                with act.Fori(0, NE // 2 - 1) as e:
                    for s in range(2):
                        act.wait_ge(ex_ps, 2 * NT * e + NT * (s + 1))
                        act.wait_ge(ew_in[s], 16 * e + 32)
                        for k in range(KT):
                            nc.scalar.copy(ewh[:, s, k, :], ew[:, s, k, :]).then_inc(e_hi, 1)

        @block.vector
        def _(dve):
            def taps_of(g):
                nc.vector.tensor_copy(parg[:, :], par[:, bass.ds(g, 1), :].rearrange("p a b -> p (a b)")).then_inc(par_ready, 1)

            def decays_of(g):
                a = per[:, 0:NT, bass.ds(HG * g, HG)]
                nc.vector.tensor_copy(ah[:, :, :], a).then_inc(a_ready, 1)
                dve.wait_ge(a_ready, g + 1)
                low(nc.vector, al[:, :, :], a, ah[:, :, :]).then_inc(ah_ready, 1)

            def convolve(n, q):
                dve.wait_ge(tap0, n + 1)
                for k in range(KC - 2, -1, -1):
                    sh = KC - 1 - k
                    if sh > 1:
                        dve.wait_ge(taps, 3 * n + sh - 1)
                    nc.vector.scalar_tensor_tensor(tap[:, q % 2, sh:L], bk(CONV_BANKS[q % 2])[:, 0:L - sh],
                                                   parg[:, KC * q + k:KC * q + k + 1],
                                                   tap[:, q % 2, sh:L], ALU.mult, ALU.add).then_inc(taps, 1)

            def silu(n, q, b):
                dve.wait_ge(tanh_ready, n + 1)
                nc.vector.scalar_tensor_tensor(xbc[:, q, b * L:(b + 1) * L], th[:, :], 1.0,
                                               tap[:, q % 2, :], ALU.add, ALU.mult).then_inc(xbc_ready, 1)

            dve.sem_inc(wc_lo2, KT)
            norm_vector(0)
            dve.wait_ge(wdt_hi, 1)
            low(nc.vector, wdtl, wdt, wdth).then_inc(wdt_lo, 1)
            dve.wait_ge(small_in, 16 * 7)
            dve.wait_ge(consts, 6)
            d = Count(dt_dve)

            def chain(ins):
                d.inc(ins)
                dve.wait_ge(dt_dve, d.n)

            chain(nc.vector.tensor_scalar(par[:, :, :], par[:, :, :], 0.5, None, ALU.mult))
            taps_of(0)
            dve.wait_ge(dt_tr, 1)
            chain(nc.vector.tensor_tensor(z[:, 0, :].rearrange("p (c h) -> p c h", c=NT),
                                          bk(7).rearrange("p (c h) -> p c h", c=NT),
                                          bcast[:, 0, :].unsqueeze(1).to_broadcast([P, NT, H]), ALU.add))
            chain(nc.vector.scalar_tensor_tensor(z[:, 1, :], z[:, 0, :], -1.0, z[:, 0, :], ALU.mult, ALU.min))
            convolve(0, 0)
            dve.wait_ge(dt_act, 3)
            chain(nc.vector.tensor_scalar(z[:, 3, :], z[:, 2, :], 1.0, None, ALU.add))
            chain(nc.vector.tensor_scalar(z[:, 3, :], z[:, 3, :], -1.0, None, ALU.add))
            chain(nc.vector.tensor_tensor(z[:, 3, :], z[:, 2, :], z[:, 3, :], ALU.subtract))
            chain(nc.vector.tensor_tensor(z[:, 3, :], z[:, 1, :], z[:, 3, :], ALU.add))
            dtall = per[:, NT:2 * NT, :].rearrange("p c h -> p (c h)")
            chain(nc.vector.scalar_tensor_tensor(dtall, z[:, 0, :], 0.0, z[:, 3, :], ALU.max, ALU.add))
            chain(nc.vector.scalar_tensor_tensor(per[:, 0:NT, :], per[:, NT:2 * NT, :], -1.0,
                                                 bcast[:, 1, :].unsqueeze(1).to_broadcast([P, NT, H]), ALU.mult, ALU.mult))
            decays_of(0)
            convolve(1, 1)
            silu(0, 0, 0)
            dve.wait_ge(dt_act, 6)
            chain(nc.vector.tensor_tensor(per[:, 3 * NT:4 * NT, :], per[:, 3 * NT:4 * NT, :], per[:, NT:2 * NT, :], ALU.mult))
            for q in range(1, CT):
                if q + 1 < CT:
                    convolve(q + 1, q + 1)
                silu(q, q, 0)
            dve.wait_ge(acc_clear, 1)

            def step(g, s, first, last):
                n0 = NB * CT * g
                tiles = conv_tiles(s, last)
                if s == 4 and not last:
                    taps_of(g + 1)
                if s == NT - 1 and not last:
                    dve.wait_ge(am_ready, NT * g + NT)
                    decays_of(g + 1)
                i = s - 2
                if not (first and s < 2):
                    dve.wait_ge(rg_ready, NT * g + i + 1)
                    if not (first and s == 2):
                        dve.wait_ge(yn_tr, NT * g + i)
                    nc.vector.scalar_tensor_tensor(yn[:, :], y[:, :], rg[:, i % 2:i % 2 + 1],
                                                   sg[:, i % 2, :], ALU.mult, ALU.mult).then_inc(yn_ready, 1)
                if s == 0:
                    if not first:
                        dve.wait_ge(xd_ready, NT * g)
                    nc.vector.tensor_copy(cur[:, NT:2 * NT, :], per[:, NT:2 * NT, bass.ds(HG * g, HG)])
                    nc.vector.tensor_copy(cur[:, 3 * NT:, :], per[:, 3 * NT:, bass.ds(HG * g, HG)]).then_inc(cur_ready, 1)
                if s == 1:
                    nc.vector.tensor_copy(cur[:, 2 * NT:3 * NT, :], per[:, 2 * NT:3 * NT, bass.ds(HG * g, HG)]).then_inc(grown_ready, 1)
                if s < NT:
                    dve.wait_ge(gb_ready, NT * g + s + 1)
                    nc.vector.tensor_copy(btok[:, s % 2, :], bk(5)[:, P:2 * P])
                    if not (first and s == 0):
                        dve.wait_ge(m_ready, NT * g + s)
                    nc.vector.tensor_tensor(gmask[:, :], bk(5)[:, 0:P], upto[:, :], ALU.mult).then_inc(gb_used, 1)
                    dve.wait_ge(e_ready, NT * g + s + 1)
                    dve.wait_ge(gb_used, NT * g + s + 1)
                    nc.vector.tensor_tensor(em[:, s % 2, :, :], em[:, s % 2, :, :],
                                            gmask[:, :].unsqueeze(1).to_broadcast([P, HG, P]), ALU.mult).then_inc(m_ready, 1)
                i, c = s - 1, (s - 1) % CH
                if not (first and s == 0) and s <= NT:
                    m = entered(g, i)
                    if not (first and s == 1):
                        dve.wait_ge(yn_ready, NT * g + i)
                    if c > 0:
                        dve.wait_ge(yo_ready, m + c)
                        nc.vector.tensor_tensor(pair(y[:, :]), pair(bk(6)), heads(2 * NT + i % NT), ALU.mult).then_inc(yo_used, 1)
                i = s - 2
                if tiles:
                    convolve(n0 + tiles[0], tiles[0] % CT)
                if not (first and s < 2):
                    dve.wait_ge(ynT_hi, NT * g + i + 1)
                    low(nc.vector, ynTl[:, :], bk(4), ynTh[:, :]).then_inc(ynT_lo, 1)
                i, c = s - 1, (s - 1) % CH
                if not (first and s == 0) and s <= NT:
                    if c > 0:
                        dve.wait_ge(yi_ready, NT * g + i + 1)
                        dve.wait_ge(yo_used, m + c)
                        nc.vector.tensor_tensor(y[:, :], y[:, :], bk(7), ALU.add).then_inc(y_part, 1)
                        dve.wait_ge(xd_ready, NT * g + i + 1)
                        dve.wait_ge(y_part, m + c)
                        nc.vector.tensor_tensor(y[:, :], y[:, :], xd[:, :], ALU.add).then_inc(y_ready, 1)
                    else:
                        dve.wait_ge(yi_ready, NT * g + i + 1)
                        dve.wait_ge(xd_ready, NT * g + i + 1)
                        nc.vector.tensor_tensor(y[:, :], bk(7), xd[:, :], ALU.add).then_inc(y_ready, 1)
                    if c < CH - 1:
                        dve.wait_ge(st_ready, m + c + 1)
                        if c == 0:
                            if not (first and s == 1):
                                dve.wait_ge(yo_ready, m)
                            nc.vector.tensor_copy(state[:, :], bk(6)).then_inc(state_ready, 1)
                        else:
                            dve.wait_ge(sdec_ready, (CH - 2) * NB * g + (CH - 2) * (i // CH) + c)
                            nc.vector.tensor_tensor(state[:, :], bk(6), state[:, :], ALU.add).then_inc(state_ready, 1)
                if s == 3 and not last:
                    for k in (0, 1):
                        dve.wait_ge(wc_hi, KT * g + KT + k + 1)
                        low(nc.vector, wcl[:, k, :], conv_stage(1)[:, k, :], wch[:, k, :]).then_inc(wc_lo2, 1)
                if tiles:
                    silu(n0 + tiles[0], tiles[0] % CT, tiles[0] // CT % NB)
                    convolve(n0 + tiles[1], tiles[1] % CT)
                if s < NT:
                    dve.wait_ge(tg_ready, NT * g + s + 1)
                    nc.vector.scalar_tensor_tensor(sg[:, s % 2, :], sg[:, s % 2, :], 1.0, bk(0), ALU.add,
                                                   ALU.mult).then_inc(gate_used, 1)
                if tiles:
                    silu(n0 + tiles[1], tiles[1] % CT, tiles[1] // CT % NB)
                i = s - 2
                if not (first and s < 2):
                    dve.wait_ge(o_ready, NT * g + i + 1)
                    nc.vector.tensor_tensor(acc[:, i % NT, :], acc[:, i % NT, :], bk(1), ALU.add).then_inc(out_added, 1)
                    if last and i >= 0:
                        norm_round(1, i)

            group_steps(dve, step)
            norm_vector(1, NT)
            if STAGES >= 2:
                dve.wait_ge(f_small, 48)
                nc.vector.tensor_scalar(fsc[:, 0, :], gus[:, 0, :], 0.5, None, ALU.mult).then_inc(f_dve, 1)
                dve.wait_ge(f_dve, 1)
                nc.vector.tensor_tensor(fsc[:, 1, :], fsc[:, 0, :], gus[:, 1, :], ALU.mult).then_inc(f_part, 1)
                dve.wait_ge(f_part, 1)
                dve.sem_inc(down_added, 4)
                dve.wait_ge(f_clear, 1)

                def add_down(f, b):
                    for i in range(b * CH, (b + 1) * CH):
                        dve.wait_ge(down_ps, NT * f + i + 1)
                        nc.vector.tensor_tensor(acc[:, i, :], acc[:, i, :], bk(4 + i % 4), ALU.add).then_inc(down_added, 1)

                def hid_low(f, q):
                    dve.wait_ge(hid_hi, 4 * f + q + 1)
                    low(nc.vector, hid_part(hidl, q), hidf[:, q % 2, :], hid_part(hidh, q)).then_inc(hid_ready, 1)

                def hidden_pair(f, first):
                    if not first:
                        dve.wait_ge(hid_ready, 4 * f)
                    nc.vector.tensor_copy(fscg[:, :, :], fsc[:, :, bass.ds(2 * f, 2)]).then_inc(fsc_ready, 1)
                    for q in range(4):
                        dve.wait_ge(f_tanh, 4 * f + q + 1)
                        if not (first and q < 2):
                            dve.wait_ge(hid_ready, 4 * f + q - 1)
                        nc.vector.scalar_tensor_tensor(fh[:, q % 2, :], fth[:, q % 2, :], 1.0, bk(q % 2), ALU.add,
                                                       ALU.mult).then_inc(f_part, 1)
                        dve.wait_ge(f_part, 4 * f + q + 2)
                        dve.wait_ge(up_ps, 4 * f + q + 2)
                        nc.vector.scalar_tensor_tensor(hidf[:, q % 2, :], fh[:, q % 2, :],
                                                       fscg[:, 1, q % 2:q % 2 + 1], bk(2 + q % 2),
                                                       ALU.mult, ALU.mult).then_inc(hid_f, 1)
                        if q % 2:
                            hid_low(f, q - 1)
                            hid_low(f, q)
                        if q == 1 and not first:
                            add_down(f - 1, 1)
                    add_down(f, 0)

                hidden_pair(0, True)
                with dve.Fori(1, FP) as f:
                    hidden_pair(f, False)
                add_down(FP - 1, 1)
                norm_vector(2)
            if STAGES >= 3:
                dve.wait_ge(sel_ready, 2)
                s = Count(sel_ready)
                s.n = 2

                def step(ins):
                    s.inc(ins)
                    dve.wait_ge(sel_ready, s.n)

                flat = fold[:, :, :].rearrange("p a b -> p (a b)")
                step(nc.vector.tensor_tensor(flat, ident[:, 0:32], ident[:, 32:64], ALU.add))
                step(nc.vector.tensor_tensor(flat, flat, ident[:, 64:96], ALU.add))
                step(nc.vector.tensor_tensor(flat, flat, ident[:, 96:128], ALU.add))
                step(nc.vector.tensor_scalar(sel[:, :, :], ident[:, :].unsqueeze(1).to_broadcast([P, 4, P]), 0.0, None, ALU.mult))
                for m, reps in enumerate(((0, 2), (1, 3), (0, 1), (2, 3))):
                    dst = sel[:, m, :].rearrange("p (a r d) -> p a r d", a=2, r=4)
                    for r in reps:
                        step(nc.vector.tensor_scalar(dst[:, :, r, :], fold[:, :, :], HD ** -0.5 if m < 2 else 1.0, None, ALU.mult))
                step(nc.vector.tensor_copy(identb[:, :], ident[:, :]))
                step(nc.vector.tensor_copy(future[:, :], futf[:, :]))
                dve.sem_inc(exp_ready, 2)
                dve.sem_inc(pt_lo, 2)
                dve.sem_inc(osum_ready, 1)
                dve.sem_inc(att_ready, 1)
                dve.sem_inc(prec_ready, 2)
                dve.wait_ge(a_small, 32)

                def biases(t):
                    dve.wait_ge(qk_l, 4 * t) if not isinstance(t, int) else None
                    nc.vector.tensor_copy(abg[:, :], abqk[:, :, bass.ds(t, 1)].rearrange("p a b -> p (a b)")).then_inc(bias_ready, 1)

                def prepare(t, b, piece):
                    m = NB * t + b
                    if piece < 2:
                        dve.wait_ge(qk_h, 2 * m + piece + 1)
                        nc.vector.scalar_tensor_tensor(ql[:, piece, :], bk(7), abg[:, piece:piece + 1],
                                                       qh[:, piece, :].bitcast(F32), ALU.add, ALU.subtract).then_inc(qk_l, 1)
                    elif piece % 2:
                        dve.wait_ge(st_ps, 8 * m + piece - 1)
                        nc.vector.tensor_copy(stacked(b, piece - 2), bk(7)).then_inc(st_out2, 1)

                def tile(t, last):
                    for s in range(UNITS + 4):
                        w = s - 4
                        if w >= 0:
                            if w % 4 == 0:
                                dve.wait_ge(att_ready, 8 * t + w // 4 + 1)
                            dve.wait_ge(pv_ps, UNITS * t + w + 1)
                            o = bk(6).rearrange("p (j h w d) -> p j h d w", j=2, h=HT, w=2)
                            pr = w % 4
                            for j in range(2):
                                ins = nc.vector.tensor_reduce(osum[:, 2 * pr + j, :], o[:, j, 2 * pr + j, :, :], AX, ALU.add)
                            ins.then_inc(osum_ready, 1)
                        if s < UNITS:
                            kw = (s % 16 // 4 + 1) * P
                            dve.wait_ge(s_ready, UNITS * t + s + 1)
                            nc.vector.tensor_reduce(nmax[:, s % 2, :], banks[:, 2 * (s % 2):2 * (s % 2) + 2, 0:kw],
                                                    AX, ALU.max, negate=True).then_inc(max_ready, 1)
                        w = s - 2
                        if 0 <= w < UNITS:
                            kw = (w % 16 // 4 + 1) * P
                            for j in range(2):
                                dve.wait_ge(pt_hi, 2 * UNITS * t + 2 * w + j + 1)
                                low(nc.vector, pTl[:, w % 2, j, 0:kw], bk(4 + j)[:, 0:kw],
                                    pTh[:, w % 2, j, 0:kw]).then_inc(pt_lo, 1)
                        gq = s // 4 - 1
                        if s % 4 == 1 and gq >= 0:
                            dve.wait_ge(exp_ready, UNITS * t + s - 1 + 2)
                            dve.wait_ge(att_ready, 8 * t + gq + 1)
                            nc.vector.reciprocal(prec[:, :], psum[:, gq % 2, :]).then_inc(prec_ready, 1)
                        if s % 4 == 3 and gq >= 0:
                            dve.wait_ge(osum_ready, UNITS * t + s - 4 + 1 + 1)
                            dve.wait_ge(prec_ready, 8 * t + gq + 3)
                            nc.vector.tensor_tensor(
                                att[:, gq, bass.ds(P * t, P)].rearrange("p (h d) -> p h d", d=HD), osum[:, :, :],
                                prec[:, :].unsqueeze(2).to_broadcast([P, HT, HD]), ALU.mult).then_inc(att_ready, 1)
                        if s == 16 and not last:
                            biases(t + 1)
                        ahead = passes_ahead(t, s, last)
                        if ahead:
                            prepare(*ahead)

                biases(0)
                for i in range(10):
                    if i < NT:
                        dve.wait_ge(v_ps, i + 1)
                        if i >= 2:
                            dve.wait_ge(v_ready, i - 1)
                        nc.vector.tensor_tensor(vf[:, i % 2, :], bk(i % 2), abv[:, :], ALU.add).then_inc(v_f, 1)
                    prepare(0, 0, i)
                    if i < NT:
                        dve.wait_ge(v_hi, i + 1)
                        nc.vector.tensor_tensor(v[:, i, :, 1, :], vf[:, i % 2, :].rearrange("p (h d) -> p h d", d=HD),
                                                v[:, i, :, 0, :].bitcast(F32), ALU.subtract).then_inc(v_ready, 1)
                with dve.Fori(0, AT - 1) as t:
                    tile(t, False)
                tile(AT - 1, True)
                dve.wait_ge(abo_in, 16)
                for i in range(NT + 1):
                    if i < NT:
                        dve.wait_ge(at_hi, i + 1)
                        low(nc.vector, attTl[:, i % 2, :], bk(i % 2), attTh[:, i % 2, :]).then_inc(at_lo, 1)
                    if i >= 1:
                        dve.wait_ge(ao_ps, i)
                        nc.vector.tensor_tensor(acc[:, i - 1, :], bk(6 + (i - 1) % 2), abo[:, :], ALU.add).then_inc(ao_ready, 1)
                        norm_round(3, i - 1)
                norm_vector(3, NT)
            if STAGES >= 4:
                dve.wait_ge(lg_tr, 1)
                r = Count(r_dve)

                def rstep(ins, wait=True):
                    r.inc(ins)
                    if wait:
                        dve.wait_ge(r_dve, r.n)

                rstep(nc.vector.tensor_copy(lg[:, :, :], bk(2)[:, 0:NT * NE].rearrange("p (a b) -> p a b", a=NT)))
                for i in range(NT):
                    rstep(nc.vector.max(top[:, i, :], lg[:, i, :]), i == NT - 1)
                for i in range(NT):
                    rstep(nc.vector.max_index(topi[:, i, :], top[:, i, :], lg[:, i, :]), i == NT - 1)
                rstep(nc.vector.tensor_tensor(rt[:, 0, :], top[:, :, 1], top[:, :, 0], ALU.subtract))
                rstep(nc.vector.tensor_copy(topf[:, :, :], topi[:, :, :]))
                dve.wait_ge(r_act, 1)
                dve.wait_ge(r_iota, 1)
                rstep(nc.vector.tensor_scalar(rt[:, 2, :], rt[:, 1, :], 1.0, None, ALU.add))
                rstep(nc.vector.reciprocal(rt[:, 2, :], rt[:, 2, :]))
                rstep(nc.vector.tensor_tensor(rt[:, 3, :], rt[:, 2, :], rt[:, 1, :], ALU.mult))
                for c in range(2):
                    rstep(nc.vector.tensor_tensor(oh[:, c, :, :], which[:, :].unsqueeze(1).to_broadcast([P, NT, NE]),
                                                  topf[:, :, c].unsqueeze(2).to_broadcast([P, NT, NE]), ALU.is_equal))
                    rstep(nc.vector.tensor_tensor(oh[:, c, :, :], oh[:, c, :, :],
                                                  rt[:, 2 + c, :].unsqueeze(2).to_broadcast([P, NT, NE]), ALU.mult))
                rstep(nc.vector.tensor_tensor(we[:, :, :], oh[:, 0, :, :], oh[:, 1, :, :], ALU.add))
                dve.wait_ge(d_clear, 1)
                dve.sem_inc(ex_added, NT)

                def add_expert(e, s, i):
                    dve.wait_ge(ex_ps, 2 * NT * e + NT * s + i + 1)
                    nc.vector.scalar_tensor_tensor(acc[:, i, :], bk(i), we[:, i, bass.ds(2 * e + s, 1)],
                                                   acc[:, i, :], ALU.mult, ALU.add).then_inc(ex_added, 1)

                with dve.Fori(0, NE // 2 - 1) as e:
                    for s in range(2):
                        for i in range(NT):
                            add_expert(e, s, i)
                for s in range(2):
                    for i in range(NT):
                        add_expert(NE // 2 - 1, s, i)
                        if s == 1:
                            norm_round(4, i)
                norm_vector(4, NT)

        @block.tensor
        def _(pe):
            mat = nc.tensor.matmul
            pe.sem_inc(up_ps, 1)
            pe.wait_ge(consts, 6)
            norm_tensor(0)
            norm_wait(pe, 0, "lo", NT)
            pe.wait_ge(wdt_lo, 1)
            def convolved(n, q, b):
                ch, tok = slice(q * P, (q + 1) * P), slice(b * L, (b + 1) * L)
                products(bk(CONV_BANKS[q % 2]), [(wch[:, k, ch], wcl[:, k, ch], xTh[:, k, tok], xTl[:, k, tok])
                                                 for k in range(KT)]).then_inc(h_ready, 1)

            def step(g, s, first, last):
                n0 = NB * CT * g
                tiles = conv_tiles(s, last)
                if s < NT:
                    tok = slice(s * P, (s + 1) * P)
                    if s % CH == 0:
                        pe.wait_ge(xbc_ready, n0 + CT * (s // CH + 1))
                    if not (first and s < 3):
                        pe.wait_ge(ynT_lo, NT * g + s - 2)
                    elif s:
                        pe.wait_ge(x_out, NT * g + s)
                    for j in range(KT):
                        m = pe.transpose(bk(4)[:, j * P:(j + 1) * P], xbc[:, j, tok], ident[:, :])
                    m.then_inc(x_tr, 1)
                    if not (first and s == 0):
                        pe.wait_ge(gb_used, NT * g + s)
                    pe.transpose(bk(5)[:, P:2 * P], xbc[:, JB, tok], ident[:, :])
                    mat(bk(5)[:, 0:P], xbc[:, JB, tok], xbc[:, JC, tok], start=True, stop=True).then_inc(gb_ready, 1)
                    pe.wait_ge(am_ready, NT * g + s + 1)
                    if not (first and s == 0):
                        pe.wait_ge(e_ready, NT * g + s)
                    pe.wait_ge(taps, 3 * conv_made(g, s, last))
                    for w in range(2):
                        for part in range(2):
                            m = mat(bk(2 + w), after[:, :],
                                    am[:, part, 4 * w:4 * w + 4, :].rearrange("p h t -> p (h t)"),
                                    start=(part == 0), stop=(part == 1))
                    m.then_inc(d_ready, 1)
                if tiles:
                    if s == 4:
                        pe.wait_ge(wc_lo, 2 * g + KT + 2)
                        pe.wait_ge(wc_lo2, 2 * g + KT + 2)
                    if not (first and s == 0):
                        pe.wait_ge(gate_used, NT * g + s)
                    convolved(n0 + tiles[0], tiles[0] % CT, tiles[0] // CT % NB)
                i = s - 2
                if not (first and s < 2):
                    pe.wait_ge(yn_ready, NT * g + i + 1)
                    if s < NT:
                        pe.wait_ge(x_out, NT * g + s + 1)
                    else:
                        pe.wait_ge(ynT_lo, NT * g + i)
                    for j in range(KT):
                        m = pe.transpose(bk(4)[:, j * P:(j + 1) * P], yn[:, j * P:(j + 1) * P], ident[:, :])
                    m.then_inc(yn_tr, 1)
                i, c = s - 1, (s - 1) % CH
                if not (first and s == 0) and s <= NT:
                    tok = slice(i % NT * P, (i % NT + 1) * P)
                    m0 = entered(g, i)
                    if c > 0:
                        pe.wait_ge(state_ready, m0 + c)
                        mat(bk(6), xbc[:, JC, tok], state[:, :], start=True, stop=True).then_inc(yo_ready, 1)
                    pe.wait_ge(m_ready, NT * g + i + 1)
                    pe.wait_ge(dtx_ready, NT * g + i + 1)
                    if not (first and s == 1):
                        pe.wait_ge(y_ready, NT * g + i)
                    for h in range(HG):
                        m = mat(bk(7)[:, h * HP:(h + 1) * HP], em[:, i % 2, h, :], dtx[:, h * HP:(h + 1) * HP],
                                start=True, stop=True)
                    m.then_inc(yi_ready, 1)
                    if c < CH - 1:
                        pe.wait_ge(xdec_ready, m0 + c + 1)
                        if c > 0:
                            pe.wait_ge(yo_used, m0 + c)
                        elif not (first and s == 1):
                            pe.wait_ge(yo_used, m0)
                        mat(bk(6), btok[:, i % 2, :], xdec[:, :], start=True, stop=True).then_inc(st_ready, 1)
                if tiles:
                    pe.wait_ge(e_ready, NT * g + s + 1)
                    convolved(n0 + tiles[1], tiles[1] % CT, tiles[1] // CT % NB)
                if s < NT:
                    if s == 0:
                        pe.wait_ge(wg_lo, KT * g + KT)
                    if tiles:
                        pe.wait_ge(taps, 3 * (n0 + tiles[0]) + 3)
                    elif not (first and s == 0):
                        pe.wait_ge(gate_used, NT * g + s)
                    tok = slice(s * P, (s + 1) * P)
                    products(bk(0), [(xTh[:, k, tok], xTl[:, k, tok], wgh[:, k, :], wgl[:, k, :])
                                     for k in range(KT)]).then_inc(gate_ready, 1)
                i = s - 2
                if not (first and s < 2):
                    if s == 2:
                        pe.wait_ge(wo_lo, KT * g + KT)
                    if not (first and s == 2):
                        pe.wait_ge(out_added, NT * g + i)
                    pe.wait_ge(ynT_lo, NT * g + i + 1)
                    products(bk(1), [(ynTh[:, k * P:(k + 1) * P], ynTl[:, k * P:(k + 1) * P], woh[:, k, :], wol[:, k, :])
                                     for k in range(KT)]).then_inc(o_ready, 1)

            for b in range(NB):
                tok = slice(b * L, (b + 1) * L)
                products(bk(5 + b)[0:H, :], [(wdth[:, k, :], wdtl[:, k, :], xTh[:, k, tok], xTl[:, k, tok])
                                             for k in range(KT)]).then_inc(dt_ps, 1)
            pe.wait_ge(wc_lo, KT)
            convolved(0, 0, 0)
            pe.wait_ge(dt_t, 2)
            for i in range(NT):
                m = pe.transpose(bk(7)[:, i * H:(i + 1) * H], sg[0:H, i // CH, i % CH * P:(i % CH + 1) * P], ident[0:H, 0:H])
            m.then_inc(dt_tr, 1)
            convolved(1, 1, 0)
            pe.wait_ge(dt_dve, 9)
            for n, mask in enumerate((upto[:, :], after[:, :].bitcast(F32), ones[:, :])):
                mat(bk(3 + n), mask, per[:, 0:NT, :].rearrange("p c h -> p (c h)"), start=True, stop=True).then_inc(dt_cum, 1)
            for q in range(2, CT):
                pe.wait_ge(taps, 3 * (q - 1))
                convolved(q, q, 0)
            pe.wait_ge(dt_act, 6)
            group_steps(pe, step)
            if STAGES >= 2:
                tile_done(pe, 1, NT - 1)
                norm_tensor(1)
                norm_wait(pe, 1, "lo", NT)

                def gate_up(f, b, first):
                    tok = slice(b * L, (b + 1) * L)
                    for ft in range(2):
                        q = 2 * b + ft
                        if not (first and q < 2):
                            pe.wait_ge(hid_f, 4 * f + q - 1)
                        for w, done in ((0, gate_ps), (1, up_ps)):
                            for k in range(KT):
                                for part in (xTh, xTl):
                                    m = mat(bk(2 * w + ft), gu[:, k, ft, w, :], part[:, k, tok],
                                            start=(k == 0 and part is xTh), stop=(k == KT - 1 and part is xTl))
                            m.then_inc(done, 1)

                def down(f, b):
                    pe.wait_ge(hid_ready, 4 * f + 2 * b + 2)
                    for i in range(b * CH, (b + 1) * CH):
                        pe.wait_ge(down_added, NT * f + i + 1)
                        for k in range(2):
                            for part in (hidh, hidl):
                                m = mat(bk(4 + i % 4), part[:, k, i * P:(i + 1) * P], dn[:, k, :],
                                        start=(k == 0 and part is hidh), stop=(k == 1 and part is hidl))
                        m.then_inc(down_ps, 1)

                def hidden_pair(f, first):
                    pe.wait_ge(gu_cast, KT * f + KT)
                    gate_up(f, 0, first)
                    if not first:
                        down(f - 1, 1)
                    gate_up(f, 1, first)
                    pe.wait_ge(dn_cast, 2 * f + 2)
                    down(f, 0)

                hidden_pair(0, True)
                with pe.Fori(1, FP) as f:
                    hidden_pair(f, False)
                down(FP - 1, 1)
            if STAGES >= 3:
                norm_tensor(2)
                norm_wait(pe, 2, "lo", NT)
                pe.wait_ge(aw_lo, KT)
                pe.wait_ge(sel_ready, 2 + 4 + 8 + 2)

                def prepare(t, b, piece):
                    m = NB * t + b
                    first = isinstance(t, int)
                    if piece < 2:
                        if piece:
                            pe.wait_ge(qk_l, 2 * m + 1)
                        elif not first:
                            pe.wait_ge(st_out2, 4 * m)
                        if piece == 0 and b == 0:
                            pe.wait_ge(aq_lo, 2 * t + 2)
                        tok = slice(b * L, (b + 1) * L)
                        products(bk(7), [(aqh[:, piece, k, :], aql[:, piece, k, :], xTh[:, k, tok], xTl[:, k, tok])
                                         for k in range(KT)]).then_inc(qk_ps, 1)
                    else:
                        w, pr = (piece - 2) // 4, (piece - 2) % 4
                        if piece == 2:
                            pe.wait_ge(qk_l, 2 * m + 2)
                        else:
                            pe.wait_ge((st_out, st_out2)[(piece - 1) % 2], 4 * m + (piece - 1) // 2)
                        rows = slice(32 * pr, 32 * pr + 32)
                        mat(bk(7), sel[rows, 2 * w, :], qh[rows, w, :], start=True, stop=False)
                        mat(bk(7), sel[rows, 2 * w + 1, :], ql[rows, w, :], start=False, stop=True).then_inc(st_ps, 1)

                def tile(t, last):
                    for s in range(UNITS + 3):
                        if s < UNITS:
                            b, qi, pr = s // 16, s % 16 // 4, s % 4
                            kw = (qi + 1) * P
                            if s % 16 == 0:
                                pe.wait_ge(st_out, 4 * (NB * t + b) + 4)
                                pe.wait_ge(st_out2, 4 * (NB * t + b) + 4)
                            pe.wait_ge(exp_ready, UNITS * t + s + 1)
                            for j in range(2):
                                rows = slice(64 * j, 64 * j + 64)
                                o = bk(2 * (s % 2) + j)
                                kn = max(kw, 2 * P)
                                mat(o[:, 0:kn], qs[rows, b, pr, qi * P:kw], ks[rows, b, pr, 0:kn], start=True, stop=False)
                                m = mat(o[:, kw - P:kw], identb[:, :], future[:, :], start=False, stop=True)
                            m.then_inc(s_ready, 1)
                        w = s - 2
                        if 0 <= w < UNITS:
                            pe.wait_ge(exp_ready, UNITS * t + w + 1 + 2)
                            for j in range(2):
                                pe.wait_ge(pt_lo, 2 * UNITS * t + 2 * w + j + 1)
                                for c in range(w % 16 // 4 + 1):
                                    m = pe.transpose(bk(4 + j)[:, c * P:(c + 1) * P], prob[:, w % 2, j, c * P:(c + 1) * P], ident[:, :])
                                m.then_inc(pt_ps, 1)
                        w = s - 3
                        if w >= 0:
                            b, qi = w // 16, w % 16 // 4
                            pe.wait_ge(pt_lo, 2 * UNITS * t + 2 * w + 2 + 2)
                            pe.wait_ge(osum_ready, UNITS * t + w + 1)
                            for j in range(2):
                                o = bk(6)[:, 2 * P * j:2 * P * (j + 1)]
                                for c in range(qi + 1):
                                    vals = v[:, b * CH + c, bass.ds(HT * t, HT), :, :].rearrange("p h w d -> p (h w d)")
                                    for part in (pTh, pTl):
                                        m = mat(o, part[:, w % 2, j, c * P:(c + 1) * P], vals,
                                                start=(c == 0 and part is pTh), stop=(c == qi and part is pTl))
                            m.then_inc(pv_ps, 1)
                        ahead = passes_ahead(t, s, last)
                        if ahead:
                            prepare(*ahead)

                for i in range(10):
                    if i < NT:
                        if i >= 2:
                            pe.wait_ge(v_f, i - 1)
                        tok = slice(i * P, (i + 1) * P)
                        products(bk(i % 2), [(xTh[:, k, tok], xTl[:, k, tok], awh[:, k, :], awl[:, k, :])
                                             for k in range(KT)]).then_inc(v_ps, 1)
                    prepare(0, 0, i)
                pe.wait_ge(v_ready, NT)
                with pe.Fori(0, AT - 1) as t:
                    tile(t, False)
                tile(AT - 1, True)
                for i in range(NT + 1):
                    if i < NT:
                        if i == 0:
                            pe.wait_ge(att_ready, 8 * AT + 1)
                        if i >= 2:
                            pe.wait_ge(at_lo, i - 1)
                        for k in range(KT):
                            m = pe.transpose(bk(i % 2)[:, k * P:(k + 1) * P], att[:, i, k * P:(k + 1) * P], ident[:, :])
                        m.then_inc(at_ps, 1)
                    if i >= 1:
                        j = i - 1
                        pe.wait_ge(at_lo, j + 1)
                        pe.wait_ge(aw_lo, 2 * KT)
                        if j >= 2:
                            pe.wait_ge(ao_ready, j - 1)
                        cols = [slice(k * P, (k + 1) * P) for k in range(KT)]
                        products(bk(6 + j % 2), [(attTh[:, j % 2, c], attTl[:, j % 2, c], awh[:, k, :], awl[:, k, :])
                                                 for k, c in enumerate(cols)]).then_inc(ao_ps, 1)
            if STAGES >= 4:
                norm_tensor(3)
                norm_wait(pe, 3, "lo", NT)
                pe.wait_ge(rw_lo, 1)

                def stream(i):
                    return lambda wh, wl: [(xTh[:, k, i * P:(i + 1) * P], xTl[:, k, i * P:(i + 1) * P], wh[:, k, :], wl[:, k, :])
                                           for k in range(KT)]

                for b in range(NB):
                    tok = slice(b * L, (b + 1) * L)
                    products(bk(b)[0:NE, :], [(rwh[:, k, :], rwl[:, k, :], xTh[:, k, tok], xTl[:, k, tok])
                                              for k in range(KT)]).then_inc(lg_ps, 1)
                pe.wait_ge(lg_t, 2)
                for i in range(NT):
                    m = pe.transpose(bk(2)[:, i * NE:(i + 1) * NE], lgT[0:NE, i // CH, i % CH * P:(i % CH + 1) * P],
                                     ident[0:NE, 0:NE])
                m.then_inc(lg_tr, 1)
                pe.wait_ge(r_dve, 1)
                with pe.Fori(0, NE // 2) as e:
                    for s in range(2):
                        pe.wait_ge(e_lo, 2 * KT * e + KT * (s + 1))
                        for i in range(NT):
                            pe.wait_ge(ex_added, 2 * NT * e + NT * s + i + 1)
                            products(bk(i), stream(i)(ewh[:, s], ewl[:, s])).then_inc(ex_ps, 1)


def kernel(**inputs):
    from concourse.bacc import Bacc
    from concourse.bass_utils import run_bass_kernel_spmd

    a = {k: np.asarray(v) for k, v in inputs.items()}

    def rows(w):
        return w.T.reshape(KT, P, -1).transpose(1, 0, 2)

    w_in = a["L0_attn_in_proj_w"]
    inner, gn = H * HP, G * NS
    gate_w, x_w, b_w, c_w, dt_w = np.split(w_in, [inner, 2 * inner, 2 * inner + gn, 2 * inner + 2 * gn])

    def by_group(x, b, c):
        return np.concatenate([m.reshape(G, -1, *m.shape[1:]) for m in (x, b, c)], 1)

    conv = by_group(x_w, b_w, c_w)
    cw = by_group(*np.split(a["L0_attn_conv_weight"], [inner, inner + gn])).reshape(G, CT, P, KC)
    cb = by_group(*np.split(a["L0_attn_conv_bias"], [inner, inner + gn])).reshape(G, CT, P)
    gu = np.stack([a["L0_ffn_gate_t"], a["L0_ffn_up_t"]]).reshape(2, FP, 2, P, KT, P)
    arrays = {
        "hidden": a["L0_attn_hidden_states"].reshape(NB * L, DM),
        "w_conv": np.stack([rows(m) for m in conv]),
        "w_gate": np.stack([rows(m) for m in gate_w.reshape(G, GI, DM)]),
        "w_dt": rows(dt_w),
        "conv_w": cw.transpose(2, 0, 1, 3),
        "conv_b": cb.transpose(2, 0, 1),
        "dt_bias": a["L0_attn_dt_bias"],
        "A_log": a["L0_attn_A_log"],
        "Dskip": a["L0_attn_D"],
        "norm_w": a["L0_attn_norm_weight"].reshape(G, KT, P).transpose(2, 0, 1),
        "w_out": a["L0_attn_out_proj_w"].reshape(DM, G, KT, P).transpose(1, 3, 2, 0),
        "ff_gu": gu.transpose(1, 5, 4, 2, 0, 3),
        "ff_dn": a["L0_ffn_down_t"].reshape(DM, FP, 2, P).transpose(1, 3, 2, 0),
        "gate_s": a["L0_ffn_gate_s"].reshape(FT, P).T,
        "up_s": a["L0_ffn_up_s"].reshape(FT, P).T,
        "down_s": a["L0_ffn_down_s"],
        "wq": a["L1_attn_Wq"].reshape(AT, P, KT, P).transpose(0, 3, 2, 1),
        "wk": a["L1_attn_Wk"].reshape(AT, P, KT, P).transpose(0, 3, 2, 1),
        "bqk": np.stack([a["L1_attn_bq"], a["L1_attn_bk"]]).reshape(2, AT, P).transpose(2, 0, 1),
        "wv": rows(a["L1_attn_Wv"]),
        "bv": a["L1_attn_bv"],
        "wo": rows(a["L1_attn_Wo"]),
        "bo": a["L1_attn_bo"],
        "gate_w": a["L1_ffn_gate_w"].reshape(KT, P, NE).transpose(1, 0, 2),
        "expert_w": a["L1_ffn_expert_w"].reshape(NE, KT, P, DM).transpose(0, 2, 1, 3),
    }
    arrays = {k: np.ascontiguousarray(v) for k, v in arrays.items()}
    nc = Bacc("TRN2", target_bir_lowering=False, num_devices=1)
    args = {k: nc.dram_tensor(f"in_{k}", v.shape, mybir.dt.from_np(v.dtype), kind="ExternalInput").ap()
            for k, v in arrays.items()}
    out = nc.dram_tensor("out", (NB * L, DM), F32, kind="ExternalOutput").ap()
    program(nc, out=out, **args)
    r = run_bass_kernel_spmd(nc, [{f"in_{k}": v for k, v in arrays.items()}], core_ids=[0])
    return r.results[0]["out"].reshape(NB, L, DM)
```
